# Optimizing a Trainium2 kernel written in Bass

```python
import numpy as np
import jax
import jax.numpy as jnp

def _softmax(x, axis=-1):
    return jax.nn.softmax(x, axis=axis)

def _gelu(x):
    return jax.nn.gelu(x, approximate=True)

def _silu(x):
    return jax.nn.silu(x)

def _sigmoid(x):
    return jax.nn.sigmoid(x)

def _layernorm(x, axis=-1, eps=1e-05):
    m = jnp.mean(x, axis=axis, keepdims=True)
    v = jnp.var(x, axis=axis, keepdims=True)
    return (x - m) / jnp.sqrt(v + eps)

def _scatter_add(tgt, idx, src, axis=0):
    return tgt.at[idx].add(src)

def _segment_sum(src, seg, n):
    return jax.ops.segment_sum(src, seg, n)
kernel_name = 'mk_vit_tower_d1_tok_img512_r4_66f744'

def setup_inputs(seed: int=0):
    np.random.seed(seed)
    _w = jnp.asarray

    def _rec_inputs():
        import jax
        import jax.numpy as jnp
        _rk = jax.random.key(seed)
        x = -0.000356955 + 1 * jax.random.normal(jax.random.fold_in(_rk, 1), (64, 3, 112, 112), jnp.float32)
        return x
    x = _rec_inputs()

    def _L0_tok_setup():
        import jax, jax.numpy as jnp
        import numpy as np
        IMG = 112
        P = 16
        C = 3
        D = 128
        DC = 8
        DS = 4
        NH = IMG // P
        NPATCH = NH * NH
        PDIM = C * P * P
        BATCH = 32
        EPS = 1e-05
        key = jax.random.key(seed)
        ks = jax.random.split(key, 10)

        def lin(k, fan_in, shape):
            bound = 1.0 / np.sqrt(fan_in)
            return jax.random.uniform(k, shape, jnp.float32, -bound, bound)
        return {'images': jax.random.normal(ks[0], (BATCH, C, IMG, IMG), jnp.float32), 'W_patch': lin(ks[1], PDIM, (PDIM, D)), 'b_patch': jnp.zeros((D,), jnp.float32), 'pos_embed': jax.random.normal(ks[2], (1, NPATCH, D), jnp.float32) * 0.02, 'W_coord': lin(ks[3], D, (D, DC)), 'b_coord': jnp.zeros((DC,), jnp.float32), 'W_spinor': lin(ks[4], D, (D, DS)), 'b_spinor': jnp.zeros((DS,), jnp.float32), 'W_embed': lin(ks[5], DC, (DC, D)), 'b_embed': jnp.zeros((D,), jnp.float32), 'ln_gamma': jnp.ones((D,), jnp.float32), 'ln_beta': jnp.zeros((D,), jnp.float32), 'W_out': lin(ks[6], D, (D, D)), 'b_out': jnp.zeros((D,), jnp.float32)}
    _L0_tok_all = _L0_tok_setup()
    _L0_tok_in = {k: v for k, v in _L0_tok_all.items() if k in ('W_patch', 'b_patch', 'pos_embed', 'W_coord', 'b_coord', 'W_spinor', 'b_spinor', 'W_embed', 'b_embed', 'ln_gamma', 'ln_beta', 'W_out', 'b_out')}
    del _L0_tok_all

    def _L0_attn_setup():
        import jax, jax.numpy as jnp
        import numpy as np
        HX_INIT = 1e-06

        def log_g(x):
            return jnp.where(x >= 0, jnp.log(jax.nn.relu(x) + 0.5), -jax.nn.softplus(-x))
        key = jax.random.key(seed)
        k1, k2, k3 = jax.random.split(key, 3)
        N, L, H_in, H = (8, 1024, 128, 128)
        x = jax.random.normal(k1, (N, L, H_in), dtype=jnp.float32)
        W = jax.random.normal(k2, (3 * H, H_in), dtype=jnp.float32) * 0.05
        b = jax.random.normal(k3, (3 * H,), dtype=jnp.float32) * 0.05
        return {'x': x, 'W': W, 'b': b}
    _L0_attn_all = _L0_attn_setup()
    _L0_attn_in = {k: v for k, v in _L0_attn_all.items() if k in ('W', 'b')}
    del _L0_attn_all

    def _L0_ffn_setup():
        import jax, jax.numpy as jnp
        import numpy as np
        from jax import lax
        B, S, IN, D, E, NH = (8, 128, 128, 256, 4, 16)
        DH = D // NH
        EPS = 1e-05
        SCALE = np.float32(1.0 / np.sqrt(DH))

        def _ln(x, g, b):
            m = x.mean(-1, keepdims=True)
            v = ((x - m) ** 2).mean(-1, keepdims=True)
            return (x - m) * lax.rsqrt(v + EPS) * g + b

        def _lstm_dir(x, Wi, Wh, b):
            bsz = x.shape[0]
            h0 = jnp.zeros((bsz, Wh.shape[0]), x.dtype)

            def step(carry, xt):
                h, c = carry
                zg = xt @ Wi + h @ Wh + b
                i, f, g, o = jnp.split(zg, 4, axis=-1)
                c = jax.nn.sigmoid(f) * c + jax.nn.sigmoid(i) * jnp.tanh(g)
                h = jax.nn.sigmoid(o) * jnp.tanh(c)
                return ((h, c), h)
            _, hs = lax.scan(step, (h0, h0), jnp.swapaxes(x, 0, 1))
            return jnp.swapaxes(hs, 0, 1)

        def _expert(x, p):
            ew1, eb1, ew2, eb2, eg, ebeta, aiw, aib, aow, aob, wif, whf, bf, wibk, whbk, bbk, sw1, sb1, sw2, sb2, tw1, tb1, tw2, tb2, dw1, db1, dw2, db2, dg, dbeta = p
            h = _ln(jax.nn.relu(x @ ew1 + eb1) @ ew2 + eb2, eg, ebeta)
            qkv = h @ aiw + aib
            q, k, v = jnp.split(qkv, 3, axis=-1)

            def heads(t):
                return t.reshape(t.shape[0], t.shape[1], NH, DH).transpose(0, 2, 1, 3)
            q, k, v = (heads(q), heads(k), heads(v))
            attn = jax.nn.softmax(jnp.einsum('bhqd,bhkd->bhqk', q, k) * SCALE, axis=-1)
            o = jnp.einsum('bhqk,bhkd->bhqd', attn, v).transpose(0, 2, 1, 3).reshape(h.shape)
            h = o @ aow + aob
            hf = _lstm_dir(h, wif, whf, bf)
            hb = _lstm_dir(h[:, ::-1], wibk, whbk, bbk)[:, ::-1]
            mem = jnp.concatenate([hf, hb], axis=-1)
            gate_s = jax.nn.sigmoid(jax.nn.relu(mem @ sw1 + sb1) @ sw2 + sb2)
            gate_t = jnp.tanh(jax.nn.relu(mem @ tw1 + tb1) @ tw2 + tb2)
            g = gate_s * gate_t
            return _ln(jax.nn.relu(g @ dw1 + db1) @ dw2 + db2, dg, dbeta)

        def _forward(x, router_w, router_b, *p):
            outs = jax.vmap(lambda pe: _expert(x, pe))(tuple(p))
            w = jax.nn.softmax(x @ router_w + router_b, axis=-1)
            return jnp.einsum('ebsd,bse->bsd', outs, w)
        key = jax.random.key(seed)
        ks = iter(jax.random.split(key, 64))

        def rn(shape, scale=0.02):
            return jax.random.normal(next(ks), shape, dtype=jnp.float32) * scale
        z = lambda shape: jnp.zeros(shape, dtype=jnp.float32)
        return {'x': jax.random.normal(next(ks), (B, S, IN), dtype=jnp.float32), 'router_w': rn((IN, E)), 'router_b': z((E,)), 'enc_w1': rn((E, IN, D)), 'enc_b1': z((E, D)), 'enc_w2': rn((E, D, D)), 'enc_b2': z((E, D)), 'enc_g': jnp.ones((E, D), jnp.float32), 'enc_beta': z((E, D)), 'attn_in_w': rn((E, D, 3 * D)), 'attn_in_b': z((E, 3 * D)), 'attn_out_w': rn((E, D, D)), 'attn_out_b': z((E, D)), 'lstm_wi_f': rn((E, D, 4 * D)), 'lstm_wh_f': rn((E, D, 4 * D)), 'lstm_b_f': z((E, 4 * D)), 'lstm_wi_b': rn((E, D, 4 * D)), 'lstm_wh_b': rn((E, D, 4 * D)), 'lstm_b_b': z((E, 4 * D)), 'sig_w1': rn((E, 2 * D, D)), 'sig_b1': z((E, D)), 'sig_w2': rn((E, D, D)), 'sig_b2': z((E, D)), 'tan_w1': rn((E, 2 * D, D)), 'tan_b1': z((E, D)), 'tan_w2': rn((E, D, D)), 'tan_b2': z((E, D)), 'dec_w1': rn((E, D, D)), 'dec_b1': z((E, D)), 'dec_w2': rn((E, D, IN)), 'dec_b2': z((E, IN)), 'dec_g': jnp.ones((E, IN), jnp.float32), 'dec_beta': z((E, IN))}
    _L0_ffn_all = _L0_ffn_setup()
    _L0_ffn_in = {k: v for k, v in _L0_ffn_all.items() if k in ('router_w', 'router_b', 'enc_w1', 'enc_b1', 'enc_w2', 'enc_b2', 'enc_g', 'enc_beta', 'attn_in_w', 'attn_in_b', 'attn_out_w', 'attn_out_b', 'lstm_wi_f', 'lstm_wh_f', 'lstm_b_f', 'lstm_wi_b', 'lstm_wh_b', 'lstm_b_b', 'sig_w1', 'sig_b1', 'sig_w2', 'sig_b2', 'tan_w1', 'tan_b1', 'tan_w2', 'tan_b2', 'dec_w1', 'dec_b1', 'dec_w2', 'dec_b2', 'dec_g', 'dec_beta')}
    del _L0_ffn_all
    return {'x': x, 'L0_tok_W_patch': _L0_tok_in['W_patch'], 'L0_tok_b_patch': _L0_tok_in['b_patch'], 'L0_tok_pos_embed': _L0_tok_in['pos_embed'], 'L0_tok_W_coord': _L0_tok_in['W_coord'], 'L0_tok_b_coord': _L0_tok_in['b_coord'], 'L0_tok_W_spinor': _L0_tok_in['W_spinor'], 'L0_tok_b_spinor': _L0_tok_in['b_spinor'], 'L0_tok_W_embed': _L0_tok_in['W_embed'], 'L0_tok_b_embed': _L0_tok_in['b_embed'], 'L0_tok_ln_gamma': _L0_tok_in['ln_gamma'], 'L0_tok_ln_beta': _L0_tok_in['ln_beta'], 'L0_tok_W_out': _L0_tok_in['W_out'], 'L0_tok_b_out': _L0_tok_in['b_out'], 'L0_attn_W': _L0_attn_in['W'], 'L0_attn_b': _L0_attn_in['b'], 'L0_ffn_router_w': _L0_ffn_in['router_w'], 'L0_ffn_router_b': _L0_ffn_in['router_b'], 'L0_ffn_enc_w1': _L0_ffn_in['enc_w1'], 'L0_ffn_enc_b1': _L0_ffn_in['enc_b1'], 'L0_ffn_enc_w2': _L0_ffn_in['enc_w2'], 'L0_ffn_enc_b2': _L0_ffn_in['enc_b2'], 'L0_ffn_enc_g': _L0_ffn_in['enc_g'], 'L0_ffn_enc_beta': _L0_ffn_in['enc_beta'], 'L0_ffn_attn_in_w': _L0_ffn_in['attn_in_w'], 'L0_ffn_attn_in_b': _L0_ffn_in['attn_in_b'], 'L0_ffn_attn_out_w': _L0_ffn_in['attn_out_w'], 'L0_ffn_attn_out_b': _L0_ffn_in['attn_out_b'], 'L0_ffn_lstm_wi_f': _L0_ffn_in['lstm_wi_f'], 'L0_ffn_lstm_wh_f': _L0_ffn_in['lstm_wh_f'], 'L0_ffn_lstm_b_f': _L0_ffn_in['lstm_b_f'], 'L0_ffn_lstm_wi_b': _L0_ffn_in['lstm_wi_b'], 'L0_ffn_lstm_wh_b': _L0_ffn_in['lstm_wh_b'], 'L0_ffn_lstm_b_b': _L0_ffn_in['lstm_b_b'], 'L0_ffn_sig_w1': _L0_ffn_in['sig_w1'], 'L0_ffn_sig_b1': _L0_ffn_in['sig_b1'], 'L0_ffn_sig_w2': _L0_ffn_in['sig_w2'], 'L0_ffn_sig_b2': _L0_ffn_in['sig_b2'], 'L0_ffn_tan_w1': _L0_ffn_in['tan_w1'], 'L0_ffn_tan_b1': _L0_ffn_in['tan_b1'], 'L0_ffn_tan_w2': _L0_ffn_in['tan_w2'], 'L0_ffn_tan_b2': _L0_ffn_in['tan_b2'], 'L0_ffn_dec_w1': _L0_ffn_in['dec_w1'], 'L0_ffn_dec_b1': _L0_ffn_in['dec_b1'], 'L0_ffn_dec_w2': _L0_ffn_in['dec_w2'], 'L0_ffn_dec_b2': _L0_ffn_in['dec_b2'], 'L0_ffn_dec_g': _L0_ffn_in['dec_g'], 'L0_ffn_dec_beta': _L0_ffn_in['dec_beta']}

def reference(x, L0_tok_W_patch, L0_tok_b_patch, L0_tok_pos_embed, L0_tok_W_coord, L0_tok_b_coord, L0_tok_W_spinor, L0_tok_b_spinor, L0_tok_W_embed, L0_tok_b_embed, L0_tok_ln_gamma, L0_tok_ln_beta, L0_tok_W_out, L0_tok_b_out, L0_attn_W, L0_attn_b, L0_ffn_router_w, L0_ffn_router_b, L0_ffn_enc_w1, L0_ffn_enc_b1, L0_ffn_enc_w2, L0_ffn_enc_b2, L0_ffn_enc_g, L0_ffn_enc_beta, L0_ffn_attn_in_w, L0_ffn_attn_in_b, L0_ffn_attn_out_w, L0_ffn_attn_out_b, L0_ffn_lstm_wi_f, L0_ffn_lstm_wh_f, L0_ffn_lstm_b_f, L0_ffn_lstm_wi_b, L0_ffn_lstm_wh_b, L0_ffn_lstm_b_b, L0_ffn_sig_w1, L0_ffn_sig_b1, L0_ffn_sig_w2, L0_ffn_sig_b2, L0_ffn_tan_w1, L0_ffn_tan_b1, L0_ffn_tan_w2, L0_ffn_tan_b2, L0_ffn_dec_w1, L0_ffn_dec_b1, L0_ffn_dec_w2, L0_ffn_dec_b2, L0_ffn_dec_g, L0_ffn_dec_beta):
    import jax
    import jax.numpy as jnp

    def _L0_tok_ref(images, W_patch, b_patch, pos_embed, W_coord, b_coord, W_spinor, b_spinor, W_embed, b_embed, ln_gamma, ln_beta, W_out, b_out):
        import jax, jax.numpy as jnp
        import numpy as np
        IMG = 112
        P = 16
        C = 3
        D = 128
        DC = 8
        DS = 4
        NH = IMG // P
        NPATCH = NH * NH
        PDIM = C * P * P
        BATCH = 32
        EPS = 1e-05
        B = images.shape[0]
        patches = images.reshape(B, C, NH, P, NH, P)
        patches = patches.transpose(0, 2, 4, 1, 3, 5).reshape(B, NPATCH, PDIM)
        x = patches @ W_patch + b_patch + pos_embed
        coords = x @ W_coord + b_coord
        spinor = x @ W_spinor + b_spinor
        K0 = jnp.sum(spinor * spinor, axis=-1)
        x_manifold = coords @ W_embed + b_embed
        x_enh = x_manifold * K0[..., None] + x
        mu = jnp.mean(x_enh, axis=-1, keepdims=True)
        var = jnp.mean(jnp.square(x_enh - mu), axis=-1, keepdims=True)
        x_norm = (x_enh - mu) * jax.lax.rsqrt(var + EPS) * ln_gamma + ln_beta
        return x_norm @ W_out + b_out

    def _L0_attn_ref(x, W, b):
        import jax, jax.numpy as jnp
        import numpy as np
        HX_INIT = 1e-06

        def log_g(x):
            return jnp.where(x >= 0, jnp.log(jax.nn.relu(x) + 0.5), -jax.nn.softplus(-x))
        N, L, _ = x.shape
        H = W.shape[0] // 3
        pre = jnp.einsum('nli,oi->nlo', x, W) + b
        f_pre, i_pre, h_pre = jnp.split(pre, 3, axis=-1)
        diff = jax.nn.softplus(-f_pre) - jax.nn.softplus(-i_pre)
        log_f = -jax.nn.softplus(diff)
        log_i = -jax.nn.softplus(-diff)
        log_tilde_h = log_g(h_pre)
        log_h0 = jnp.full((N, 1, H), jnp.log(jnp.asarray(HX_INIT, x.dtype)), dtype=x.dtype)
        log_values = jnp.concatenate([log_h0, log_i + log_tilde_h], axis=1)
        a_star = jnp.pad(jnp.cumsum(log_f, axis=1), ((0, 0), (1, 0), (0, 0)))
        log_h = a_star + jax.lax.cumlogsumexp(log_values - a_star, axis=1)
        return jnp.exp(log_h)[:, 1:]

    def _L0_ffn_ref(x, router_w, router_b, enc_w1, enc_b1, enc_w2, enc_b2, enc_g, enc_beta, attn_in_w, attn_in_b, attn_out_w, attn_out_b, lstm_wi_f, lstm_wh_f, lstm_b_f, lstm_wi_b, lstm_wh_b, lstm_b_b, sig_w1, sig_b1, sig_w2, sig_b2, tan_w1, tan_b1, tan_w2, tan_b2, dec_w1, dec_b1, dec_w2, dec_b2, dec_g, dec_beta):
        import jax, jax.numpy as jnp
        import numpy as np
        from jax import lax
        B, S, IN, D, E, NH = (8, 128, 128, 256, 4, 16)
        DH = D // NH
        EPS = 1e-05
        SCALE = np.float32(1.0 / np.sqrt(DH))

        def _ln(x, g, b):
            m = x.mean(-1, keepdims=True)
            v = ((x - m) ** 2).mean(-1, keepdims=True)
            return (x - m) * lax.rsqrt(v + EPS) * g + b

        def _lstm_dir(x, Wi, Wh, b):
            bsz = x.shape[0]
            h0 = jnp.zeros((bsz, Wh.shape[0]), x.dtype)

            def step(carry, xt):
                h, c = carry
                zg = xt @ Wi + h @ Wh + b
                i, f, g, o = jnp.split(zg, 4, axis=-1)
                c = jax.nn.sigmoid(f) * c + jax.nn.sigmoid(i) * jnp.tanh(g)
                h = jax.nn.sigmoid(o) * jnp.tanh(c)
                return ((h, c), h)
            _, hs = lax.scan(step, (h0, h0), jnp.swapaxes(x, 0, 1))
            return jnp.swapaxes(hs, 0, 1)

        def _expert(x, p):
            ew1, eb1, ew2, eb2, eg, ebeta, aiw, aib, aow, aob, wif, whf, bf, wibk, whbk, bbk, sw1, sb1, sw2, sb2, tw1, tb1, tw2, tb2, dw1, db1, dw2, db2, dg, dbeta = p
            h = _ln(jax.nn.relu(x @ ew1 + eb1) @ ew2 + eb2, eg, ebeta)
            qkv = h @ aiw + aib
            q, k, v = jnp.split(qkv, 3, axis=-1)

            def heads(t):
                return t.reshape(t.shape[0], t.shape[1], NH, DH).transpose(0, 2, 1, 3)
            q, k, v = (heads(q), heads(k), heads(v))
            attn = jax.nn.softmax(jnp.einsum('bhqd,bhkd->bhqk', q, k) * SCALE, axis=-1)
            o = jnp.einsum('bhqk,bhkd->bhqd', attn, v).transpose(0, 2, 1, 3).reshape(h.shape)
            h = o @ aow + aob
            hf = _lstm_dir(h, wif, whf, bf)
            hb = _lstm_dir(h[:, ::-1], wibk, whbk, bbk)[:, ::-1]
            mem = jnp.concatenate([hf, hb], axis=-1)
            gate_s = jax.nn.sigmoid(jax.nn.relu(mem @ sw1 + sb1) @ sw2 + sb2)
            gate_t = jnp.tanh(jax.nn.relu(mem @ tw1 + tb1) @ tw2 + tb2)
            g = gate_s * gate_t
            return _ln(jax.nn.relu(g @ dw1 + db1) @ dw2 + db2, dg, dbeta)

        def _forward(x, router_w, router_b, *p):
            outs = jax.vmap(lambda pe: _expert(x, pe))(tuple(p))
            w = jax.nn.softmax(x @ router_w + router_b, axis=-1)
            return jnp.einsum('ebsd,bse->bsd', outs, w)
        return _forward(x, router_w, router_b, enc_w1, enc_b1, enc_w2, enc_b2, enc_g, enc_beta, attn_in_w, attn_in_b, attn_out_w, attn_out_b, lstm_wi_f, lstm_wh_f, lstm_b_f, lstm_wi_b, lstm_wh_b, lstm_b_b, sig_w1, sig_b1, sig_w2, sig_b2, tan_w1, tan_b1, tan_w2, tan_b2, dec_w1, dec_b1, dec_w2, dec_b2, dec_g, dec_beta)
    h = _L0_tok_ref(x, L0_tok_W_patch, L0_tok_b_patch, L0_tok_pos_embed, L0_tok_W_coord, L0_tok_b_coord, L0_tok_W_spinor, L0_tok_b_spinor, L0_tok_W_embed, L0_tok_b_embed, L0_tok_ln_gamma, L0_tok_ln_beta, L0_tok_W_out, L0_tok_b_out)
    h = h + _L0_attn_ref(_layernorm(h, axis=-1), L0_attn_W, L0_attn_b)
    h = h + _L0_ffn_ref(_layernorm(h, axis=-1), L0_ffn_router_w, L0_ffn_router_b, L0_ffn_enc_w1, L0_ffn_enc_b1, L0_ffn_enc_w2, L0_ffn_enc_b2, L0_ffn_enc_g, L0_ffn_enc_beta, L0_ffn_attn_in_w, L0_ffn_attn_in_b, L0_ffn_attn_out_w, L0_ffn_attn_out_b, L0_ffn_lstm_wi_f, L0_ffn_lstm_wh_f, L0_ffn_lstm_b_f, L0_ffn_lstm_wi_b, L0_ffn_lstm_wh_b, L0_ffn_lstm_b_b, L0_ffn_sig_w1, L0_ffn_sig_b1, L0_ffn_sig_w2, L0_ffn_sig_b2, L0_ffn_tan_w1, L0_ffn_tan_b1, L0_ffn_tan_w2, L0_ffn_tan_b2, L0_ffn_dec_w1, L0_ffn_dec_b1, L0_ffn_dec_w2, L0_ffn_dec_b2, L0_ffn_dec_g, L0_ffn_dec_beta)
    return h

_drawn_inputs = setup_inputs


def setup_inputs(seed=0):
    import zlib

    import numpy as np

    out = dict(_drawn_inputs(seed))
    spreads = {'L0_tok_b_patch': (0.0, 0.1),
     'L0_tok_b_coord': (0.0, 0.1),
     'L0_tok_b_spinor': (0.0, 0.1),
     'L0_tok_b_embed': (0.0, 0.1),
     'L0_tok_ln_gamma': (1.0, 0.2),
     'L0_tok_ln_beta': (0.0, 0.1),
     'L0_tok_b_out': (0.0, 0.1),
     'L0_ffn_router_b': (0.0, 0.537),
     'L0_ffn_enc_b1': (0.0, 0.8),
     'L0_ffn_enc_b2': (0.0, 0.8),
     'L0_ffn_enc_g': (1.0, 0.6),
     'L0_ffn_enc_beta': (0.0, 0.8),
     'L0_ffn_attn_in_b': (0.0, 0.8),
     'L0_ffn_attn_out_b': (0.0, 0.8),
     'L0_ffn_lstm_b_f': (0.0, 0.8),
     'L0_ffn_lstm_b_b': (0.0, 0.8),
     'L0_ffn_sig_b1': (0.0, 0.8),
     'L0_ffn_sig_b2': (0.0, 0.8),
     'L0_ffn_tan_b1': (0.0, 0.8),
     'L0_ffn_tan_b2': (0.0, 0.451),
     'L0_ffn_dec_b1': (0.0, 0.1),
     'L0_ffn_dec_b2': (0.0, 0.1),
     'L0_ffn_dec_g': (1.0, 0.2),
     'L0_ffn_dec_beta': (0.0, 0.1)}
    factors = {'L0_tok_pos_embed': 2.705,
     'L0_ffn_enc_w1': 8.0,
     'L0_ffn_enc_w2': 8.0,
     'L0_ffn_attn_in_w': 8.0,
     'L0_ffn_attn_out_w': 8.0,
     'L0_ffn_lstm_wi_f': 8.0,
     'L0_ffn_lstm_wh_f': 8.0,
     'L0_ffn_lstm_wi_b': 8.0,
     'L0_ffn_lstm_wh_b': 8.0,
     'L0_ffn_sig_w1': 8.0,
     'L0_ffn_sig_w2': 8.0,
     'L0_ffn_tan_w1': 8.0,
     'L0_ffn_tan_w2': 8.0,
     'L0_ffn_dec_w1': 3.368}
    for name, (base, spread) in spreads.items():
        noise = np.random.default_rng([zlib.crc32(name.encode()), seed]).standard_normal(out[name].shape)
        drawn = base * np.exp(spread * noise) if base else spread * noise
        out[name] = jnp.asarray(drawn.astype(out[name].dtype))
    for name, factor in factors.items():
        out[name] = (out[name] * factor).astype(out[name].dtype)
    return out
```

```python
from contextlib import ExitStack

import numpy as np

import concourse.bass as bass
from concourse import mybir

ALU = mybir.AluOpType
ACT = mybir.ActivationFunctionType
AX = mybir.AxisListType
F32 = mybir.dt.float32
BF16 = mybir.dt.bfloat16

P = 128
NB = 64
T = 49
N = NB * T
BC = 8
CH = BC * T
NCH = N // CH
ITERS = NCH // 2
E = 4
DF = 256
NH = 16
DH = DF // NH
TP = 64
KP = 6
PATCH = 16
GRID = 7
EPS = 1e-5
H_INIT = 1e-6

ENC_COLS = [("w1", 256), ("w2", 512), ("aiw", 1536), ("aow", 512), ("b1", 2), ("b2", 2), ("g", 2),
            ("beta", 2), ("bq", 2), ("bk", 2), ("bv", 2), ("bo", 2)]
DEC_COLS = [("sw1", 1024), ("tw1", 1024), ("sw2", 512), ("tw2", 512), ("dw1", 512), ("dw2", 256),
            ("sb1", 2), ("sb2", 2), ("tb1", 2), ("tb2", 2), ("db1", 2), ("db2", 1), ("g", 1), ("beta", 1)]
TOK_COLS = [("wp", KP * P), ("wo", P), ("wg", 3 * P), ("wr", E), ("wc", 8), ("ws", 4), ("bp", 1),
            ("be", 1), ("g", 1), ("beta", 1), ("bo", 1), ("bg", 3), ("pos", T)]
LSTM_COLS = 4 * 2 * 1024
CONST_COLS = [("ident", P), ("mask", 8), ("onesbd", 32)]


def width(cols):
    return sum(w for _, w in cols)


def views(ap, cols):
    out, at = {}, 0
    for name, w in cols:
        out[name] = ap[:, at:at + w]
        at += w
    return out


class Steps:

    def __init__(self, sem, names):
        self.sem, self.names = sem, names.split()
        self.count = len(self.names)

    def before(self, it):
        return it * self.count + 1

    def after(self, it, name):
        return it * self.count + self.names.index(name) + 2


TOK_STEPS = "embed addpos coord coordb sq2 proj man mul add mean center square var sqrt recip norm affine out store"
GRU_STEPS = ("mean center square var sqrt recip norm pre prebias relu abs exp ln soft diff expd expn "
             "gate mix ready")
FIN_STEPS = "mean center square var sqrt recip norm route bias max1 max2 shift exp sum1 sum2 recw weight"
ENC_STEPS = "w1 relu w2 bias mean center square var sqrt recip norm affine"
ATT_STEPS = "copy q qevac k kevac v vevac pairs addbv out store"
PAIR_STEPS = "maskv maskp scores max shift exp turn turned pv recip norm"
DEC_STEPS = ("st1 relu st2 sig tanh gate d1 drelu d2 bias mean center square var sqrt recip norm affine "
             "route mulw add")


def build(nc, patches, tokw, wembed, bcoord, bspin, rbias, consts, selw, encw, lstmw, lstmb, decw, out):
    ctx = ExitStack()
    with ctx:
        def sb(name, shape, dt=F32):
            return ctx.enter_context(nc.sbuf_tensor(name, shape, dt))

        def sem(name):
            return ctx.enter_context(nc.semaphore(name))

        memory = sb("memory", [P, 4 * N])
        hidden = sb("hidden", [P, 2 * N + 16])
        mixed = sb("mixed", [P, 2 * N])
        xn = sb("xn", [P, N])
        acc = sb("acc", [P, N])
        routed = sb("routed", [P, N])
        enc_sb = sb("enc_sb", [P, width(ENC_COLS)])
        lstm_sb = sb("lstm_sb", [P, LSTM_COLS])
        dec_sb = sb("dec_sb", [P, width(DEC_COLS)])
        const_sb = sb("const_sb", [P, width(CONST_COLS)])
        avg = sb("avg", [P, P])
        sel_sb = sb("sel_sb", [P, P])
        vbd = sb("vbd", [P, BC * 8 * 32])
        cell = sb("cell", [P, DF])
        hstep = sb("hstep", [P, DF])
        tcell = sb("tcell", [P, DF])
        eps = sb("eps", [P, 1])
        ones3 = sb("ones3", [P, TP], BF16)
        ps = ctx.enter_context(nc.psum_tensor("ps", [P, 8, 512], F32))

        const = views(const_sb, CONST_COLS)
        ident = const["ident"]
        enc = views(enc_sb, ENC_COLS)
        dec = views(dec_sb, DEC_COLS)
        tok = views(lstm_sb, TOK_COLS)
        tw = width(TOK_COLS)
        wrep = lstm_sb[:, tw:tw + E * P].rearrange("p (e m) -> p e m", e=E)
        rb_sb = lstm_sb[:, tw + 512:tw + 516]
        wembed_sb = lstm_sb[0:8, tw + 516:tw + 644]
        bcoord_sb = lstm_sb[0:8, tw + 644:tw + 645]
        bspin_sb = lstm_sb[0:4, tw + 645:tw + 646]
        ones4 = lstm_sb[0:4, tw + 648:tw + 776]
        mem4 = memory[:, :].rearrange("p (k n) -> p k n", k=4)
        hid2 = hidden[:, 0:2 * N].rearrange("p (k n) -> p k n", k=2)
        mix2 = mixed[:, :].rearrange("p (k n) -> p k n", k=2)

        def held(eng):
            eng.sem_inc(passed[eng.engine == G.engine], 1)

        def bank(b, w=CH, rows=P):
            return ps[0:rows, b, 0:w]

        def two(b):
            return ps[:, b:b + 2, 0:CH]

        def carve(base, start, *widths):
            got, at = [], start
            for w in widths:
                got.append(base[:, at:at + w])
                at += w
            return got, at

        def cols(i, s):
            return bass.ds(i * (2 * CH) + s * CH, CH)

        patches_in, tokw_in, enc_in, lstm_in, lstmb_in, dec_in, saved = (
            sem(x) for x in ("patches_in", "tokw_in", "enc_in", "lstm_in", "lstmb_in", "dec_in", "saved"))
        clear, eps_set = sem("clear"), sem("eps_set")
        passed = sem("passed_pe"), sem("passed_pool")
        G = nc.gpsimd
        tk = [Steps(sem(f"tok_step{s}"), TOK_STEPS) for s in (0, 1)]
        gr = [Steps(sem(f"gru_step{s}"), GRU_STEPS) for s in (0, 1)]
        fi = [Steps(sem(f"fin_step{s}"), FIN_STEPS) for s in (0, 1)]
        en = [Steps(sem(f"enc_step{s}"), ENC_STEPS) for s in (0, 1)]
        at = Steps(sem("att_step"), ATT_STEPS)
        pr = [Steps(sem(f"pair_step{s}"), PAIR_STEPS) for s in (0, 1)]
        de = [Steps(sem(f"dec_step{s}"), DEC_STEPS) for s in (0, 1)]
        scan = sem("scan")
        SCAN = 4
        bias_split = sem("bias_split")
        SPLIT = 7
        x_turned = sem("x_turned")
        z_in = sem("z_in")
        z_lo, z_hi = sem("z_lo"), sem("z_hi")
        gates = sem("gates")
        c_new, ig_new = sem("c_new"), sem("ig_new")
        c_tanh = sem("c_tanh")
        h_new = sem("h_new")
        h_turned = sem("h_turned")
        h_kept = sem("h_kept")
        h_saved = sem("h_saved")

        def ln_space(base, start, k):
            (x, sq, sd, rs), end = carve(base, start, k * CH, k * CH, CH, CH)
            x, sq = (v.rearrange("p (k n) -> p k n", k=k) for v in (x, sq))
            return x, sq, sd, rs, end

        tok_space, gru_space, fin_space, enc_space, dec_space = [], [], [], [], []
        for s in (0, 1):
            x, sq, sd, rs, end = ln_space(hidden, s * (2 * N // 2), 1)
            (raw, co, sp, xm), _ = carve(hidden, end, CH, CH, CH, CH)
            tok_space.append((x, sq, sd, rs, raw, co, sp, xm))
            x, sq, sd, rs, end = ln_space(memory, s * (2 * N), 1)
            (pf, ph, re, ab, ft, gt), _ = carve(memory, end, 2 * CH, CH, 2 * CH, 2 * CH, 2 * CH, CH)
            gru_space.append((x, sq, sd, rs, pf, ph, re, ab, ft, gt))
            (lo, sh, m1), _ = carve(memory, end, 4 * CH, 4 * CH, 2 * CH)
            fin_space.append((x, sq, sd, rs, lo, sh, m1))
            x, sq, sd, rs, end = ln_space(memory, s * (2 * N), 2)
            (a,), _ = carve(memory, end, 2 * CH)
            enc_space.append((x, sq, sd, rs, a))
            base = (hidden, mixed)[s]
            x, sq, sd, rs, end = ln_space(base, 0, 1)
            (a, b, g, y), _ = carve(base, end, 2 * CH, 2 * CH, 2 * CH, CH)
            dec_space.append((x, sq, sd, rs, a, b, g, y))
        (km0, km1, prob0, prob1, pt0, pt1, rec0, rec1, qs, ks, hc, ot), _ = carve(
            memory, 0, 1568, 1568, 1024, 1024, 784, 784, 196, 196, 2 * CH + 16, 2 * CH, 2 * CH + 32, 2 * CH)
        (mx0, mx1), _ = carve(memory, 4 * N - 32, 16, 16)
        masked = [v.rearrange("p (m b h t) -> p m b h t", m=2, b=2, h=8) for v in (km0, km1)]
        prob = [v.rearrange("p (h t) -> p h t", h=NH) for v in (prob0, prob1)]
        probT = [v.rearrange("p (h bt) -> p h bt", h=8) for v in (pt0, pt1)]
        rec = [rec0, rec1]
        mx = [mx0, mx1]
        vb = vbd[:, :].rearrange("p (b h c) -> p b h c", b=BC, h=8)
        hc2 = hc.rearrange("p (k n) -> p k n", k=2)
        (b32, btmp, b3f, gate, xs, hT), _ = carve(hidden, 0, 2048, 1024, 1024, 1024, 512, 256)
        btmp = btmp.bitcast(BF16)
        bias3 = b3f.bitcast(BF16)
        xs4 = xs.rearrange("p (r k c) -> p r k c", r=2, k=2)
        hT2 = hT.rearrange("p (k c) -> p k c", k=2)
        wl = lstm_sb[:, :].rearrange("p (w k n) -> p w k n", w=4, k=2)

        block = ctx.enter_context(nc.Block())

        @block.sync
        def _(sp):
            sp.dma_start(const_sb[:, :], consts).then_inc(tokw_in, 16)
            sp.dma_start(lstm_sb[:, 0:tw], tokw).then_inc(tokw_in, 16)
            sp.dma_start(wembed_sb, wembed).then_inc(tokw_in, 16)
            sp.dma_start(bcoord_sb, bcoord).then_inc(tokw_in, 16)
            sp.dma_start(bspin_sb, bspin).then_inc(tokw_in, 16)
            sp.dma_start(rb_sb, rbias.partition_broadcast(P)).then_inc(tokw_in, 16)
            sp.dma_start(mem4, patches[:, 0:4, :]).then_inc(patches_in, 16)
            sp.dma_start(mix2, patches[:, 4:6, :]).then_inc(patches_in, 16)
            with sp.Fori(0, E) as e:
                sp.wait_ge(at.sem, at.before(e * NCH))
                sp.dma_start(enc_sb[:, :], encw[e]).then_inc(enc_in, 16)
                for s in (0, 1):
                    sp.wait_ge(de[s].sem, de[s].before(e * ITERS))
                sp.dma_start(dec_sb[:, :], decw[e]).then_inc(dec_in, 16)
                sp.dma_start(sel_sb[:, :], selw[e]).then_inc(dec_in, 16)
                for s in (0, 1):
                    sp.wait_ge(fi[s].sem, fi[s].before(ITERS))
                sp.wait_ge(h_saved, e * (2 * T) + 1)
                sp.dma_start(lstm_sb[:, :], lstmw[e]).then_inc(lstm_in, 16)
                sp.wait_ge(at.sem, at.before((e + 1) * NCH))
                sp.dma_start(b32, lstmb[e].partition_broadcast(P)).then_inc(lstmb_in, 16)
            for s in (0, 1):
                sp.wait_ge(de[s].sem, de[s].before(E * ITERS))
            sp.dma_start(out, acc[:, :]).then_inc(saved, 16)
            sp.wait_ge(saved, 16)

        @block.tensor
        def _(pe):
            def mm(o, l, r, start=True, stop=True, **kw):
                return pe.matmul(o, l, r, start=start, stop=stop, **kw)

            def ln_mean(st, it, s, b, x, k):
                for j in range(k):
                    last = mm(bank(b), avg[:, :], x[:, j, :], j == 0, j == k - 1)
                last.then_inc(st[s].sem, 1)

            pe.wait_ge(tokw_in, 96)
            pe.wait_ge(patches_in, 32)
            pe.wait_ge(clear, 1)
            with pe.Fori(0, ITERS) as i:
                for s in (0, 1):
                    x, sq, sd, rs, raw, co, sp_, xm = tok_space[s]
                    st, b = tk[s], 4 * s
                    pe.wait_ge(st.sem, st.before(i))
                    for j in range(KP):
                        src = mem4[:, j, cols(i, s)] if j < 4 else mix2[:, j - 4, cols(i, s)]
                        last = mm(bank(b), tok["wp"][:, j * P:(j + 1) * P], src, j == 0, j == KP - 1)
                    last.then_inc(st.sem, 1)
                for s in (0, 1):
                    x, sq, sd, rs, raw, co, sp_, xm = tok_space[s]
                    st, b = tk[s], 4 * s
                    pe.wait_ge(st.sem, st.after(i, "addpos"))
                    mm(bank(b + 1, rows=8), tok["wc"], raw)
                    mm(bank(b + 2, rows=4), tok["ws"], raw).then_inc(st.sem, 1)
                for s in (0, 1):
                    x, sq, sd, rs, raw, co, sp_, xm = tok_space[s]
                    st, b = tk[s], 4 * s
                    pe.wait_ge(st.sem, st.after(i, "sq2"))
                    mm(bank(b + 3), ones4, sp_[0:4, :])
                    mm(bank(b + 1), wembed_sb, co[0:8, :]).then_inc(st.sem, 1)
                for s in (0, 1):
                    pe.wait_ge(tk[s].sem, tk[s].after(i, "add"))
                    ln_mean(tk, i, s, 4 * s, tok_space[s][0], 1)
                for s in (0, 1):
                    pe.wait_ge(tk[s].sem, tk[s].after(i, "square"))
                    ln_mean(tk, i, s, 4 * s + 2, tok_space[s][1], 1)
                for s in (0, 1):
                    pe.wait_ge(tk[s].sem, tk[s].after(i, "affine"))
                    mm(bank(4 * s), tok["wo"], tok_space[s][5]).then_inc(tk[s].sem, 1)

            with pe.Fori(0, ITERS) as i:
                for s in (0, 1):
                    pe.wait_ge(gr[s].sem, gr[s].before(i))
                    for q in (0, 1):
                        pe.wait_ge(tk[q].sem, tk[q].before(ITERS))
                    mm(bank(4 * s), avg[:, :], acc[:, cols(i, s)]).then_inc(gr[s].sem, 1)
                for s in (0, 1):
                    pe.wait_ge(gr[s].sem, gr[s].after(i, "square"))
                    ln_mean(gr, i, s, 4 * s + 3, gru_space[s][1], 1)
                for s in (0, 1):
                    pe.wait_ge(gr[s].sem, gr[s].after(i, "norm"))
                    for j in range(3):
                        last = mm(bank(4 * s + j), tok["wg"][:, j * P:(j + 1) * P], gru_space[s][0][:, 0, :])
                    last.then_inc(gr[s].sem, 1)

            pe.wait_ge(scan, SCAN)
            with pe.Fori(0, ITERS) as i:
                for s in (0, 1):
                    pe.wait_ge(fi[s].sem, fi[s].before(i))
                    mm(bank(4 * s), avg[:, :], acc[:, cols(i, s)]).then_inc(fi[s].sem, 1)
                for s in (0, 1):
                    pe.wait_ge(fi[s].sem, fi[s].after(i, "square"))
                    ln_mean(fi, i, s, 4 * s + 1, fin_space[s][1], 1)
                for s in (0, 1):
                    pe.wait_ge(fi[s].sem, fi[s].after(i, "norm"))
                    for j in range(E):
                        last = mm(bank(4 * s + j), wrep[:, j, :], xn[:, cols(i, s)])
                    last.then_inc(fi[s].sem, 1)
            for s in (0, 1):
                pe.wait_ge(fi[s].sem, fi[s].before(ITERS))

            with pe.Fori(0, E) as e:
                pe.wait_ge(enc_in, e * 16 + 16)
                for s in (0, 1):
                    pe.wait_ge(de[s].sem, de[s].before(e * ITERS))
                held(pe)
                with pe.Fori(0, ITERS) as i:
                    it = e * ITERS + i
                    for s in (0, 1):
                        pe.wait_ge(en[s].sem, en[s].before(it))
                        for m in (0, 1):
                            last = mm(bank(4 * s + m), enc["w1"][:, m * P:(m + 1) * P], xn[:, cols(i, s)])
                        last.then_inc(en[s].sem, 1)
                    for s in (0, 1):
                        a = enc_space[s][4]
                        pe.wait_ge(en[s].sem, en[s].after(it, "relu"))
                        for m in (0, 1):
                            for k in (0, 1):
                                last = mm(bank(4 * s + 2 + m), enc["w2"][:, k * DF + m * P:k * DF + (m + 1) * P],
                                          a[:, k * CH:(k + 1) * CH], k == 0, k == 1)
                        last.then_inc(en[s].sem, 1)
                    for s in (0, 1):
                        pe.wait_ge(en[s].sem, en[s].after(it, "bias"))
                        ln_mean(en, it, s, 4 * s, enc_space[s][0], 2)
                    for s in (0, 1):
                        pe.wait_ge(en[s].sem, en[s].after(it, "square"))
                        ln_mean(en, it, s, 4 * s + 1, enc_space[s][1], 2)
                with pe.Fori(0, NCH) as j:
                    it = e * NCH + j

                    def project(w0, rhs, step):
                        for m in (0, 1):
                            for k in (0, 1):
                                c = k * 3 * DF + w0 + m * P
                                last = mm(bank(6 + m), enc["aiw"][:, c:c + P], rhs(k), k == 0, k == 1)
                        last.then_inc(at.sem, 1)

                    pe.wait_ge(at.sem, at.after(it, "copy"))
                    project(0, lambda k: hc2[:, k, 0:CH], "q")
                    pe.wait_ge(at.sem, at.after(it, "qevac"))
                    project(DF, lambda k: hc2[:, k, 0:CH], "k")
                    pe.wait_ge(at.sem, at.after(it, "kevac"))
                    for p in range(4):
                        for k in (0, 1):
                            for h in (0, 1):
                                b0 = (2 * p + h) * T
                                last = mm(ps[64 * h:64 * h + 64, 6 + p // 2, (p % 2) * DF:(p % 2 + 1) * DF],
                                          hc2[:, k, b0:b0 + TP],
                                          enc["aiw"][:, k * 3 * DF + 2 * DF:(k + 1) * 3 * DF], k == 0, k == 1)
                    last.then_inc(at.sem, 1)
                    for r in (0, 1):
                        pit = it * 2 + r
                        for s in (0, 1):
                            p, st = 2 * r + s, pr[s]
                            pe.wait_ge(st.sem, st.after(pit, "maskp"))
                            for m in (0, 1):
                                for h in (0, 1):
                                    b0 = m * CH + (2 * p + h) * T
                                    last = mm(ps[64 * h:64 * h + 64, 3 * s + m, 0:CH], qs[:, b0:b0 + TP],
                                              masked[s][:, m, h, :, :].rearrange("p h t -> p (h t)"))
                            last.then_inc(st.sem, 1)
                        for s in (0, 1):
                            st = pr[s]
                            pe.wait_ge(st.sem, st.after(pit, "exp"))
                            for hp in range(8):
                                c = (hp % 4) * P
                                last = pe.transpose(ps[:, 3 * s + hp // 4, c:c + P],
                                                    prob[s][:, 2 * hp:2 * hp + 2, :].rearrange("p h t -> p (h t)"),
                                                    ident)
                            last.then_inc(st.sem, 1)
                        for s in (0, 1):
                            p, st = 2 * r + s, pr[s]
                            pe.wait_ge(st.sem, st.after(pit, "turned"))
                            if r == 0:
                                pe.wait_ge(at.sem, at.after(it, "vevac"))
                            for m in (0, 1):
                                for h in (0, 1):
                                    for q in range(4):
                                        c = m * 2 * T + h * T
                                        mm(ps[32 * q:32 * q + 32, 3 * s + 2, c:c + T],
                                           vb[:, 2 * p + h, 4 * m + q, :],
                                           probT[s][:, 4 * m + q, h * T:(h + 1) * T])
                            for q in range(4):
                                last = mm(ps[32 * q:32 * q + 32, 3 * s + 2, 4 * T:8 * T], const["onesbd"],
                                          probT[s][:, q::4, :])
                            last.then_inc(st.sem, 1)
                    pe.wait_ge(at.sem, at.after(it, "addbv"))
                    for m in (0, 1):
                        for k in (0, 1):
                            c = k * DF + m * P
                            last = mm(bank(6 + m), enc["aow"][:, c:c + P], ot[:, k * CH:(k + 1) * CH], k == 0, k == 1)
                    last.then_inc(at.sem, 1)

                pe.wait_ge(lstm_in, e * 16 + 16)
                pe.wait_ge(bias_split, e * SPLIT + SPLIT)

                def input_part(t, par):
                    pe.wait_ge(x_turned, e * T + t + 1)
                    for half in (0, 1):
                        for d in (0, 1):
                            mm(ps[64 * d:64 * d + 64, 2 * par + half, :], ones3[:, :],
                               bias3[:, d * 1024 + half * 512:d * 1024 + half * 512 + 512],
                               True, False, skip_group_check=True)
                        for k in (0, 1):
                            for d in (0, 1):
                                last = mm(ps[64 * d:64 * d + 64, 2 * par + half, :], xs4[:, par, k, 64 * d:64 * d + 64],
                                          wl[:, 2 * d, k, half * 512:half * 512 + 512], False, False,
                                          skip_group_check=True)
                    last.then_inc(z_in, 1)

                def step(t, par, last_step=False):
                    pe.wait_ge(h_kept, e * (T + 1) + t + 1)
                    for half in (0, 1):
                        for k in (0, 1):
                            for d in (0, 1):
                                last = mm(ps[64 * d:64 * d + 64, 2 * par + half, :], hT2[:, k, 64 * d:64 * d + 64],
                                          wl[:, 2 * d + 1, k, half * 512:half * 512 + 512], False, k == 1,
                                          skip_group_check=True)
                        last.then_inc(z_lo if half == 0 else z_hi, 1)
                    if not last_step:
                        input_part(t + 1, 1 - par)
                    pe.wait_ge(h_new, e * T + t + 1)
                    for k in (0, 1):
                        last = pe.transpose(ps[:, 4, k * P:(k + 1) * P], hstep[:, k * P:(k + 1) * P], ident)
                    last.then_inc(h_turned, 1)

                input_part(0, 0)
                with pe.Fori(0, T // 2) as i:
                    step(i * 2, 0)
                    step(i * 2 + 1, 1)
                step(T - 1, 0, last_step=True)

                pe.wait_ge(dec_in, e * 32 + 32)
                pe.wait_ge(h_saved, e * (2 * T) + 2 * T + 1)
                held(pe)
                with pe.Fori(0, ITERS) as i:
                    it = e * ITERS + i
                    for s in (0, 1):
                        pe.wait_ge(de[s].sem, de[s].before(it))
                        for g, w in enumerate(("sw1", "tw1")):
                            for m in (0, 1):
                                for k in range(4):
                                    last = mm(bank(4 * s + 2 * g + m), dec[w][:, k * DF + m * P:k * DF + (m + 1) * P],
                                              mem4[:, k, cols(i, s)], k == 0, k == 3)
                        last.then_inc(de[s].sem, 1)
                    for s in (0, 1):
                        x, sq, sd, rs, a, b, g_, y = dec_space[s]
                        pe.wait_ge(de[s].sem, de[s].after(it, "relu"))
                        for g, w in enumerate(("sw2", "tw2")):
                            for m in (0, 1):
                                for k in (0, 1):
                                    last = mm(bank(4 * s + 2 * g + m), dec[w][:, k * DF + m * P:k * DF + (m + 1) * P],
                                              (a, b)[g][:, k * CH:(k + 1) * CH], k == 0, k == 1)
                        last.then_inc(de[s].sem, 1)
                    for s in (0, 1):
                        g_ = dec_space[s][6]
                        pe.wait_ge(de[s].sem, de[s].after(it, "gate"))
                        for m in (0, 1):
                            for k in (0, 1):
                                last = mm(bank(4 * s + m), dec["dw1"][:, k * DF + m * P:k * DF + (m + 1) * P],
                                          g_[:, k * CH:(k + 1) * CH], k == 0, k == 1)
                        last.then_inc(de[s].sem, 1)
                    for s in (0, 1):
                        a = dec_space[s][4]
                        pe.wait_ge(de[s].sem, de[s].after(it, "drelu"))
                        for k in (0, 1):
                            last = mm(bank(4 * s + 2), dec["dw2"][:, k * P:(k + 1) * P],
                                      a[:, k * CH:(k + 1) * CH], k == 0, k == 1)
                        last.then_inc(de[s].sem, 1)
                    for s in (0, 1):
                        pe.wait_ge(de[s].sem, de[s].after(it, "bias"))
                        ln_mean(de, it, s, 4 * s + 3, dec_space[s][0], 1)
                    for s in (0, 1):
                        pe.wait_ge(de[s].sem, de[s].after(it, "square"))
                        ln_mean(de, it, s, 4 * s, dec_space[s][1], 1)
                    for s in (0, 1):
                        pe.wait_ge(de[s].sem, de[s].after(it, "affine"))
                        mm(bank(4 * s + 1), sel_sb[:, :], routed[:, cols(i, s)]).then_inc(de[s].sem, 1)

        @block.vector
        def _(dve):
            V = nc.vector

            def ts(o, i, a, b, op0, op1=None):
                return V.tensor_scalar(o, i, a, b, op0, op1) if op1 else V.tensor_scalar(o, i, a, None, op0)

            def ln_center(st, it, s, b, x, src, k, need):
                dve.wait_ge(st[s].sem, st[s].after(it, need))
                V.tensor_tensor(x, src, bank(b).unsqueeze(1).broadcast_to([P, k, CH]),
                                ALU.subtract).then_inc(st[s].sem, 1)

            def ln_rest(st, it, s, x, sd, rs, k, o=None):
                dve.wait_ge(st[s].sem, st[s].after(it, "sqrt"))
                V.reciprocal(rs, sd).then_inc(st[s].sem, 1)
                dve.wait_ge(st[s].sem, st[s].after(it, "recip"))
                V.tensor_tensor(x if o is None else o, x, rs.unsqueeze(1).broadcast_to([P, k, CH]),
                                ALU.mult).then_inc(st[s].sem, 1)

            V.memset(avg[:, :], 1.0 / P)
            V.memset(hidden[:, 2 * N:2 * N + 16], 0.0)
            V.memset(vbd[:, :], 0.0)
            V.memset(routed[:, :], 0.0)
            V.memset(ones3[:, :], 0.0).then_inc(clear, 1)
            dve.wait_ge(clear, 1)
            for r in (0, 32, 64):
                V.memset(ones3[r:r + 1, :], 1.0)
            started = [st.sem for st in tk + gr + fi + en + [at] + pr + de] + [h_saved]
            for c, first in enumerate(started):
                V.memset(cell[:, c:c + 1], 0.0).then_inc(first, 1)
            dve.wait_ge(tokw_in, 96)
            V.memset(ones4, 1.0)
            V.tensor_copy(wrep, tok["wr"].unsqueeze(2).broadcast_to([P, E, P]))
            ts(tok["pos"], tok["pos"], tok["bp"], None, ALU.add).then_inc(clear, 1)

            dve.wait_ge(clear, 2)
            with dve.Fori(0, ITERS) as i:
                for s in (0, 1):
                    x, sq, sd, rs, raw, co, sp_, xm = tok_space[s]
                    st, b = tk[s], 4 * s
                    dve.wait_ge(st.sem, st.after(i, "embed"))
                    V.tensor_tensor(raw.rearrange("p (b t) -> p b t", t=T), bank(b).rearrange("p (b t) -> p b t", t=T),
                                    tok["pos"].unsqueeze(1).broadcast_to([P, BC, T]), ALU.add).then_inc(st.sem, 1)
                for s in (0, 1):
                    x, sq, sd, rs, raw, co, sp_, xm = tok_space[s]
                    st, b = tk[s], 4 * s
                    dve.wait_ge(st.sem, st.after(i, "man"))
                    V.tensor_tensor(xm, xm, bank(b + 3), ALU.mult).then_inc(st.sem, 1)
                    dve.wait_ge(st.sem, st.after(i, "mul"))
                    V.tensor_tensor(x[:, 0, :], xm, raw, ALU.add).then_inc(st.sem, 1)
                for s in (0, 1):
                    x = tok_space[s][0]
                    ln_center(tk, i, s, 4 * s, x, x, 1, "mean")
                for s in (0, 1):
                    x, sq, sd, rs = tok_space[s][:4]
                    ln_rest(tk, i, s, x, sd, rs, 1)

            with dve.Fori(0, ITERS) as i:
                for s in (0, 1):
                    x = gru_space[s][0]
                    ln_center(gr, i, s, 4 * s, x, acc[:, cols(i, s)].unsqueeze(1), 1, "mean")
                for s in (0, 1):
                    x, sq, sd, rs = gru_space[s][:4]
                    ln_rest(gr, i, s, x, sd, rs, 1)
                for s in (0, 1):
                    x, sq, sd, rs, pf, ph, re, ab, ft, gt = gru_space[s]
                    st = gr[s]
                    dve.wait_ge(st.sem, st.after(i, "ln"))
                    V.tensor_tensor(re, re, ab, ALU.add).then_inc(st.sem, 1)
                    dve.wait_ge(st.sem, st.after(i, "soft"))
                    V.tensor_tensor(rs, re[:, 0:CH], re[:, CH:], ALU.subtract)
                    ts(sd, ph, 0.0, None, ALU.min).then_inc(st.sem, 1)
                for s in (0, 1):
                    x, sq, sd, rs, pf, ph, re, ab, ft, gt = gru_space[s]
                    st = gr[s]
                    dve.wait_ge(st.sem, st.after(i, "expn"))
                    ts(ft, ft, 1.0, None, ALU.add)
                    ts(gt, gt, 1.0, None, ALU.add).then_inc(st.sem, 1)
                    dve.wait_ge(st.sem, st.after(i, "gate"))
                    V.reciprocal(ft, ft)
                    V.reciprocal(gt, gt).then_inc(st.sem, 1)
                    dve.wait_ge(st.sem, st.after(i, "mix"))
                    V.scalar_tensor_tensor(out=gt, in0=ph, scalar=0.0, in1=gt, op0=ALU.max,
                                           op1=ALU.add).then_inc(clear, 1)
                    dve.wait_ge(clear, 3 + 2 * i + s)
                    V.tensor_copy(mixed[:, cols(i, s)], ft[:, 0:CH])
                    V.tensor_tensor(mixed[:, bass.ds(i * (2 * CH) + (s * CH + N), CH)], gt, ft[:, CH:],
                                    ALU.mult).then_inc(st.sem, 1)
            for s in (0, 1):
                dve.wait_ge(gr[s].sem, gr[s].before(ITERS))
            f0 = mixed[:, 0:N].rearrange("p (b t) -> p b t", t=T)[:, :, 0]
            g0 = mixed[:, N:2 * N].rearrange("p (b t) -> p b t", t=T)[:, :, 0]
            V.scalar_tensor_tensor(out=g0, in0=f0, scalar=H_INIT, in1=g0, op0=ALU.mult, op1=ALU.add).then_inc(scan, 1)
            dve.wait_ge(scan, 1)
            V.memset(f0, 0.0).then_inc(scan, 1)
            dve.wait_ge(scan, 2)
            V.tensor_tensor_scan(memory[:, 0:N], mixed[:, 0:N], mixed[:, N:2 * N], 0.0, ALU.mult,
                                 ALU.add).then_inc(scan, 1)
            dve.wait_ge(scan, 3)
            V.tensor_tensor(acc[:, :], acc[:, :], memory[:, 0:N], ALU.add).then_inc(scan, 1)

            with dve.Fori(0, ITERS) as i:
                for s in (0, 1):
                    x = fin_space[s][0]
                    ln_center(fi, i, s, 4 * s, x, acc[:, cols(i, s)].unsqueeze(1), 1, "mean")
                for s in (0, 1):
                    x, sq, sd, rs = fin_space[s][:4]
                    ln_rest(fi, i, s, x, sd, rs, 1, xn[:, cols(i, s)].unsqueeze(1))
                for s in (0, 1):
                    x, sq, sd, rs, lo, sh, m1 = fin_space[s]
                    st = fi[s]
                    lo4 = lo.rearrange("p (e n) -> p e n", e=E)
                    dve.wait_ge(st.sem, st.after(i, "bias"))
                    V.tensor_tensor(m1, lo[:, 0:2 * CH], lo[:, 2 * CH:], ALU.max).then_inc(st.sem, 1)
                    dve.wait_ge(st.sem, st.after(i, "max1"))
                    V.tensor_tensor(rs, m1[:, 0:CH], m1[:, CH:], ALU.max).then_inc(st.sem, 1)
                    dve.wait_ge(st.sem, st.after(i, "max2"))
                    V.tensor_tensor(lo4, lo4, rs.unsqueeze(1).broadcast_to([P, E, CH]), ALU.subtract).then_inc(st.sem, 1)
                for s in (0, 1):
                    x, sq, sd, rs, lo, sh, m1 = fin_space[s]
                    st = fi[s]
                    dve.wait_ge(st.sem, st.after(i, "exp"))
                    V.tensor_tensor(m1, sh[:, 0:2 * CH], sh[:, 2 * CH:], ALU.add).then_inc(st.sem, 1)
                    dve.wait_ge(st.sem, st.after(i, "sum1"))
                    V.tensor_tensor(rs, m1[:, 0:CH], m1[:, CH:], ALU.add).then_inc(st.sem, 1)
                    dve.wait_ge(st.sem, st.after(i, "sum2"))
                    V.reciprocal(sd, rs).then_inc(st.sem, 1)
                    dve.wait_ge(st.sem, st.after(i, "recw"))
                    for k in range(E):
                        r = 32 * k
                        last = V.tensor_tensor(routed[r:r + 1, cols(i, s)], sh[r:r + 1, k * CH:(k + 1) * CH],
                                               sd[r:r + 1, :], ALU.mult)
                    last.then_inc(st.sem, 1)

            with dve.Fori(0, E) as e:
                with dve.Fori(0, ITERS) as i:
                    it = e * ITERS + i
                    for s in (0, 1):
                        x = enc_space[s][0]
                        dve.wait_ge(en[s].sem, en[s].after(it, "mean"))
                        V.scalar_tensor_tensor(out=x, in0=bank(4 * s).unsqueeze(1).broadcast_to([P, 2, CH]),
                                               scalar=-0.5, in1=x, op0=ALU.mult, op1=ALU.add).then_inc(en[s].sem, 1)
                    for s in (0, 1):
                        x, sq, sd, rs, a = enc_space[s]
                        ln_rest(en, it, s, x, sd, rs, 2)
                dve.wait_ge(en[0].sem, en[0].before((e + 1) * ITERS))
                dve.wait_ge(en[1].sem, en[1].before((e + 1) * ITERS))
                for s in (0, 1):
                    V.memset(prob[s][:, :, T:TP], 0.0)
                V.memset(qs[:, 2 * CH:2 * CH + 16], 0.0)
                with dve.Fori(0, NCH) as j:
                    it = e * NCH + j
                    dve.wait_ge(at.sem, at.after(it, "q"))
                    for m in (0, 1):
                        last = ts(qs[:, m * CH:(m + 1) * CH], bank(6 + m), enc["bq"][:, m:m + 1], DH ** -0.5,
                                  ALU.add, ALU.mult)
                    last.then_inc(at.sem, 1)
                    for r in (0, 1):
                        pit = it * 2 + r
                        for s in (0, 1):
                            p = 2 * r + s
                            dve.wait_ge(at.sem, at.after(it, "kevac"))
                            kk = ks[:, 2 * p * T:2 * (p + 1) * T].rearrange("p (b t) -> p b t", b=2)
                            V.tensor_tensor(masked[s][:, 0, :, :, :], kk.unsqueeze(2).broadcast_to([P, 2, 8, T]),
                                            const["mask"].unsqueeze(1).unsqueeze(3).broadcast_to([P, 2, 8, T]),
                                            ALU.mult).then_inc(pr[s].sem, 1)
                        if r == 0:
                            dve.wait_ge(at.sem, at.after(it, "v"))
                            for half in (0, 1):
                                for h in (0, 1):
                                    for o in (0, 1):
                                        src = ps[64 * h:64 * h + 64, 6 + half, :].rearrange(
                                            "p (b g o d) -> p b g o d", b=2, g=8, o=2)[:, :, :, o, :]
                                        last = V.tensor_copy(
                                            vb[64 * o:64 * o + 64, 4 * half + h:4 * half + h + 3:2, :, DH * o:DH * (o + 1)], src)
                            last.then_inc(at.sem, 1)
                        for s in (0, 1):
                            st = pr[s]
                            sc = two(3 * s).rearrange("p m (h t) -> p m h t", t=T)
                            dve.wait_ge(st.sem, st.after(pit, "scores"))
                            V.tensor_reduce(mx[s].rearrange("p (m h) -> p m h", m=2), sc, AX.X, ALU.max).then_inc(st.sem, 1)
                            dve.wait_ge(st.sem, st.after(pit, "max"))
                            V.tensor_tensor(prob[s][:, :, 0:T].rearrange("p (m h) t -> p m h t", m=2), sc,
                                            mx[s].rearrange("p (m h) -> p m h", m=2).unsqueeze(3).broadcast_to([P, 2, 8, T]),
                                            ALU.subtract).then_inc(st.sem, 1)
                        for s in (0, 1):
                            p, st = 2 * r + s, pr[s]
                            dve.wait_ge(st.sem, st.after(pit, "pv"))
                            V.reciprocal(rec[s], ps[:, 3 * s + 2, 4 * T:8 * T]).then_inc(st.sem, 1)
                            dve.wait_ge(st.sem, st.after(pit, "recip"))
                            o = ot.rearrange("p (m n) -> p m n", m=2)[:, :, 2 * p * T:2 * (p + 1) * T]
                            V.tensor_tensor(o, ps[:, 3 * s + 2, 0:4 * T].rearrange("p (m n) -> p m n", m=2),
                                            rec[s].rearrange("p (m n) -> p m n", m=2), ALU.mult).then_inc(st.sem, 1)
                    for s in (0, 1):
                        dve.wait_ge(pr[s].sem, pr[s].before(it * 2 + 2))
                    V.memset(mx[0][:, 0:1], 0.0).then_inc(at.sem, 1)
                    for m in (0, 1):
                        last = ts(ot[:, m * CH:(m + 1) * CH], ot[:, m * CH:(m + 1) * CH], enc["bv"][:, m:m + 1],
                                  None, ALU.add)
                    last.then_inc(at.sem, 1)

                dve.wait_ge(lstmb_in, e * 16 + 16)
                n = e * SPLIT
                V.tensor_copy(btmp, b32).then_inc(bias_split, 1)
                dve.wait_ge(bias_split, n + 1)
                V.tensor_copy(bias3[0:32, :], btmp[0:32, :])
                V.tensor_copy(bias3[96:128, :], btmp[96:128, :])
                V.tensor_tensor(b32, b32, btmp, ALU.subtract).then_inc(bias_split, 1)
                dve.wait_ge(bias_split, n + 2)
                V.tensor_copy(btmp, b32).then_inc(bias_split, 1)
                dve.wait_ge(bias_split, n + 3)
                V.tensor_copy(bias3[32:64, :], btmp[32:64, :])
                V.tensor_tensor(b32, b32, btmp, ALU.subtract).then_inc(bias_split, 1)
                dve.wait_ge(bias_split, n + 4)
                V.tensor_copy(btmp, b32).then_inc(bias_split, 1)
                dve.wait_ge(bias_split, n + 5)
                V.tensor_copy(bias3[64:96, :], btmp[64:96, :]).then_inc(bias_split, 1)
                V.memset(cell[:, :], 0.0).then_inc(bias_split, 1)
                dve.wait_ge(bias_split, n + SPLIT)
                V.memset(hT, 0.0).then_inc(h_kept, 1)
                with dve.Fori(0, T) as t:
                    k = e * T + t
                    dve.wait_ge(gates, k * 3 + 1)
                    V.tensor_tensor(cell[:, :], cell[:, :], gate[:, DF:2 * DF], ALU.mult).then_inc(c_new, 1)
                    dve.wait_ge(gates, k * 3 + 2)
                    V.tensor_tensor(gate[:, 0:DF], gate[:, 0:DF], gate[:, 2 * DF:3 * DF], ALU.mult).then_inc(ig_new, 1)
                    dve.wait_ge(c_new, k * 2 + 1)
                    dve.wait_ge(ig_new, k + 1)
                    V.tensor_tensor(cell[:, :], cell[:, :], gate[:, 0:DF], ALU.add).then_inc(c_new, 1)
                    dve.wait_ge(c_tanh, k + 1)
                    dve.wait_ge(gates, k * 3 + 3)
                    V.tensor_tensor(hstep[:, :], gate[:, 3 * DF:], tcell[:, :], ALU.mult).then_inc(h_new, 1)
                    dve.wait_ge(h_turned, k + 1)
                    dve.wait_ge(h_saved, k * 2 + 1)
                    V.tensor_copy(hT, ps[:, 4, 0:DF]).then_inc(h_kept, 1)

                with dve.Fori(0, ITERS) as i:
                    it = e * ITERS + i
                    for s in (0, 1):
                        x, sq, sd, rs, a, b, g_, y = dec_space[s]
                        dve.wait_ge(de[s].sem, de[s].after(it, "tanh"))
                        V.tensor_tensor(g_, a, b, ALU.mult).then_inc(de[s].sem, 1)
                    for s in (0, 1):
                        x = dec_space[s][0]
                        ln_center(de, it, s, 4 * s + 3, x, x, 1, "mean")
                    for s in (0, 1):
                        x, sq, sd, rs = dec_space[s][:4]
                        ln_rest(de, it, s, x, sd, rs, 1)
                    for s in (0, 1):
                        y = dec_space[s][7]
                        dve.wait_ge(de[s].sem, de[s].after(it, "route"))
                        V.tensor_tensor(y, y, bank(4 * s + 1), ALU.mult).then_inc(de[s].sem, 1)
                        dve.wait_ge(de[s].sem, de[s].after(it, "mulw"))
                        V.tensor_tensor(acc[:, cols(i, s)], acc[:, cols(i, s)], y, ALU.add).then_inc(de[s].sem, 1)

        @block.scalar
        def _(act):
            A = nc.scalar.activation
            ID = ACT.Identity

            def ln_square(st, it, s, sq, x):
                act.wait_ge(st[s].sem, st[s].after(it, "center"))
                A(sq, x, ACT.Square).then_inc(st[s].sem, 1)

            def ln_sqrt(st, it, s, sd, b, scale=1.0):
                act.wait_ge(st[s].sem, st[s].after(it, "var"))
                A(sd, bank(b), ACT.Sqrt, bias=eps[:, 0:1], scale=scale).then_inc(st[s].sem, 1)

            act.wait_ge(eps_set, 1)
            with act.Fori(0, ITERS) as i:
                for s in (0, 1):
                    x, sq, sd, rs, raw, co, sp_, xm = tok_space[s]
                    st, b = tk[s], 4 * s
                    act.wait_ge(st.sem, st.after(i, "coord"))
                    A(co[0:8, :], bank(b + 1, rows=8), ID, bias=bcoord_sb).then_inc(st.sem, 1)
                    A(sp_[0:4, :], bank(b + 2, rows=4), ACT.Square, bias=bspin_sb).then_inc(st.sem, 1)
                for s in (0, 1):
                    x, sq, sd, rs, raw, co, sp_, xm = tok_space[s]
                    st, b = tk[s], 4 * s
                    act.wait_ge(st.sem, st.after(i, "proj"))
                    A(xm, bank(b + 1), ID, bias=tok["be"]).then_inc(st.sem, 1)
                for s in (0, 1):
                    ln_square(tk, i, s, tok_space[s][1], tok_space[s][0])
                for s in (0, 1):
                    ln_sqrt(tk, i, s, tok_space[s][2], 4 * s + 2)
                for s in (0, 1):
                    x, sq, sd, rs, raw, co, sp_, xm = tok_space[s]
                    act.wait_ge(tk[s].sem, tk[s].after(i, "norm"))
                    A(co, x[:, 0, :], ID, bias=tok["beta"], scale=tok["g"]).then_inc(tk[s].sem, 1)
                for s in (0, 1):
                    act.wait_ge(tk[s].sem, tk[s].after(i, "out"))
                    A(acc[:, cols(i, s)], bank(4 * s), ID, bias=tok["bo"]).then_inc(tk[s].sem, 1)

            with act.Fori(0, ITERS) as i:
                for s in (0, 1):
                    ln_square(gr, i, s, gru_space[s][1], gru_space[s][0])
                for s in (0, 1):
                    ln_sqrt(gr, i, s, gru_space[s][2], 4 * s + 3)
                for s in (0, 1):
                    x, sq, sd, rs, pf, ph, re, ab, ft, gt = gru_space[s]
                    st = gr[s]
                    act.wait_ge(st.sem, st.after(i, "pre"))
                    for m in (0, 1):
                        A(pf[:, m * CH:(m + 1) * CH], bank(4 * s + m), ID, bias=tok["bg"][:, m:m + 1])
                    A(ph, bank(4 * s + 2), ID, bias=tok["bg"][:, 2:3]).then_inc(st.sem, 1)
                    act.wait_ge(st.sem, st.after(i, "prebias"))
                    A(re, pf, ACT.Relu, scale=-1.0).then_inc(st.sem, 1)
                    A(ab, pf, ACT.Abs).then_inc(st.sem, 1)
                    act.wait_ge(st.sem, st.after(i, "abs"))
                    A(ab, ab, ACT.Exp, scale=-1.0).then_inc(st.sem, 1)
                for s in (0, 1):
                    st, ab = gr[s], gru_space[s][7]
                    act.wait_ge(st.sem, st.after(i, "exp"))
                    A(ab, ab, ACT.Ln, bias=1.0).then_inc(st.sem, 1)
                for s in (0, 1):
                    x, sq, sd, rs, pf, ph, re, ab, ft, gt = gru_space[s]
                    st = gr[s]
                    act.wait_ge(st.sem, st.after(i, "diff"))
                    A(ft[:, 0:CH], rs, ACT.Exp)
                    A(ft[:, CH:], rs, ACT.Exp, scale=-1.0).then_inc(st.sem, 1)
                    A(gt, sd, ACT.Exp, scale=-1.0).then_inc(st.sem, 1)

            with act.Fori(0, ITERS) as i:
                for s in (0, 1):
                    ln_square(fi, i, s, fin_space[s][1], fin_space[s][0])
                for s in (0, 1):
                    ln_sqrt(fi, i, s, fin_space[s][2], 4 * s + 1)
                for s in (0, 1):
                    lo, st = fin_space[s][4], fi[s]
                    act.wait_ge(st.sem, st.after(i, "route"))
                    for k in range(E):
                        last = A(lo[:, k * CH:(k + 1) * CH], bank(4 * s + k), ID, bias=rb_sb[:, k:k + 1])
                    last.then_inc(st.sem, 1)
                for s in (0, 1):
                    lo, sh, st = fin_space[s][4], fin_space[s][5], fi[s]
                    act.wait_ge(st.sem, st.after(i, "shift"))
                    A(sh, lo, ACT.Exp).then_inc(st.sem, 1)

            with act.Fori(0, E) as e:
                with act.Fori(0, ITERS) as i:
                    it = e * ITERS + i
                    for s in (0, 1):
                        a, st = enc_space[s][4], en[s]
                        act.wait_ge(st.sem, st.after(it, "w1"))
                        for m in (0, 1):
                            last = A(a[:, m * CH:(m + 1) * CH], bank(4 * s + m), ACT.Relu, bias=enc["b1"][:, m:m + 1])
                        last.then_inc(st.sem, 1)
                    for s in (0, 1):
                        x, st = enc_space[s][0], en[s]
                        act.wait_ge(st.sem, st.after(it, "w2"))
                        for m in (0, 1):
                            last = A(x[:, m, :], bank(4 * s + 2 + m), ID, bias=enc["b2"][:, m:m + 1])
                        last.then_inc(st.sem, 1)
                    for s in (0, 1):
                        ln_square(en, it, s, enc_space[s][1], enc_space[s][0])
                    for s in (0, 1):
                        ln_sqrt(en, it, s, enc_space[s][2], 4 * s + 1, scale=0.5)
                    for s in (0, 1):
                        x, st = enc_space[s][0], en[s]
                        act.wait_ge(st.sem, st.after(it, "norm"))
                        for m in (0, 1):
                            last = A(hid2[:, m, cols(i, s)], x[:, m, :], ID, bias=enc["beta"][:, m:m + 1],
                                     scale=enc["g"][:, m:m + 1])
                        last.then_inc(st.sem, 1)
                with act.Fori(0, NCH) as j:
                    it = e * NCH + j
                    act.wait_ge(at.sem, at.after(it, "k"))
                    for m in (0, 1):
                        last = A(ks[:, m * CH:(m + 1) * CH], bank(6 + m), ID, bias=enc["bk"][:, m:m + 1])
                    last.then_inc(at.sem, 1)
                    for r in (0, 1):
                        pit = it * 2 + r
                        for s in (0, 1):
                            st = pr[s]
                            act.wait_ge(st.sem, st.after(pit, "shift"))
                            A(prob[s][:, :, 0:T], prob[s][:, :, 0:T], ACT.Exp).then_inc(st.sem, 1)
                        for s in (0, 1):
                            st = pr[s]
                            act.wait_ge(st.sem, st.after(pit, "turn"))
                            src = ps[:, 3 * s:3 * s + 2, :].rearrange("p m (hb t) -> p m hb t", t=TP)[:, :, :, 0:T]
                            A(probT[s].rearrange("p (m h) (b t) -> p m (h b) t", m=2, b=2), src,
                              ACT.Copy).then_inc(st.sem, 1)
                    act.wait_ge(at.sem, at.after(it, "out"))
                    for m in (0, 1):
                        last = A(mix2[:, m, bass.ts(j, CH)], bank(6 + m), ID, bias=enc["bo"][:, m:m + 1])
                    last.then_inc(at.sem, 1)
                def lstm_step(t, par):
                    k = e * T + t
                    act.wait_ge(z_lo, k + 1)
                    A(gate[:, 0:2 * DF], ps[:, 2 * par, :], ACT.Sigmoid).then_inc(gates, 1)
                    act.wait_ge(z_hi, k + 1)
                    A(gate[:, 2 * DF:3 * DF], ps[:, 2 * par + 1, 0:DF], ACT.Tanh).then_inc(gates, 1)
                    A(gate[:, 3 * DF:], ps[:, 2 * par + 1, DF:], ACT.Sigmoid).then_inc(gates, 1)
                    act.wait_ge(c_new, k * 2 + 2)
                    A(tcell[:, :], cell[:, :], ACT.Tanh).then_inc(c_tanh, 1)

                with act.Fori(0, T // 2) as i:
                    lstm_step(i * 2, 0)
                    lstm_step(i * 2 + 1, 1)
                lstm_step(T - 1, 0)

                with act.Fori(0, ITERS) as i:
                    it = e * ITERS + i
                    for s in (0, 1):
                        x, sq, sd, rs, a, b, g_, y = dec_space[s]
                        act.wait_ge(de[s].sem, de[s].after(it, "st1"))
                        for m in (0, 1):
                            A(a[:, m * CH:(m + 1) * CH], bank(4 * s + m), ACT.Relu, bias=dec["sb1"][:, m:m + 1])
                        for m in (0, 1):
                            last = A(b[:, m * CH:(m + 1) * CH], bank(4 * s + 2 + m), ACT.Relu, bias=dec["tb1"][:, m:m + 1])
                        last.then_inc(de[s].sem, 1)
                    for s in (0, 1):
                        x, sq, sd, rs, a, b, g_, y = dec_space[s]
                        act.wait_ge(de[s].sem, de[s].after(it, "st2"))
                        for m in (0, 1):
                            last = A(a[:, m * CH:(m + 1) * CH], bank(4 * s + m), ACT.Sigmoid, bias=dec["sb2"][:, m:m + 1])
                        last.then_inc(de[s].sem, 1)
                        for m in (0, 1):
                            last = A(b[:, m * CH:(m + 1) * CH], bank(4 * s + 2 + m), ACT.Tanh, bias=dec["tb2"][:, m:m + 1])
                        last.then_inc(de[s].sem, 1)
                    for s in (0, 1):
                        a = dec_space[s][4]
                        act.wait_ge(de[s].sem, de[s].after(it, "d1"))
                        for m in (0, 1):
                            last = A(a[:, m * CH:(m + 1) * CH], bank(4 * s + m), ACT.Relu, bias=dec["db1"][:, m:m + 1])
                        last.then_inc(de[s].sem, 1)
                    for s in (0, 1):
                        x = dec_space[s][0]
                        act.wait_ge(de[s].sem, de[s].after(it, "d2"))
                        A(x[:, 0, :], bank(4 * s + 2), ID, bias=dec["db2"]).then_inc(de[s].sem, 1)
                    for s in (0, 1):
                        ln_square(de, it, s, dec_space[s][1], dec_space[s][0])
                    for s in (0, 1):
                        ln_sqrt(de, it, s, dec_space[s][2], 4 * s)
                    for s in (0, 1):
                        x, y = dec_space[s][0], dec_space[s][7]
                        act.wait_ge(de[s].sem, de[s].after(it, "norm"))
                        A(y, x[:, 0, :], ID, bias=dec["beta"], scale=dec["g"]).then_inc(de[s].sem, 1)

        @block.gpsimd
        def _(pool):
            G.memset(eps[:, :], EPS).then_inc(eps_set, 1)
            with pool.Fori(0, E) as e:
                for s in (0, 1):
                    pool.wait_ge(en[s].sem, en[s].before((e + 1) * ITERS))
                held(pool)
                with pool.Fori(0, NCH) as j:
                    it = e * NCH + j
                    pool.wait_ge(at.sem, at.before(it))
                    held(pool)
                    for k in (0, 1):
                        last = G.tensor_copy(hc2[:, k, :], hidden[:, bass.ds(j * CH + k * N, CH + 16)])
                    last.then_inc(at.sem, 1)
                    for r in (0, 1):
                        pit = it * 2 + r
                        for s in (0, 1):
                            p, st = 2 * r + s, pr[s]
                            pool.wait_ge(st.sem, st.after(pit, "maskv"))
                            kk = ks[:, CH + 2 * p * T:CH + 2 * (p + 1) * T].rearrange("p (b t) -> p b t", b=2)
                            G.tensor_tensor(masked[s][:, 1, :, :, :], kk.unsqueeze(2).broadcast_to([P, 2, 8, T]),
                                            const["mask"].unsqueeze(1).unsqueeze(3).broadcast_to([P, 2, 8, T]),
                                            ALU.mult).then_inc(st.sem, 1)
                pool.wait_ge(at.sem, at.before((e + 1) * NCH))
                held(pool)

                def save(t):
                    k = e * T + t
                    pool.wait_ge(h_kept, e * (T + 1) + t + 2)
                    held(pool)
                    G.tensor_copy(mem4[:, 0:2, bass.ds(t, NB, step=T)], hT2[:, :, 0:64]).then_inc(h_saved, 1)
                    G.tensor_copy(mem4[:, 2:4, bass.ds(t * -1 + (T - 1), NB, step=T)], hT2[:, :, 64:128]).then_inc(h_saved, 1)

                def turn(t, par):
                    G.tensor_copy(xs4[:, par, :, 0:64], mix2[:, :, bass.ds(t, NB, step=T)])
                    G.tensor_copy(xs4[:, par, :, 64:128],
                                  mix2[:, :, bass.ds(t * -1 + (T - 1), NB, step=T)]).then_inc(x_turned, 1)

                turn(0, 0)
                turn(1, 1)
                with pool.Fori(0, T // 2 - 1) as i:
                    for par in (0, 1):
                        save(i * 2 + par)
                        pool.wait_ge(z_in, e * T + i * 2 + (par + 1))
                        held(pool)
                        turn(i * 2 + (par + 2), par)
                save(T - 3)
                pool.wait_ge(z_in, e * T + T - 2)
                held(pool)
                turn(T - 1, 0)
                save(T - 2)
                save(T - 1)


def pack(inputs, names, rows):
    parts = []
    for name in names:
        a = np.asarray(inputs["L0_ffn_" + name])
        if a.ndim == 2:
            a = a[:, :, None]
        e, r, w = a.shape
        parts.append(a.reshape(e, r // P, P, w).transpose(0, 2, 1, 3).reshape(e, P, -1))
    return np.ascontiguousarray(np.concatenate(parts, axis=2))


def kernel(**inputs):
    import concourse.bacc as bacc
    from concourse.bass_utils import run_bass_kernel_spmd

    t = {k[7:]: np.asarray(v) for k, v in inputs.items() if k.startswith("L0_tok_")}
    x = np.asarray(inputs["x"])
    patches = x.reshape(NB, 3, GRID, PATCH, GRID, PATCH).transpose(1, 3, 5, 0, 2, 4).reshape(KP, P, N)
    patches = patches.transpose(1, 0, 2)
    wp = t["W_patch"].reshape(KP, P, P).transpose(1, 0, 2).reshape(P, KP * P)
    wg = np.asarray(inputs["L0_attn_W"]).T
    bg = np.asarray(inputs["L0_attn_b"]).reshape(3, P).T
    tokw = np.concatenate(
        [wp, t["W_out"], wg, np.asarray(inputs["L0_ffn_router_w"]), t["W_coord"], t["W_spinor"]]
        + [t[k][:, None] for k in ("b_patch", "b_embed", "ln_gamma", "ln_beta", "b_out")]
        + [bg, t["pos_embed"][0].T], axis=1)
    f = np.float32
    consts = np.concatenate(
        [np.eye(P, dtype=f), np.kron(np.eye(8, dtype=f), np.ones((DH, 1), f)),
         np.kron(np.eye(2, dtype=f), np.ones((TP, DH), f))], axis=1)
    selw = np.zeros((E, P, P), f)
    for k in range(E):
        selw[k, 32 * k] = 1.0
    encw = pack(inputs, ["enc_w1", "enc_w2", "attn_in_w", "attn_out_w", "enc_b1", "enc_b2", "enc_g", "enc_beta",
                         "attn_in_b", "attn_out_b"], 0)
    decw = pack(inputs, ["sig_w1", "tan_w1", "sig_w2", "tan_w2", "dec_w1", "dec_w2", "sig_b1", "sig_b2", "tan_b1",
                         "tan_b2", "dec_b1", "dec_b2", "dec_g", "dec_beta"], 0)
    lstmw = pack(inputs, ["lstm_wi_f", "lstm_wh_f", "lstm_wi_b", "lstm_wh_b"], 0)
    lstmb = np.concatenate([np.asarray(inputs["L0_ffn_lstm_b_f"]), np.asarray(inputs["L0_ffn_lstm_b_b"])], axis=1)
    arrays = {
        "patches": patches, "tokw": tokw, "wembed": t["W_embed"], "bcoord": t["b_coord"][:, None],
        "bspin": t["b_spinor"][:, None], "rbias": np.asarray(inputs["L0_ffn_router_b"]), "consts": consts,
        "selw": selw, "encw": encw, "lstmw": lstmw, "lstmb": lstmb, "decw": decw,
    }
    arrays = {k: np.ascontiguousarray(v) for k, v in arrays.items()}
    nc = bacc.Bacc("TRN2", target_bir_lowering=False, num_devices=1)
    aps = {k: nc.dram_tensor("in_" + k, v.shape, mybir.dt.from_np(v.dtype), kind="ExternalInput").ap()
           for k, v in arrays.items()}
    out = nc.dram_tensor("out", (P, N), F32, kind="ExternalOutput").ap()
    build(nc, out=out, **aps)
    r = run_bass_kernel_spmd(nc, [{"in_" + k: v for k, v in arrays.items()}], core_ids=[0])
    return np.ascontiguousarray(r.results[0]["out"].reshape(P, NB, T).transpose(1, 2, 0))
```

```python
from contextlib import ExitStack

import numpy as np

import concourse.bass as bass
from concourse import mybir

ALU = mybir.AluOpType
ACT = mybir.ActivationFunctionType
AX = mybir.AxisListType
F32 = mybir.dt.float32
BF16 = mybir.dt.bfloat16

P = 128
NB = 64
T = 49
N = NB * T
BC = 8
CH = BC * T
NCH = N // CH
STREAMS = 4
S4 = range(STREAMS)
ITERS = NCH // STREAMS
SPLIT_CHUNK = 4
SLOTS = 8
LOOPS = NCH // 2
E = 4
DF = 256
NH = 16
DH = DF // NH
TP = 64
KP = 6
PATCH = 16
GRID = 7
EPS = 1e-5
H_INIT = 1e-6

ENC_COLS = [("w1", 256), ("w2", 512), ("aiw", 1536), ("aow", 512), ("b1", 2), ("b2", 2), ("g", 2),
            ("beta", 2), ("bq", 2), ("bk", 2), ("bv", 2), ("bo", 2)]
DEC_COLS = [("sw1", 1024), ("tw1", 1024), ("sw2", 512), ("tw2", 512), ("dw1", 512), ("dw2", 256),
            ("sb1", 2), ("sb2", 2), ("tb1", 2), ("tb2", 2), ("db1", 2), ("db2", 1), ("g", 1), ("beta", 1)]
TOK_COLS = [("wp", KP * P), ("wo", P), ("wg", 3 * P), ("wr", E), ("wc", 8), ("ws", 4), ("bp", 1),
            ("be", 1), ("g", 1), ("beta", 1), ("bo", 1), ("bg", 3), ("pos", T)]
LSTM_COLS = 4 * 2 * 1024
CONST_COLS = [("ident", P), ("mask", 8), ("onesbd", 32)]


def width(cols):
    return sum(w for _, w in cols)


def views(ap, cols):
    out, at = {}, 0
    for name, w in cols:
        out[name] = ap[:, at:at + w]
        at += w
    return out


class Steps:

    def __init__(self, sem, names):
        self.sem, self.names = sem, names.split()
        self.count = len(self.names)

    def before(self, it, shift=0):
        return it * self.count + (shift * self.count + 1)

    def after(self, it, name, shift=0):
        return it * self.count + (shift * self.count + self.names.index(name) + 2)


TOK_STEPS = ("embed addpos coord coordb sq2 proj man mul add mean center square var sqrt recip norm affine "
             "out store")
GRU_STEPS = ("mean center square var sqrt recip norm pre prebias preh hbias relu abs exp ln soft diff gates "
             "gh ready")
FIN_STEPS = ("mean center square var sqrt recip norm route bias route2 bias2 max1 max2 shift exp sum1 sum2 "
             "recw weight")
ENC_STEPS = "w1 relu w2 bias square var sqrt recip norm affine"
IN_STEPS = "copy q qevac k kevac v vfirst vlast"
OUT_STEPS = "out store"
MASK_STEPS = "maskv maskp"
PAIR_STEPS = "scores max shift exp turn turned"
SUM_STEPS = "pv recip norm"
DEC_STEPS = ("s1 srelu t1 trelu s2 sig t2 tanh gate d1 drelu d2 square var sqrt recip norm affine route "
             "mulw add")


def build(nc, patches, tokw, wembed, bcoord, bspin, rbias, consts, selw, encw, lstmw, lstmb, decw, out):
    ctx = ExitStack()
    with ctx:
        def sb(name, shape, dt=F32):
            return ctx.enter_context(nc.sbuf_tensor(name, shape, dt))

        def sem(name):
            return ctx.enter_context(nc.semaphore(name))

        memory = sb("memory", [P, 4 * N])
        hidden = sb("hidden", [P, 2 * N + 16])
        mixed = sb("mixed", [P, 2 * N])
        xn = sb("xn", [P, N])
        acc = sb("acc", [P, N])
        routed = sb("routed", [P, N])
        enc_sb = sb("enc_sb", [P, width(ENC_COLS)])
        lstm_sb = sb("lstm_sb", [P, LSTM_COLS])
        dec_sb = sb("dec_sb", [P, width(DEC_COLS)])
        const_sb = sb("const_sb", [P, width(CONST_COLS)])
        avg = sb("avg", [P, P])
        sel_sb = sb("sel_sb", [P, P])
        vbd = sb("vbd", [P, BC * 8 * 32])
        cell = sb("cell", [P, DF])
        hstep = sb("hstep", [P, DF])
        eps = sb("eps", [P, 1])
        ones_fb = sb("ones_fb", [P, 2, TP], BF16)
        bias3 = sb("bias3", [P, 4 * DF], BF16)
        rowsum = sb("rowsum", [P, 4])
        ps = ctx.enter_context(nc.psum_tensor("ps", [P, 8, 512], F32))

        const = views(const_sb, CONST_COLS)
        ident = const["ident"]
        enc = views(enc_sb, ENC_COLS)
        dec = views(dec_sb, DEC_COLS)
        tok = views(lstm_sb, TOK_COLS)
        tw = width(TOK_COLS)
        wrep = lstm_sb[:, tw:tw + E * P].rearrange("p (e m) -> p e m", e=E)
        rb_sb = lstm_sb[:, tw + 512:tw + 516]
        wembed_sb = lstm_sb[0:8, tw + 516:tw + 644]
        bcoord_sb = lstm_sb[0:8, tw + 644:tw + 645]
        bspin_sb = lstm_sb[0:4, tw + 645:tw + 646]
        ones4 = lstm_sb[0:4, tw + 648:tw + 776]
        mem4 = memory[:, :].rearrange("p (k n) -> p k n", k=4)
        hid2 = hidden[:, 0:2 * N].rearrange("p (k n) -> p k n", k=2)
        mix2 = mixed[:, :].rearrange("p (k n) -> p k n", k=2)

        def held(eng):
            eng.sem_inc(passed[eng.engine == G.engine], 1)

        def bank(b, w=CH, rows=P):
            return ps[0:rows, b, 0:w]

        def two(b):
            return ps[:, b:b + 2, 0:CH]

        def tile(ap, m, w=CH):
            return ap[:, m * w:(m + 1) * w]

        def carve(base, start, *widths):
            got, at = [], start
            for w in widths:
                got.append(base[:, at:at + w])
                at += w
            return got, at

        def cols(i, s):
            return bass.ds(i * (STREAMS * CH) + s * CH, CH)

        patches_in, tokw_in, enc_in, lstm_in, lstmb_in, dec_in, saved = (
            sem(x) for x in ("patches_in", "tokw_in", "enc_in", "lstm_in", "lstmb_in", "dec_in", "saved"))
        clear, eps_set = sem("clear"), sem("eps_set")
        passed = sem("passed_pe"), sem("passed_pool")
        G = nc.gpsimd
        tk = [Steps(sem(f"tok_step{s}"), TOK_STEPS) for s in S4]
        gr = [Steps(sem(f"gru_step{s}"), GRU_STEPS) for s in S4]
        fi = [Steps(sem(f"fin_step{s}"), FIN_STEPS) for s in S4]
        en = [Steps(sem(f"enc_step{s}"), ENC_STEPS) for s in S4]
        ai = [Steps(sem(f"attin_step{s}"), IN_STEPS) for s in (0, 1)]
        ao = [Steps(sem(f"attout_step{s}"), OUT_STEPS) for s in (0, 1)]
        pr = [Steps(sem(f"pair_step{s}"), PAIR_STEPS) for s in (0, 1)]
        mk = [Steps(sem(f"mask_step{s}"), MASK_STEPS) for s in (0, 1)]
        su = [Steps(sem(f"sum_step{s}"), SUM_STEPS) for s in (0, 1)]
        de = [Steps(sem(f"dec_step{s}"), DEC_STEPS) for s in S4]
        scan = sem("scan")
        SCAN = 4
        bias_split = sem("bias_split")
        SPLIT = 6
        bias_products = sem("bias_products")
        enc_prep = sem("enc_prep")
        dec_mean = sem("dec_mean")
        dec_prep = sem("dec_prep")
        PREP = 4
        x_turned = sem("x_turned")
        z_in = sem("z_in")
        z_lo, z_hi = sem("z_lo"), sem("z_hi")
        gates = sem("gates")
        v_cleared = sem("v_cleared")
        c_new, ig_new = sem("c_new"), sem("ig_new")
        c_tanh = sem("c_tanh")
        h_new = sem("h_new")
        h_turned = sem("h_turned")
        h_kept = sem("h_kept")
        h_saved = sem("h_saved")

        def slots(base, start, *tiles):
            return carve(base, start, *(n * CH for n in tiles))[0]

        tok_space = [slots(base, start, 1, 1, 1, 1, 1, 1, 1)
                     for base, start in ((hidden, 0), (hidden, N), (xn, 0), (dec_sb, 0))]
        gru_space = [slots(memory, s * N, 1, 1, 1, 1, 2, 2) for s in S4]
        fin_space = [slots(memory, s * N, 1, 1, 4, 2) for s in S4]
        enc_space = [slots(memory, s * N, 2, 2, 1, 2) for s in S4]
        dec_space = [slots(base, start, 1, 1, 1, 2, 2)
                     for base, start in ((hidden, 0), (hidden, N), (mixed, 0), (mixed, N))]
        (km0, km1, prob0, prob1, pt0, pt1, rec0, rec1, hc0, hc1, vodd, mx0, mx1, ot0, ot1), att_end = carve(
            memory, 0, 1568, 1568, 1024, 1024, 784, 784, 196, 196, 2 * CH + 32, 2 * CH + 32, BC * 8 * 32, 16, 16, 2 * CH, 2 * CH)
        assert att_end <= 4 * N
        (qs0, qs1, ks0, ks1), _ = carve(dec_sb, 0, 2 * CH + 16, 2 * CH + 16, 2 * CH, 2 * CH)
        masked = [v.rearrange("p (m b h t) -> p m b h t", m=2, b=2, h=8) for v in (km0, km1)]
        prob = [v.rearrange("p (h t) -> p h t", h=NH) for v in (prob0, prob1)]
        probT = [v.rearrange("p (h bt) -> p h bt", h=8) for v in (pt0, pt1)]
        rec = [rec0, rec1]
        mx = [mx0, mx1]
        vb = [v.rearrange("p (b h c) -> p b h c", b=BC, h=8) for v in (vbd[:, :], vodd)]
        hc = [v.rearrange("p (k n) -> p k n", k=2) for v in (hc0, hc1)]
        qs, ks = (qs0, qs1), (ks0, ks1)
        ot = (ot0, ot1)
        (b32, btmp), _ = carve(mixed, SPLIT_CHUNK * CH, 4 * DF, 2 * DF)
        btmp = btmp.bitcast(BF16)
        (gate, xs, hT), _ = carve(hidden, 0, 4 * DF, 4 * P, DF)
        xs4 = xs.rearrange("p (r k c) -> p r k c", r=2, k=2)
        hT2 = hT.rearrange("p (k c) -> p k c", k=2)
        wl = lstm_sb[:, :].rearrange("p (w k n) -> p w k n", w=4, k=2)

        def v_places(c, half, copy):
            for h in (0, 1):
                for o in (0, 1):
                    src = ps[64 * h:64 * h + 64, 6 + half, :].rearrange(
                        "p (b g o d) -> p b g o d", b=2, g=8, o=2)[:, :, :, o, :]
                    last = copy(vb[c][64 * o:64 * o + 64, 4 * half + h:4 * half + h + 3:2, :,
                                      DH * o:DH * (o + 1)], src)
            return last

        block = ctx.enter_context(nc.Block())

        @block.sync
        def _(sp):
            sp.dma_start(const_sb[:, :], consts).then_inc(tokw_in, 16)
            sp.dma_start(lstm_sb[:, 0:tw], tokw).then_inc(tokw_in, 16)
            sp.dma_start(wembed_sb, wembed).then_inc(tokw_in, 16)
            sp.dma_start(bcoord_sb, bcoord).then_inc(tokw_in, 16)
            sp.dma_start(bspin_sb, bspin).then_inc(tokw_in, 16)
            sp.dma_start(rb_sb, rbias.partition_broadcast(P)).then_inc(tokw_in, 16)
            sp.dma_start(mem4, patches[:, 0:4, :]).then_inc(patches_in, 16)
            sp.dma_start(mix2, patches[:, 4:6, :]).then_inc(patches_in, 16)
            with sp.Fori(0, E) as e:
                for c in (0, 1):
                    sp.wait_ge(ao[c].sem, ao[c].before(e * LOOPS))
                sp.dma_start(enc_sb[:, :], encw[e]).then_inc(enc_in, 16)
                for s in S4:
                    sp.wait_ge(fi[s].sem, fi[s].before(ITERS))
                sp.wait_ge(h_saved, e * (2 * T) + 1)
                sp.dma_start(lstm_sb[:, :], lstmw[e]).then_inc(lstm_in, 16)
                for s in S4:
                    sp.wait_ge(de[s].sem, de[s].before(e * ITERS))
                sp.dma_start(b32, lstmb[e]).then_inc(lstmb_in, 16)
                for c in (0, 1):
                    sp.wait_ge(ao[c].sem, ao[c].before((e + 1) * LOOPS))
                sp.dma_start(dec_sb[:, :], decw[e]).then_inc(dec_in, 16)
                sp.dma_start(sel_sb[:, :], selw[e]).then_inc(dec_in, 16)
            for s in S4:
                sp.wait_ge(de[s].sem, de[s].before(E * ITERS))
            sp.dma_start(out, acc[:, :]).then_inc(saved, 16)
            sp.wait_ge(saved, 16)

        @block.tensor
        def _(pe):
            def mm(o, l, r, start=True, stop=True, **kw):
                return pe.matmul(o, l, r, start=start, stop=stop, **kw)

            def average(st, it, need, s, m, x, k):
                pe.wait_ge(st[s].sem, st[s].after(it, need))
                for j in range(k):
                    last = mm(bank(2 * s + m), avg[:, :], tile(x, j), j == 0, j == k - 1)
                last.then_inc(st[s].sem, 1)

            def product(st, s, w, stride, rhs, k, ms=(0, 1)):
                for m in ms:
                    for j in range(k):
                        last = mm(bank(2 * s + m), w[:, j * stride + m * P:j * stride + (m + 1) * P], rhs(j),
                                  j == 0, j == k - 1)
                last.then_inc(st[s].sem, 1)

            pe.wait_ge(tokw_in, 96)
            pe.wait_ge(patches_in, 32)
            pe.wait_ge(clear, 5)
            with pe.Fori(0, ITERS) as i:
                for s in S4:
                    pe.wait_ge(tk[s].sem, tk[s].before(i))
                    product(tk, s, tok["wp"], P, lambda j: mem4[:, j, cols(i, s)] if j < 4 else mix2[:, j - 4, cols(i, s)],
                            KP, (0,))
                for s in S4:
                    raw = tok_space[s][3]
                    pe.wait_ge(tk[s].sem, tk[s].after(i, "addpos"))
                    mm(bank(2 * s + 1, rows=8), tok["wc"], raw)
                    mm(bank(2 * s, rows=4), tok["ws"], raw).then_inc(tk[s].sem, 1)
                for s in S4:
                    x, sq, rs, raw, co, sp_, xm = tok_space[s]
                    pe.wait_ge(tk[s].sem, tk[s].after(i, "sq2"))
                    mm(bank(2 * s), ones4, sp_[0:4, :])
                    mm(bank(2 * s + 1), wembed_sb, co[0:8, :]).then_inc(tk[s].sem, 1)
                for s in S4:
                    average(tk, i, "add", s, 0, tok_space[s][0], 1)
                for s in S4:
                    average(tk, i, "square", s, 1, tok_space[s][1], 1)
                for s in S4:
                    pe.wait_ge(tk[s].sem, tk[s].after(i, "affine"))
                    mm(bank(2 * s), tok["wo"], tok_space[s][4]).then_inc(tk[s].sem, 1)

            for s in S4:
                pe.wait_ge(tk[s].sem, tk[s].before(ITERS))
            with pe.Fori(0, ITERS) as i:
                for s in S4:
                    pe.wait_ge(gr[s].sem, gr[s].before(i))
                    mm(bank(2 * s), avg[:, :], acc[:, cols(i, s)]).then_inc(gr[s].sem, 1)
                for s in S4:
                    average(gr, i, "square", s, 1, gru_space[s][1], 1)
                for s in S4:
                    pe.wait_ge(gr[s].sem, gr[s].after(i, "norm"))
                    product(gr, s, tok["wg"], 0, lambda j: gru_space[s][0], 1)
                for s in S4:
                    pe.wait_ge(gr[s].sem, gr[s].after(i, "prebias"))
                    mm(bank(2 * s), tok["wg"][:, 2 * P:3 * P], gru_space[s][0]).then_inc(gr[s].sem, 1)

            pe.wait_ge(scan, SCAN)
            with pe.Fori(0, ITERS) as i:
                for s in S4:
                    pe.wait_ge(fi[s].sem, fi[s].before(i))
                    mm(bank(2 * s), avg[:, :], acc[:, cols(i, s)]).then_inc(fi[s].sem, 1)
                for s in S4:
                    average(fi, i, "square", s, 1, fin_space[s][3], 1)
                for need, k in (("norm", 0), ("bias", 2)):
                    for s in S4:
                        pe.wait_ge(fi[s].sem, fi[s].after(i, need))
                        mm(bank(2 * s), wrep[:, k, :], xn[:, cols(i, s)])
                        mm(bank(2 * s + 1), wrep[:, k + 1, :], xn[:, cols(i, s)]).then_inc(fi[s].sem, 1)
            for s in S4:
                pe.wait_ge(fi[s].sem, fi[s].before(ITERS))

            with pe.Fori(0, E) as e:
                pe.wait_ge(enc_in, e * 16 + 16)
                for s in S4:
                    pe.wait_ge(de[s].sem, de[s].before(e * ITERS))
                held(pe)
                for k in (0, 1):
                    mm(ps[:, 7, 0:1], avg[:, :], enc["b2"][:, k:k + 1], k == 0, k == 1)
                for m in (0, 1):
                    for k in (0, 1):
                        last = mm(ps[:, 7, 2 + m:3 + m], enc["aow"][:, k * DF + m * P:k * DF + (m + 1) * P],
                                  enc["bv"][:, k:k + 1], k == 0, k == 1)
                last.then_inc(bias_products, 1)
                with pe.Fori(0, ITERS) as i:
                    it = e * ITERS + i
                    for s in S4:
                        pe.wait_ge(en[s].sem, en[s].before(it))
                        if s == 3:
                            pe.wait_ge(enc_prep, e * PREP + PREP)
                        product(en, s, enc["w1"], 0, lambda j: xn[:, cols(i, s)], 1)
                    for s in S4:
                        pe.wait_ge(en[s].sem, en[s].after(it, "relu"))
                        product(en, s, enc["w2"], DF, lambda j: tile(enc_space[s][3], j), 2)
                    for s in S4:
                        average(en, it, "square", s, 1, enc_space[s][1], 2)

                def project(c, w0, st):
                    for m in (0, 1):
                        for k in (0, 1):
                            at = k * 3 * DF + w0 + m * P
                            last = mm(bank(6 + m), enc["aiw"][:, at:at + P], hc[c][:, k, 0:CH], k == 0, k == 1)
                    last.then_inc(st.sem, 1)

                def project_q(c, it, shift):
                    pe.wait_ge(ai[c].sem, ai[c].after(it, "copy", shift))
                    project(c, 0, ai[c])

                def project_k(c, it, shift):
                    pe.wait_ge(ai[c].sem, ai[c].after(it, "qevac", shift))
                    project(c, DF, ai[c])

                def project_v(c, it, shift):
                    pe.wait_ge(ai[c].sem, ai[c].after(it, "kevac", shift))
                    for p in range(4):
                        for k in (0, 1):
                            for h in (0, 1):
                                b0 = (2 * p + h) * T
                                last = mm(ps[64 * h:64 * h + 64, 6 + p // 2, (p % 2) * DF:(p % 2 + 1) * DF],
                                          hc[c][:, k, b0:b0 + TP],
                                          enc["aiw"][:, k * 3 * DF + 2 * DF:(k + 1) * 3 * DF], k == 0, k == 1)
                    last.then_inc(ai[c].sem, 1)

                def project_out(c, pit, pshift):
                    for q in (0, 1):
                        pe.wait_ge(su[q].sem, su[q].after(pit, "norm", pshift))
                    for m in (0, 1):
                        for k in (0, 1):
                            last = mm(bank(6 + m), enc["aow"][:, k * DF + m * P:k * DF + (m + 1) * P],
                                      tile(ot[c], k), k == 0, k == 1)
                    last.then_inc(ao[c].sem, 1)

                def scores(u, pit, shift):
                    c, p, st, b = u // 4 % 2, u % 4, pr[u % 2], 3 * (u % 2)
                    pe.wait_ge(mk[u % 2].sem, mk[u % 2].after(pit, "maskp", shift))
                    pe.wait_ge(st.sem, st.before(pit, shift))
                    for m in (0, 1):
                        for h in (0, 1):
                            b0 = m * CH + (2 * p + h) * T
                            last = mm(ps[64 * h:64 * h + 64, b + m, 0:CH], qs[c][:, b0:b0 + TP],
                                      masked[u % 2][:, m, h, :, :].rearrange("p h t -> p (h t)"))
                    last.then_inc(st.sem, 1)

                def turn_probs(u, pit, shift):
                    st, b = pr[u % 2], 3 * (u % 2)
                    pe.wait_ge(st.sem, st.after(pit, "exp", shift))
                    for hp in range(8):
                        at = (hp % 4) * P
                        last = pe.transpose(ps[:, b + hp // 4, at:at + P],
                                            prob[u % 2][:, 2 * hp:2 * hp + 2, :].rearrange("p h t -> p (h t)"), ident)
                    last.then_inc(st.sem, 1)

                def weigh(u, pit, shift):
                    c, p, st, b = u // 4 % 2, u % 4, su[u % 2], 3 * (u % 2) + 2
                    pe.wait_ge(pr[u % 2].sem, pr[u % 2].after(pit, "turned", shift))
                    pe.wait_ge(st.sem, st.before(pit, shift))
                    for m in (0, 1):
                        for h in (0, 1):
                            for q in range(4):
                                at = m * 2 * T + h * T
                                mm(ps[32 * q:32 * q + 32, b, at:at + T], vb[c][:, 2 * p + h, 4 * m + q, :],
                                   probT[u % 2][:, 4 * m + q, h * T:(h + 1) * T])
                    for q in range(4):
                        last = mm(ps[32 * q:32 * q + 32, b, 4 * T:8 * T], const["onesbd"], probT[u % 2][:, q::4, :])
                    last.then_inc(st.sem, 1)

                def slot(i, u, first, final):
                    c, p = u // 4, u % 4
                    cit, pit = e * LOOPS + i, e * (2 * SLOTS) + i * (SLOTS // 2)
                    scores(u, pit, u // 2)
                    nxt = (1 - c, cit, c)
                    has_next = not (final and c == 1)
                    if p == 0 and not (first and u == 0):
                        weigh((u - 1) % SLOTS, pit, (u - 1) // 2)
                    if p == 0 and has_next:
                        pe.wait_ge(ai[c].sem, ai[c].after(cit, "vlast"))
                        project_q(*nxt)
                    if p == 1 and not (first and c == 0):
                        if has_next:
                            pe.wait_ge(ai[1 - c].sem, ai[1 - c].after(cit, "qevac", c))
                        project_out(1 - c, pit, u // 2 - 1)
                    if p == 2 and has_next:
                        if not (first and c == 0):
                            pe.wait_ge(ao[1 - c].sem, ao[1 - c].after(cit, "store", c - 1))
                        project_k(*nxt)
                    if p == 3 and has_next:
                        project_v(*nxt)
                    if u == 1:
                        pe.wait_ge(ai[0].sem, ai[0].after(cit, "vlast"))
                    if u == 5:
                        pe.wait_ge(ai[1].sem, ai[1].after(cit, "vlast"))
                    if p != 0:
                        weigh(u - 1, pit, (u - 1) // 2)
                    turn_probs(u, pit, u // 2)

                for s in S4:
                    pe.wait_ge(en[s].sem, en[s].before(e * ITERS, ITERS))
                project_q(0, e * LOOPS, 0)
                project_k(0, e * LOOPS, 0)
                project_v(0, e * LOOPS, 0)
                for u in range(SLOTS):
                    slot(0, u, True, False)
                with pe.Fori(1, LOOPS - 1) as i:
                    for u in range(SLOTS):
                        slot(i, u, False, False)
                for u in range(SLOTS):
                    slot(LOOPS - 1, u, False, True)
                weigh(SLOTS - 1, e * (2 * SLOTS), 2 * SLOTS - 1)
                pe.wait_ge(ao[0].sem, ao[0].after(e * LOOPS, "store", LOOPS - 1))
                project_out(1, e * (2 * SLOTS), 2 * SLOTS - 1)

                pe.wait_ge(lstm_in, e * 16 + 16)
                pe.wait_ge(bias_split, e * SPLIT + SPLIT)

                def input_part(t, par, between=None):
                    pe.wait_ge(x_turned, e * T + t + 1)
                    for half in (0, 1):
                        for d in (0, 1):
                            mm(ps[64 * d:64 * d + 64, 2 * par + half, :], ones_fb[:, d, :],
                               bias3[:, half * 512:half * 512 + 512],
                               True, False, skip_group_check=True)
                        for k in (0, 1):
                            for d in (0, 1):
                                last = mm(ps[64 * d:64 * d + 64, 2 * par + half, :], xs4[:, par, k, 64 * d:64 * d + 64],
                                          wl[:, 2 * d, k, half * 512:half * 512 + 512], False, False,
                                          skip_group_check=True)
                            if half == 1 and k == 0 and between:
                                between()
                    last.then_inc(z_in, 1)

                def step(t, par, last_step=False):
                    pe.wait_ge(h_kept, e * (T + 1) + t + 1)
                    for half in (0, 1):
                        for k in (0, 1):
                            for d in (0, 1):
                                last = mm(ps[64 * d:64 * d + 64, 2 * par + half, :], hT2[:, k, 64 * d:64 * d + 64],
                                          wl[:, 2 * d + 1, k, half * 512:half * 512 + 512], False, k == 1,
                                          skip_group_check=True)
                        last.then_inc(z_lo if half == 0 else z_hi, 1)

                    def turn_h():
                        pe.wait_ge(h_new, e * T + t + 1)
                        for k in (0, 1):
                            turned = pe.transpose(ps[:, 4, k * P:(k + 1) * P], hstep[:, k * P:(k + 1) * P], ident)
                        turned.then_inc(h_turned, 1)

                    if last_step:
                        turn_h()
                    else:
                        input_part(t + 1, 1 - par, turn_h)

                input_part(0, 0)
                with pe.Fori(0, T // 2) as i:
                    step(i * 2, 0)
                    step(i * 2 + 1, 1)
                step(T - 1, 0, last_step=True)

                pe.wait_ge(dec_in, e * 32 + 32)
                pe.wait_ge(h_saved, e * (2 * T) + 2 * T + 1)
                held(pe)
                mm(ps[:, 7, 0:1], avg[:, :], dec["db2"]).then_inc(dec_mean, 1)
                with pe.Fori(0, ITERS) as i:
                    it = e * ITERS + i
                    for s in S4:
                        pe.wait_ge(de[s].sem, de[s].before(it))
                        if s == 3:
                            pe.wait_ge(dec_prep, e * PREP + PREP)
                        product(de, s, dec["sw1"], DF, lambda j: mem4[:, j, cols(i, s)], 4)
                    for s in S4:
                        pe.wait_ge(de[s].sem, de[s].after(it, "srelu"))
                        product(de, s, dec["tw1"], DF, lambda j: mem4[:, j, cols(i, s)], 4)
                    for need, w, src in (("trelu", "sw2", 3), ("sig", "tw2", 4), ("gate", "dw1", 3)):
                        for s in S4:
                            pe.wait_ge(de[s].sem, de[s].after(it, need))
                            product(de, s, dec[w], DF, lambda j: tile(dec_space[s][src], j), 2)
                    for s in S4:
                        pe.wait_ge(de[s].sem, de[s].after(it, "drelu"))
                        product(de, s, dec["dw2"], P, lambda j: tile(dec_space[s][4], j), 2, (0,))
                    for s in S4:
                        average(de, it, "square", s, 1, dec_space[s][1], 1)
                    for s in S4:
                        pe.wait_ge(de[s].sem, de[s].after(it, "affine"))
                        mm(bank(2 * s + 1), sel_sb[:, :], routed[:, cols(i, s)]).then_inc(de[s].sem, 1)

        @block.vector
        def _(dve):
            V = nc.vector

            def ts(o, i, a, b, op0, op1=None):
                return V.tensor_scalar(o, i, a, b, op0, op1) if op1 else V.tensor_scalar(o, i, a, None, op0)

            def center(st, it, s, x, src, need="mean", b=0):
                dve.wait_ge(st[s].sem, st[s].after(it, need))
                V.tensor_tensor(x, src, bank(2 * s + b), ALU.subtract).then_inc(st[s].sem, 1)

            def recip(st, it, s, rs):
                dve.wait_ge(st[s].sem, st[s].after(it, "sqrt"))
                V.reciprocal(rs, rs).then_inc(st[s].sem, 1)

            def norm(st, it, s, x, rs, k, o=None):
                dve.wait_ge(st[s].sem, st[s].after(it, "recip"))
                x3 = x.rearrange("p (k n) -> p k n", k=k)
                V.tensor_tensor(x3 if o is None else o, x3, rs.unsqueeze(1).broadcast_to([P, k, CH]),
                                ALU.mult).then_inc(st[s].sem, 1)

            def centre(prep, e, w, wide):
                w3 = w.rearrange("p (k n) -> p k n", k=2)
                n = e * PREP
                V.tensor_reduce(rowsum[:, 0:2], w3, AX.X, ALU.add).then_inc(prep, 1)
                dve.wait_ge(prep, n + 1)
                ts(rowsum[:, 2:4], rowsum[:, 0:2], 1.0 / wide, None, ALU.mult).then_inc(prep, 1)
                dve.wait_ge(prep, n + 2)
                V.tensor_tensor(w3, w3, rowsum[:, 2:4].unsqueeze(2).broadcast_to([P, 2, wide]),
                                ALU.subtract).then_inc(prep, 1)

            V.memset(avg[:, :], 1.0 / P)
            V.memset(hidden[:, 2 * N:2 * N + 16], 0.0)
            V.memset(vbd[:, :], 0.0)
            V.memset(routed[:, :], 0.0)
            V.memset(ones_fb[:, :, :], 0.0).then_inc(clear, 1)
            dve.wait_ge(clear, 1)
            for r in (0, 32, 64):
                V.memset(ones_fb[r:r + 2, 1, :], 1.0)
                V.memset(ones_fb[r:r + 1, 0, :], 1.0).then_inc(clear, 1)
            dve.wait_ge(clear, 4)
            for r in (0, 32, 64):
                V.memset(ones_fb[r:r + 1, 1, :], 0.0)
            started = [st.sem for st in tk + gr + fi + en + ai + ao + pr + mk + su + de] + [h_saved]
            for c, first in enumerate(started):
                V.memset(cell[:, c:c + 1], 0.0).then_inc(first, 1)
            dve.wait_ge(tokw_in, 96)
            V.memset(ones4, 1.0)
            V.tensor_copy(wrep, tok["wr"].unsqueeze(2).broadcast_to([P, E, P]))
            ts(tok["pos"], tok["pos"], tok["bp"], None, ALU.add).then_inc(clear, 1)

            dve.wait_ge(clear, 5)
            with dve.Fori(0, ITERS) as i:
                for s in S4:
                    raw = tok_space[s][3]
                    dve.wait_ge(tk[s].sem, tk[s].after(i, "embed"))
                    V.tensor_tensor(raw.rearrange("p (b t) -> p b t", t=T),
                                    bank(2 * s).rearrange("p (b t) -> p b t", t=T),
                                    tok["pos"].unsqueeze(1).broadcast_to([P, BC, T]), ALU.add).then_inc(tk[s].sem, 1)
                for s in S4:
                    x, sq, rs, raw, co, sp_, xm = tok_space[s]
                    dve.wait_ge(tk[s].sem, tk[s].after(i, "man"))
                    V.tensor_tensor(xm, xm, bank(2 * s), ALU.mult).then_inc(tk[s].sem, 1)
                for s in S4:
                    x, sq, rs, raw, co, sp_, xm = tok_space[s]
                    dve.wait_ge(tk[s].sem, tk[s].after(i, "mul"))
                    V.tensor_tensor(x, xm, raw, ALU.add).then_inc(tk[s].sem, 1)
                for s in S4:
                    center(tk, i, s, tok_space[s][0], tok_space[s][0])
                for s in S4:
                    recip(tk, i, s, tok_space[s][2])
                for s in S4:
                    norm(tk, i, s, tok_space[s][0], tok_space[s][2], 1)

            with dve.Fori(0, ITERS) as i:
                for s in S4:
                    center(gr, i, s, gru_space[s][0], acc[:, cols(i, s)])
                for s in S4:
                    recip(gr, i, s, gru_space[s][2])
                for s in S4:
                    norm(gr, i, s, gru_space[s][0], gru_space[s][2], 1)
                for s in S4:
                    x, sq, rs, ph, pf, re = gru_space[s]
                    dve.wait_ge(gr[s].sem, gr[s].after(i, "ln"))
                    V.tensor_tensor(re, re, pf, ALU.add).then_inc(gr[s].sem, 1)
                for s in S4:
                    x, sq, rs, ph, pf, re = gru_space[s]
                    dve.wait_ge(gr[s].sem, gr[s].after(i, "soft"))
                    V.tensor_tensor(rs, tile(re, 0), tile(re, 1), ALU.subtract)
                    ts(tile(pf, 0), ph, 0.0, None, ALU.min).then_inc(gr[s].sem, 1)
                for s in S4:
                    x, sq, rs, ph, pf, re = gru_space[s]
                    dve.wait_ge(gr[s].sem, gr[s].after(i, "gates"))
                    V.scalar_tensor_tensor(out=x, in0=ph, scalar=0.0, in1=x, op0=ALU.max,
                                           op1=ALU.add).then_inc(gr[s].sem, 1)
                for s in S4:
                    x, sq, rs, ph, pf, re = gru_space[s]
                    dve.wait_ge(gr[s].sem, gr[s].after(i, "gh"))
                    V.tensor_tensor(mixed[:, bass.ds(i * (STREAMS * CH) + (s * CH + N), CH)], x, sq,
                                    ALU.mult).then_inc(gr[s].sem, 1)
            for s in S4:
                dve.wait_ge(gr[s].sem, gr[s].before(ITERS))
            f0 = mixed[:, 0:N].rearrange("p (b t) -> p b t", t=T)[:, :, 0]
            g0 = mixed[:, N:2 * N].rearrange("p (b t) -> p b t", t=T)[:, :, 0]
            V.scalar_tensor_tensor(out=g0, in0=f0, scalar=H_INIT, in1=g0, op0=ALU.mult, op1=ALU.add).then_inc(scan, 1)
            dve.wait_ge(scan, 1)
            V.memset(f0, 0.0).then_inc(scan, 1)
            dve.wait_ge(scan, 2)
            V.tensor_tensor_scan(memory[:, 0:N], mixed[:, 0:N], mixed[:, N:2 * N], 0.0, ALU.mult,
                                 ALU.add).then_inc(scan, 1)
            dve.wait_ge(scan, 3)
            V.tensor_tensor(acc[:, :], acc[:, :], memory[:, 0:N], ALU.add).then_inc(scan, 1)

            with dve.Fori(0, ITERS) as i:
                for s in S4:
                    center(fi, i, s, fin_space[s][0], acc[:, cols(i, s)])
                for s in S4:
                    recip(fi, i, s, fin_space[s][1])
                for s in S4:
                    norm(fi, i, s, fin_space[s][0], fin_space[s][1], 1, xn[:, cols(i, s)].unsqueeze(1))
                for s in S4:
                    x, rs, lo, m1 = fin_space[s]
                    dve.wait_ge(fi[s].sem, fi[s].after(i, "bias2"))
                    V.tensor_tensor(m1, lo[:, 0:2 * CH], lo[:, 2 * CH:], ALU.max).then_inc(fi[s].sem, 1)
                for s in S4:
                    x, rs, lo, m1 = fin_space[s]
                    dve.wait_ge(fi[s].sem, fi[s].after(i, "max1"))
                    V.tensor_tensor(rs, tile(m1, 0), tile(m1, 1), ALU.max).then_inc(fi[s].sem, 1)
                for s in S4:
                    x, rs, lo, m1 = fin_space[s]
                    lo4 = lo.rearrange("p (e n) -> p e n", e=E)
                    dve.wait_ge(fi[s].sem, fi[s].after(i, "max2"))
                    V.tensor_tensor(lo4, lo4, rs.unsqueeze(1).broadcast_to([P, E, CH]),
                                    ALU.subtract).then_inc(fi[s].sem, 1)
                for s in S4:
                    x, rs, lo, m1 = fin_space[s]
                    dve.wait_ge(fi[s].sem, fi[s].after(i, "exp"))
                    V.tensor_tensor(m1, lo[:, 0:2 * CH], lo[:, 2 * CH:], ALU.add).then_inc(fi[s].sem, 1)
                for s in S4:
                    x, rs, lo, m1 = fin_space[s]
                    dve.wait_ge(fi[s].sem, fi[s].after(i, "sum1"))
                    V.tensor_tensor(rs, tile(m1, 0), tile(m1, 1), ALU.add).then_inc(fi[s].sem, 1)
                for s in S4:
                    x, rs, lo, m1 = fin_space[s]
                    dve.wait_ge(fi[s].sem, fi[s].after(i, "sum2"))
                    V.reciprocal(x, rs).then_inc(fi[s].sem, 1)
                for s in S4:
                    x, rs, lo, m1 = fin_space[s]
                    dve.wait_ge(fi[s].sem, fi[s].after(i, "recw"))
                    for k in range(E):
                        r = 32 * k
                        last = V.tensor_tensor(routed[r:r + 1, cols(i, s)], lo[r:r + 1, k * CH:(k + 1) * CH],
                                               x[r:r + 1, :], ALU.mult)
                    last.then_inc(fi[s].sem, 1)

            with dve.Fori(0, E) as e:
                dve.wait_ge(enc_in, e * 16 + 16)
                centre(enc_prep, e, enc["w2"], DF)
                dve.wait_ge(bias_products, e + 1)
                V.scalar_tensor_tensor(out=enc["b2"], in0=ps[:, 7, 0:1].broadcast_to([P, 2]), scalar=-0.5,
                                       in1=enc["b2"], op0=ALU.mult, op1=ALU.add)
                V.tensor_tensor(enc["bo"], enc["bo"], ps[:, 7, 2:4], ALU.add).then_inc(enc_prep, 1)
                with dve.Fori(0, ITERS) as i:
                    it = e * ITERS + i
                    for s in S4:
                        dve.wait_ge(en[s].sem, en[s].after(it, "w2"))
                        for m in (0, 1):
                            last = ts(tile(enc_space[s][0], m), bank(2 * s + m), enc["b2"][:, m:m + 1], None,
                                      ALU.add)
                        last.then_inc(en[s].sem, 1)
                    for s in S4:
                        recip(en, it, s, enc_space[s][2])
                    for s in S4:
                        norm(en, it, s, enc_space[s][0], enc_space[s][2], 2)

                for s in S4:
                    dve.wait_ge(en[s].sem, en[s].before(e * ITERS, ITERS))

                def q_evac(c, it, shift):
                    dve.wait_ge(ai[c].sem, ai[c].after(it, "q", shift))
                    for m in (0, 1):
                        last = ts(tile(qs[c], m), bank(6 + m), enc["bq"][:, m:m + 1], DH ** -0.5, ALU.add, ALU.mult)
                    last.then_inc(ai[c].sem, 1)

                def v_evac(c, it, shift):
                    dve.wait_ge(ai[c].sem, ai[c].after(it, "v", shift))
                    v_places(c, 0, V.tensor_copy).then_inc(ai[c].sem, 1)

                def mask(u, cit, cshift, pit, shift):
                    c, p = u // 4 % 2, u % 4
                    if shift is not None:
                        dve.wait_ge(pr[u % 2].sem, pr[u % 2].after(pit, "scores", shift - 1))
                    if p == 0:
                        dve.wait_ge(ai[c].sem, ai[c].after(cit, "kevac", cshift))
                    kk = ks[c][:, 2 * p * T:2 * (p + 1) * T].rearrange("p (b t) -> p b t", b=2)
                    V.tensor_tensor(masked[u % 2][:, 0, :, :, :], kk.unsqueeze(2).broadcast_to([P, 2, 8, T]),
                                    const["mask"].unsqueeze(1).unsqueeze(3).broadcast_to([P, 2, 8, T]),
                                    ALU.mult).then_inc(mk[u % 2].sem, 1)

                def finish_pair(u, pit, shift):
                    c, p, st, b = u // 4 % 2, u % 4, su[u % 2], 3 * (u % 2) + 2
                    dve.wait_ge(st.sem, st.after(pit, "pv", shift))
                    V.reciprocal(rec[u % 2], ps[:, b, 4 * T:8 * T]).then_inc(st.sem, 1)
                    dve.wait_ge(st.sem, st.after(pit, "recip", shift))
                    o = ot[c].rearrange("p (m n) -> p m n", m=2)[:, :, 2 * p * T:2 * (p + 1) * T]
                    V.tensor_tensor(o, ps[:, b, 0:4 * T].rearrange("p (m n) -> p m n", m=2),
                                    rec[u % 2].rearrange("p (m n) -> p m n", m=2), ALU.mult).then_inc(st.sem, 1)

                def split_bias(step):
                    if step == 0:
                        dve.wait_ge(lstmb_in, e * 16 + 16)
                    else:
                        dve.wait_ge(bias_split, e * SPLIT + step)
                    if step % 2 == 0:
                        V.tensor_copy(btmp, b32).then_inc(bias_split, 1)
                    else:
                        r = 16 * (step - 1)
                        V.tensor_copy(bias3[r:r + 32, :], btmp[r:r + 32, :])
                        if step == 1:
                            V.tensor_copy(bias3[96:128, :], btmp[96:128, :])
                        if step < SPLIT - 1:
                            V.tensor_tensor(b32, b32, btmp, ALU.subtract).then_inc(bias_split, 1)
                        else:
                            V.memset(cell[:, :], 0.0).then_inc(bias_split, 1)

                def slot(i, u, first, final):
                    c, p, st, b = u // 4, u % 4, pr[u % 2], 3 * (u % 2)
                    cit, pit = e * LOOPS + i, e * (2 * SLOTS) + i * (SLOTS // 2)
                    has_next = not (final and c == 1)
                    sc = two(b).rearrange("p m (h t) -> p m h t", t=T)
                    mx3 = mx[u % 2].rearrange("p (m h) -> p m h", m=2)
                    if not (final and u == SLOTS - 1):
                        mask((u + 1) % SLOTS, cit, (u + 1) // SLOTS, pit, None if first and u == 0 else (u + 1) // 2)
                    dve.wait_ge(st.sem, st.after(pit, "scores", u // 2))
                    V.tensor_reduce(mx3, sc, AX.X, ALU.max).then_inc(st.sem, 1)
                    dve.wait_ge(st.sem, st.after(pit, "max", u // 2))
                    V.tensor_tensor(prob[u % 2][:, :, 0:T].rearrange("p (m h) t -> p m h t", m=2), sc,
                                    mx3.unsqueeze(3).broadcast_to([P, 2, 8, T]), ALU.subtract).then_inc(st.sem, 1)
                    if p == 0 and has_next:
                        q_evac(1 - c, cit, c)
                    if p == 3 and has_next:
                        v_evac(1 - c, cit, c)
                    if not (first and u == 0):
                        finish_pair((u - 1) % SLOTS, pit, (u - 1) // 2)
                    if first and 1 <= u <= SPLIT:
                        split_bias(u - 1)

                for c in (0, 1):
                    V.memset(prob[c][:, :, T:TP], 0.0)
                    V.memset(qs[c][:, 2 * CH:2 * CH + 16], 0.0)
                q_evac(0, e * LOOPS, 0)
                mask(0, e * LOOPS, 0, None, None)
                dve.wait_ge(v_cleared, e + 1)
                v_evac(0, e * LOOPS, 0)
                for u in range(SLOTS):
                    slot(0, u, True, False)
                with dve.Fori(1, LOOPS - 1) as i:
                    for u in range(SLOTS):
                        slot(i, u, False, False)
                for u in range(SLOTS):
                    slot(LOOPS - 1, u, False, True)
                finish_pair(SLOTS - 1, e * (2 * SLOTS), 2 * SLOTS - 1)

                for c in (0, 1):
                    dve.wait_ge(ai[c].sem, ai[c].before((e + 1) * LOOPS))
                V.memset(hT, 0.0).then_inc(h_kept, 1)
                with dve.Fori(0, T) as t:
                    k = e * T + t
                    dve.wait_ge(gates, k * 3 + 1)
                    V.tensor_tensor(cell[:, :], cell[:, :], gate[:, DF:2 * DF], ALU.mult).then_inc(c_new, 1)
                    dve.wait_ge(gates, k * 3 + 2)
                    V.tensor_tensor(gate[:, 0:DF], gate[:, 0:DF], gate[:, 2 * DF:3 * DF], ALU.mult).then_inc(ig_new, 1)
                    dve.wait_ge(c_new, k * 2 + 1)
                    dve.wait_ge(ig_new, k + 1)
                    V.tensor_tensor(cell[:, :], cell[:, :], gate[:, 0:DF], ALU.add).then_inc(c_new, 1)
                    dve.wait_ge(c_tanh, k + 1)
                    dve.wait_ge(gates, k * 3 + 3)
                    V.tensor_tensor(hstep[:, :], gate[:, 3 * DF:], hstep[:, :], ALU.mult).then_inc(h_new, 1)
                    dve.wait_ge(h_turned, k + 1)
                    dve.wait_ge(h_saved, k * 2 + 1)
                    V.tensor_copy(hT, ps[:, 4, 0:DF]).then_inc(h_kept, 1)

                dve.wait_ge(dec_in, e * 32 + 32)
                centre(dec_prep, e, dec["dw2"], P)
                dve.wait_ge(dec_mean, e + 1)
                V.tensor_tensor(dec["db2"], dec["db2"], ps[:, 7, 0:1], ALU.subtract).then_inc(dec_prep, 1)
                with dve.Fori(0, ITERS) as i:
                    it = e * ITERS + i
                    for s in S4:
                        x, sq, rs, a, b = dec_space[s]
                        dve.wait_ge(de[s].sem, de[s].after(it, "tanh"))
                        V.tensor_tensor(a, a, b, ALU.mult).then_inc(de[s].sem, 1)
                    for s in S4:
                        recip(de, it, s, dec_space[s][2])
                    for s in S4:
                        dve.wait_ge(de[s].sem, de[s].after(it, "recip"))
                        V.scalar_tensor_tensor(out=dec_space[s][0], in0=bank(2 * s), scalar=dec["db2"],
                                               in1=dec_space[s][2], op0=ALU.add, op1=ALU.mult).then_inc(de[s].sem, 1)
                    for s in S4:
                        y = dec_space[s][1]
                        dve.wait_ge(de[s].sem, de[s].after(it, "route"))
                        V.tensor_tensor(y, y, bank(2 * s + 1), ALU.mult).then_inc(de[s].sem, 1)
                    for s in S4:
                        y = dec_space[s][1]
                        dve.wait_ge(de[s].sem, de[s].after(it, "mulw"))
                        V.tensor_tensor(acc[:, cols(i, s)], acc[:, cols(i, s)], y, ALU.add).then_inc(de[s].sem, 1)

        @block.scalar
        def _(act):
            A = nc.scalar.activation
            ID = ACT.Identity

            def square(st, it, s, sq, x):
                act.wait_ge(st[s].sem, st[s].after(it, "center"))
                A(sq, x, ACT.Square).then_inc(st[s].sem, 1)

            def deviation(st, it, s, rs, m, scale=1.0):
                act.wait_ge(st[s].sem, st[s].after(it, "var"))
                A(rs, bank(2 * s + m), ACT.Sqrt, bias=eps[:, 0:1], scale=scale).then_inc(st[s].sem, 1)

            def evac(st, it, s, need, o, bias, func=ID):
                act.wait_ge(st[s].sem, st[s].after(it, need))
                for m in (0, 1):
                    last = A(tile(o, m), bank(2 * s + m), func, bias=bias[:, m:m + 1])
                last.then_inc(st[s].sem, 1)

            act.wait_ge(eps_set, 1)
            with act.Fori(0, ITERS) as i:
                for s in S4:
                    co, sp_ = tok_space[s][4:6]
                    act.wait_ge(tk[s].sem, tk[s].after(i, "coord"))
                    A(co[0:8, :], bank(2 * s + 1, rows=8), ID, bias=bcoord_sb).then_inc(tk[s].sem, 1)
                    A(sp_[0:4, :], bank(2 * s, rows=4), ACT.Square, bias=bspin_sb).then_inc(tk[s].sem, 1)
                for s in S4:
                    act.wait_ge(tk[s].sem, tk[s].after(i, "proj"))
                    A(tok_space[s][6], bank(2 * s + 1), ID, bias=tok["be"]).then_inc(tk[s].sem, 1)
                for s in S4:
                    square(tk, i, s, tok_space[s][1], tok_space[s][0])
                for s in S4:
                    deviation(tk, i, s, tok_space[s][2], 1)
                for s in S4:
                    act.wait_ge(tk[s].sem, tk[s].after(i, "norm"))
                    A(tok_space[s][4], tok_space[s][0], ID, bias=tok["beta"], scale=tok["g"]).then_inc(tk[s].sem, 1)
                for s in S4:
                    act.wait_ge(tk[s].sem, tk[s].after(i, "out"))
                    A(acc[:, cols(i, s)], bank(2 * s), ID, bias=tok["bo"]).then_inc(tk[s].sem, 1)

            with act.Fori(0, ITERS) as i:
                for s in S4:
                    square(gr, i, s, gru_space[s][1], gru_space[s][0])
                for s in S4:
                    deviation(gr, i, s, gru_space[s][2], 1)
                for s in S4:
                    evac(gr, i, s, "pre", gru_space[s][4], tok["bg"])
                for s in S4:
                    ph = gru_space[s][3]
                    act.wait_ge(gr[s].sem, gr[s].after(i, "preh"))
                    A(ph, bank(2 * s), ID, bias=tok["bg"][:, 2:3]).then_inc(gr[s].sem, 1)
                for s in S4:
                    x, sq, rs, ph, pf, re = gru_space[s]
                    act.wait_ge(gr[s].sem, gr[s].after(i, "hbias"))
                    A(re, pf, ACT.Relu, scale=-1.0).then_inc(gr[s].sem, 1)
                for s in S4:
                    pf = gru_space[s][4]
                    act.wait_ge(gr[s].sem, gr[s].after(i, "relu"))
                    A(pf, pf, ACT.Abs).then_inc(gr[s].sem, 1)
                for s in S4:
                    pf = gru_space[s][4]
                    act.wait_ge(gr[s].sem, gr[s].after(i, "abs"))
                    A(pf, pf, ACT.Exp, scale=-1.0).then_inc(gr[s].sem, 1)
                for s in S4:
                    pf = gru_space[s][4]
                    act.wait_ge(gr[s].sem, gr[s].after(i, "exp"))
                    A(pf, pf, ACT.Ln, bias=1.0).then_inc(gr[s].sem, 1)
                for s in S4:
                    x, sq, rs, ph, pf, re = gru_space[s]
                    act.wait_ge(gr[s].sem, gr[s].after(i, "diff"))
                    A(mixed[:, cols(i, s)], rs, ACT.Sigmoid, scale=-1.0)
                    A(sq, rs, ACT.Sigmoid)
                    A(x, tile(pf, 0), ACT.Sigmoid).then_inc(gr[s].sem, 1)

            with act.Fori(0, ITERS) as i:
                for s in S4:
                    square(fi, i, s, tile(fin_space[s][3], 0), fin_space[s][0])
                for s in S4:
                    deviation(fi, i, s, fin_space[s][1], 1)
                for s in S4:
                    evac(fi, i, s, "route", fin_space[s][2][:, 0:2 * CH], rb_sb)
                for s in S4:
                    evac(fi, i, s, "route2", fin_space[s][2][:, 2 * CH:], rb_sb[:, 2:4])
                for s in S4:
                    lo = fin_space[s][2]
                    act.wait_ge(fi[s].sem, fi[s].after(i, "shift"))
                    A(lo, lo, ACT.Exp).then_inc(fi[s].sem, 1)

            with act.Fori(0, E) as e:
                with act.Fori(0, ITERS) as i:
                    it = e * ITERS + i
                    for s in S4:
                        evac(en, it, s, "w1", enc_space[s][3], enc["b1"], ACT.Relu)
                    for s in S4:
                        act.wait_ge(en[s].sem, en[s].after(it, "bias"))
                        A(enc_space[s][1], enc_space[s][0], ACT.Square).then_inc(en[s].sem, 1)
                    for s in S4:
                        deviation(en, it, s, enc_space[s][2], 1, scale=0.5)
                    for s in S4:
                        act.wait_ge(en[s].sem, en[s].after(it, "norm"))
                        for m in (0, 1):
                            last = A(hid2[:, m, cols(i, s)], tile(enc_space[s][0], m), ID,
                                     bias=enc["beta"][:, m:m + 1], scale=enc["g"][:, m:m + 1])
                        last.then_inc(en[s].sem, 1)

                def k_evac(c, it, shift):
                    act.wait_ge(ai[c].sem, ai[c].after(it, "k", shift))
                    for m in (0, 1):
                        last = A(tile(ks[c], m), bank(6 + m), ID, bias=enc["bk"][:, m:m + 1])
                    last.then_inc(ai[c].sem, 1)

                def v_evac(c, it, shift):
                    act.wait_ge(ai[c].sem, ai[c].after(it, "v", shift))
                    v_places(c, 1, lambda o, i: A(o, i, ACT.Copy)).then_inc(ai[c].sem, 1)

                def store_out(c, it, shift, chunk):
                    act.wait_ge(ao[c].sem, ao[c].after(it, "out", shift))
                    for m in (0, 1):
                        last = A(mix2[:, m, bass.ds(chunk, CH)], bank(6 + m), ID, bias=enc["bo"][:, m:m + 1])
                    last.then_inc(ao[c].sem, 1)

                def slot(i, u, first, final):
                    c, p, st, b = u // 4, u % 4, pr[u % 2], 3 * (u % 2)
                    cit, pit = e * LOOPS + i, e * (2 * SLOTS) + i * (SLOTS // 2)
                    act.wait_ge(st.sem, st.after(pit, "shift", u // 2))
                    A(prob[u % 2][:, :, 0:T], prob[u % 2][:, :, 0:T], ACT.Exp).then_inc(st.sem, 1)
                    if p == 1 and not (first and c == 0):
                        store_out(1 - c, cit, c - 1, i * (2 * CH) + (c - 1) * CH)
                    if p == 2 and not (final and c == 1):
                        k_evac(1 - c, cit, c)
                    if p == 3 and not (final and c == 1):
                        v_evac(1 - c, cit, c)
                    act.wait_ge(st.sem, st.after(pit, "turn", u // 2))
                    src = ps[:, b:b + 2, :].rearrange("p m (hb t) -> p m hb t", t=TP)[:, :, :, 0:T]
                    A(probT[u % 2].rearrange("p (m h) (b t) -> p m (h b) t", m=2, b=2), src,
                      ACT.Copy).then_inc(st.sem, 1)

                k_evac(0, e * LOOPS, 0)
                act.wait_ge(v_cleared, e + 1)
                v_evac(0, e * LOOPS, 0)
                for u in range(SLOTS):
                    slot(0, u, True, False)
                with act.Fori(1, LOOPS - 1) as i:
                    for u in range(SLOTS):
                        slot(i, u, False, False)
                for u in range(SLOTS):
                    slot(LOOPS - 1, u, False, True)
                store_out(1, e * LOOPS, LOOPS - 1, (NCH - 1) * CH)
                def lstm_step(t, par):
                    k = e * T + t
                    act.wait_ge(z_lo, k + 1)
                    A(gate[:, 0:2 * DF], ps[:, 2 * par, :], ACT.Sigmoid).then_inc(gates, 1)
                    act.wait_ge(z_hi, k + 1)
                    A(gate[:, 2 * DF:3 * DF], ps[:, 2 * par + 1, 0:DF], ACT.Tanh).then_inc(gates, 1)
                    A(gate[:, 3 * DF:], ps[:, 2 * par + 1, DF:], ACT.Sigmoid).then_inc(gates, 1)
                    act.wait_ge(c_new, k * 2 + 2)
                    A(hstep[:, :], cell[:, :], ACT.Tanh).then_inc(c_tanh, 1)

                with act.Fori(0, T // 2) as i:
                    lstm_step(i * 2, 0)
                    lstm_step(i * 2 + 1, 1)
                lstm_step(T - 1, 0)

                with act.Fori(0, ITERS) as i:
                    it = e * ITERS + i
                    for need, o, w, func in (("s1", 3, "sb1", ACT.Relu), ("t1", 4, "tb1", ACT.Relu),
                                             ("s2", 3, "sb2", ACT.Sigmoid), ("t2", 4, "tb2", ACT.Tanh),
                                             ("d1", 4, "db1", ACT.Relu)):
                        for s in S4:
                            evac(de, it, s, need, dec_space[s][o], dec[w], func)
                    for s in S4:
                        act.wait_ge(de[s].sem, de[s].after(it, "d2"))
                        A(dec_space[s][1], bank(2 * s), ACT.Square, bias=dec["db2"]).then_inc(de[s].sem, 1)
                    for s in S4:
                        deviation(de, it, s, dec_space[s][2], 1)
                    for s in S4:
                        act.wait_ge(de[s].sem, de[s].after(it, "norm"))
                        A(dec_space[s][1], dec_space[s][0], ID, bias=dec["beta"],
                          scale=dec["g"]).then_inc(de[s].sem, 1)

        @block.gpsimd
        def _(pool):
            G.memset(eps[:, :], EPS).then_inc(eps_set, 1)
            with pool.Fori(0, E) as e:
                def copy_chunk(c, it, shift, chunk):
                    pool.wait_ge(ai[c].sem, ai[c].before(it, shift))
                    held(pool)
                    for k in (0, 1):
                        last = G.tensor_copy(hc[c][:, k, :], hidden[:, bass.ds(chunk + k * N, CH + 16)])
                    last.then_inc(ai[c].sem, 1)

                def mask(u, pit, shift):
                    c, p, st = u // 4 % 2, u % 4, mk[u % 2]
                    pool.wait_ge(st.sem, st.after(pit, "maskv", shift))
                    kk = ks[c][:, CH + 2 * p * T:CH + 2 * (p + 1) * T].rearrange("p (b t) -> p b t", b=2)
                    G.tensor_tensor(masked[u % 2][:, 1, :, :, :], kk.unsqueeze(2).broadcast_to([P, 2, 8, T]),
                                    const["mask"].unsqueeze(1).unsqueeze(3).broadcast_to([P, 2, 8, T]),
                                    ALU.mult).then_inc(st.sem, 1)

                def slot(i, u, final):
                    c, p = u // 4, u % 4
                    cit, pit = e * LOOPS + i, e * (2 * SLOTS) + i * (SLOTS // 2)
                    if p == 2 and not final:
                        copy_chunk(c, cit, 1, i * (2 * CH) + (c + 2) * CH)
                    if not (final and u == SLOTS - 1):
                        mask((u + 1) % SLOTS, pit, (u + 1) // 2)

                for s in S4:
                    pool.wait_ge(en[s].sem, en[s].before(e * ITERS, ITERS))
                held(pool)
                copy_chunk(0, e * LOOPS, 0, 0)
                copy_chunk(1, e * LOOPS, 0, CH)
                G.memset(vodd, 0.0).then_inc(v_cleared, 1)
                mask(0, e * (2 * SLOTS), 0)
                with pool.Fori(0, LOOPS - 1) as i:
                    for u in range(SLOTS):
                        slot(i, u, False)
                for u in range(SLOTS):
                    slot(LOOPS - 1, u, True)
                for c in (0, 1):
                    pool.wait_ge(ao[c].sem, ao[c].before(e * LOOPS, LOOPS))
                held(pool)

                def save(t):
                    k = e * T + t
                    pool.wait_ge(h_kept, e * (T + 1) + t + 2)
                    held(pool)
                    G.tensor_copy(mem4[:, 0:2, bass.ds(t, NB, step=T)], hT2[:, :, 0:64]).then_inc(h_saved, 1)
                    G.tensor_copy(mem4[:, 2:4, bass.ds(t * -1 + (T - 1), NB, step=T)], hT2[:, :, 64:128]).then_inc(h_saved, 1)

                def turn(t, par):
                    G.tensor_copy(xs4[:, par, :, 0:64], mix2[:, :, bass.ds(t, NB, step=T)])
                    G.tensor_copy(xs4[:, par, :, 64:128],
                                  mix2[:, :, bass.ds(t * -1 + (T - 1), NB, step=T)]).then_inc(x_turned, 1)

                turn(0, 0)
                turn(1, 1)
                with pool.Fori(0, T // 2 - 1) as i:
                    for par in (0, 1):
                        save(i * 2 + par)
                        pool.wait_ge(z_in, e * T + i * 2 + (par + 1))
                        held(pool)
                        turn(i * 2 + (par + 2), par)
                save(T - 3)
                pool.wait_ge(z_in, e * T + T - 2)
                held(pool)
                turn(T - 1, 0)
                save(T - 2)
                save(T - 1)


def pack(inputs, names):
    parts = []
    for name in names:
        a = np.asarray(inputs["L0_ffn_" + name])
        if a.ndim == 2:
            a = a[:, :, None]
        e, r, w = a.shape
        parts.append(a.reshape(e, r // P, P, w).transpose(0, 2, 1, 3).reshape(e, P, -1))
    return np.ascontiguousarray(np.concatenate(parts, axis=2))


def kernel(**inputs):
    import concourse.bacc as bacc
    from concourse.bass_utils import run_bass_kernel_spmd

    t = {k[7:]: np.asarray(v) for k, v in inputs.items() if k.startswith("L0_tok_")}
    x = np.asarray(inputs["x"])
    patches = x.reshape(NB, 3, GRID, PATCH, GRID, PATCH).transpose(1, 3, 5, 0, 2, 4).reshape(KP, P, N)
    patches = patches.transpose(1, 0, 2)
    wp = t["W_patch"].reshape(KP, P, P).transpose(1, 0, 2).reshape(P, KP * P)
    wg = np.asarray(inputs["L0_attn_W"]).T
    bg = np.asarray(inputs["L0_attn_b"]).reshape(3, P).T
    tokw = np.concatenate(
        [wp, t["W_out"], wg, np.asarray(inputs["L0_ffn_router_w"]), t["W_coord"], t["W_spinor"]]
        + [t[k][:, None] for k in ("b_patch", "b_embed", "ln_gamma", "ln_beta", "b_out")]
        + [bg, t["pos_embed"][0].T], axis=1)
    f = np.float32
    consts = np.concatenate(
        [np.eye(P, dtype=f), np.kron(np.eye(8, dtype=f), np.ones((DH, 1), f)),
         np.kron(np.eye(2, dtype=f), np.ones((TP, DH), f))], axis=1)
    selw = np.zeros((E, P, P), f)
    for k in range(E):
        selw[k, 32 * k] = 1.0
    encw = pack(inputs, ["enc_w1", "enc_w2", "attn_in_w", "attn_out_w", "enc_b1", "enc_b2", "enc_g", "enc_beta",
                         "attn_in_b", "attn_out_b"])
    decw = pack(inputs, ["sig_w1", "tan_w1", "sig_w2", "tan_w2", "dec_w1", "dec_w2", "sig_b1", "sig_b2", "tan_b1",
                         "tan_b2", "dec_b1", "dec_b2", "dec_g", "dec_beta"])
    lstmw = pack(inputs, ["lstm_wi_f", "lstm_wh_f", "lstm_wi_b", "lstm_wh_b"])
    lstmb = np.stack([np.asarray(inputs["L0_ffn_lstm_b_f"]), np.asarray(inputs["L0_ffn_lstm_b_b"])], axis=1)
    lstmb = np.tile(lstmb, (1, P // 2, 1))
    arrays = {
        "patches": patches, "tokw": tokw, "wembed": t["W_embed"], "bcoord": t["b_coord"][:, None],
        "bspin": t["b_spinor"][:, None], "rbias": np.asarray(inputs["L0_ffn_router_b"]), "consts": consts,
        "selw": selw, "encw": encw, "lstmw": lstmw, "lstmb": lstmb, "decw": decw,
    }
    arrays = {k: np.ascontiguousarray(v) for k, v in arrays.items()}
    nc = bacc.Bacc("TRN2", target_bir_lowering=False, num_devices=1)
    aps = {k: nc.dram_tensor("in_" + k, v.shape, mybir.dt.from_np(v.dtype), kind="ExternalInput").ap()
           for k, v in arrays.items()}
    out = nc.dram_tensor("out", (P, N), F32, kind="ExternalOutput").ap()
    build(nc, out=out, **aps)
    r = run_bass_kernel_spmd(nc, [{"in_" + k: v for k, v in arrays.items()}], core_ids=[0])
    return np.ascontiguousarray(r.results[0]["out"].reshape(P, NB, T).transpose(1, 2, 0))
```

```python
from contextlib import ExitStack

import numpy as np

import concourse.bass as bass
from concourse import mybir

ALU = mybir.AluOpType
ACT = mybir.ActivationFunctionType
AX = mybir.AxisListType
F32 = mybir.dt.float32
F32R = mybir.dt.float32r
BF16 = mybir.dt.bfloat16

P = 128
NB = 64
T = 49
N = NB * T
BC = 8
CH = BC * T
NCH = N // CH
STREAMS = 4
S4 = range(STREAMS)
S8 = range(NCH)
ITERS = NCH // STREAMS
SPLIT_CHUNK = 4
SLOTS = 8
LOOPS = NCH // 2
E = 4
DF = 256
NH = 16
DH = DF // NH
TP = 64
KP = 6
PATCH = 16
GRID = 7
RT = 2 * T
RG = N // RT
EPS = 1e-5
H_INIT = 1e-6

ENC_COLS = [("w1", 256), ("w2", 512), ("aiw", 1536), ("aow", 512), ("b1", 2), ("b2", 2), ("g", 2),
            ("beta", 2), ("bq", 2), ("bk", 2), ("bv", 2), ("bo", 2)]
DEC_COLS = [("sw1", 1024), ("tw1", 1024), ("sw2", 512), ("tw2", 512), ("dw1", 512), ("dw2", 256),
            ("sb1", 2), ("sb2", 2), ("tb1", 2), ("tb2", 2), ("db1", 2), ("db2", 1), ("g", 1), ("beta", 1)]
TOK_COLS = [("wp", KP * P), ("wo", P), ("wg", 3 * P), ("wr", E), ("wc", 8), ("ws", 4), ("bp", 1),
            ("be", 1), ("g", 1), ("beta", 1), ("bo", 1), ("bg", 3), ("pos", T)]
LSTM_COLS = 4 * 2 * 1024
DEC_W = sum(w for _, w in DEC_COLS[:6])
SPLIT_FROM = 8
SPLIT_STEPS = 40
SPLIT_W = DEC_W // SPLIT_STEPS
CONST_COLS = [("ident", P), ("mask", 8), ("onesbd", 32)]


def width(cols):
    return sum(w for _, w in cols)


def views(ap, cols):
    out, at = {}, 0
    for name, w in cols:
        out[name] = ap[:, at:at + w]
        at += w
    return out


class Steps:

    def __init__(self, sem, names, done=0):
        self.sem, self.names = sem, names.split()
        self.count = len(self.names)
        self.start = done * self.count + 1

    def before(self, it, shift=0):
        return it * self.count + (shift * self.count + self.start)

    def after(self, it, name, shift=0):
        return it * self.count + (shift * self.count + self.names.index(name) + 1 + self.start)


TOK_STEPS = ("embed addpos coord coordb sq2 proj man mul add mean center square var sqrt recip norm affine "
             "out store")
GRU_STEPS = ("mean center square var sqrt recip norm pref fbias prei ibias preh hbias relu abs exp ln soft "
             "diff gates gh ready")
FIN_STEPS = "mean center square var sqrt recip norm"
ROUTE_STEPS = "logits bias max shift exp sum recip weight turned kept0 kept1"
ENC_STEPS = "w1 relu w2 bias square var sqrt recip norm affine"
IN_STEPS = "copy q qevac k kevac v vfirst vlast"
OUT_STEPS = "out store"
MASK_STEPS = "maskv maskp"
PAIR_STEPS = "scores max shift exp turn turned"
SUM_STEPS = "pv recip norm"
DEC_STEPS = ("mhi mlo s1 srelu shi slo t1 trelu thi tlo s2 sig t2 tanh gate ghi glo d1 drelu dhi dlo route kept "
             "d2 bias square var sqrt recip norm weigh add")


def build(nc, patches, tokw, wembed, bcoord, bspin, rbias, consts, selw, encw, lstmw, lstmb, decw, out):
    ctx = ExitStack()
    with ctx:
        def sb(name, shape, dt=F32):
            return ctx.enter_context(nc.sbuf_tensor(name, shape, dt))

        def sem(name):
            return ctx.enter_context(nc.semaphore(name))

        alias = {}
        with ExitStack() as views_only:
            for name, w in (("memory", 4 * N), ("hidden", 2 * N + 16), ("mixed", 2 * N), ("dec_sb", width(DEC_COLS)),
                            ("lstm_sb", LSTM_COLS)):
                alias[name] = views_only.enter_context(nc.sbuf_tensor(name + "_rounded", [P, w], F32R))
        memory = sb("memory", [P, 4 * N])
        hidden = sb("hidden", [P, 2 * N + 16])
        mixed = sb("mixed", [P, 2 * N])
        dec_sb = sb("dec_sb", [P, width(DEC_COLS)])
        lstm_sb = sb("lstm_sb", [P, LSTM_COLS])
        xn = sb("xn", [P, N])
        acc = sb("acc", [P, N])
        routed = sb("routed", [P, N])
        enc_sb = sb("enc_sb", [P, width(ENC_COLS)])
        const_sb = sb("const_sb", [P, width(CONST_COLS)])
        avg = sb("avg", [P, P])
        sel_sb = sb("sel_sb", [P, P])
        vbd = sb("vbd", [P, BC * 8 * 32])
        cell = sb("cell", [P, DF])
        hstep = sb("hstep", [P, DF])
        eps = sb("eps", [P, 1])
        ones_fb = sb("ones_fb", [P, 2, TP], BF16)
        bias3 = sb("bias3", [P, 4 * DF], BF16)
        rowsum = sb("rowsum", [P, 6])
        enc_fixed = sb("enc_fixed", [P, 4])
        ps = ctx.enter_context(nc.psum_tensor("ps", [P, 8, 512], F32))

        const = views(const_sb, CONST_COLS)
        ident = const["ident"]
        enc = views(enc_sb, ENC_COLS)
        dec = views(dec_sb, DEC_COLS)
        tok = views(lstm_sb, TOK_COLS)
        tw = width(TOK_COLS)
        rb_sb = lstm_sb[:, tw + 512:tw + 516]
        wembed_sb = lstm_sb[0:8, tw + 516:tw + 644]
        bcoord_sb = lstm_sb[0:8, tw + 644:tw + 645]
        bspin_sb = lstm_sb[0:4, tw + 645:tw + 646]
        ones4 = lstm_sb[0:4, tw + 648:tw + 776]
        mem4 = memory[:, :].rearrange("p (k n) -> p k n", k=4)
        hid2 = hidden[:, 0:2 * N].rearrange("p (k n) -> p k n", k=2)
        mix2 = mixed[:, :].rearrange("p (k n) -> p k n", k=2)

        def held(eng):
            eng.sem_inc(passed[eng.engine == G.engine], 1)

        def bank(b, w=CH, rows=P):
            return ps[0:rows, b, 0:w]

        def two(b):
            return ps[:, b:b + 2, 0:CH]

        def tile(ap, m, w=CH):
            return ap[:, m * w:(m + 1) * w]

        def carve(base, start, *widths):
            got, at = [], start
            for w in widths:
                got.append(base[:, at:at + w])
                at += w
            return got, at

        def chunk(s):
            return slice(s * CH, (s + 1) * CH)

        patches_in = [sem(f"patches_in{k}") for k in range(NCH // 2)]
        tokw_in, enc_in, lstm_in, lstmb_in, dec_in, saved = (
            sem(x) for x in ("tokw_in", "enc_in", "lstm_in", "lstmb_in", "dec_in", "saved"))
        clear, eps_set = sem("clear"), sem("eps_set")
        passed = sem("passed_pe"), sem("passed_pool")
        G = nc.gpsimd
        tk = [Steps(sem(f"tok_step{c}"), TOK_STEPS) for c in S8]
        gr = [Steps(sem(f"gru_step{s}"), GRU_STEPS) for s in S8]
        fi = [Steps(sem(f"fin_step{s}"), FIN_STEPS) for s in S8]
        ro = Steps(sem("route_step"), ROUTE_STEPS)
        en = [Steps(sem(f"enc_step{c}"), ENC_STEPS, done=1) for c in S8]
        ai = [Steps(sem(f"attin_step{s}"), IN_STEPS) for s in (0, 1)]
        ao = [Steps(sem(f"attout_step{s}"), OUT_STEPS) for s in (0, 1)]
        pr = [Steps(sem(f"pair_step{s}"), PAIR_STEPS) for s in (0, 1)]
        mk = [Steps(sem(f"mask_step{s}"), MASK_STEPS) for s in (0, 1)]
        su = [Steps(sem(f"sum_step{s}"), SUM_STEPS) for s in (0, 1)]
        de = [Steps(sem(f"dec_step{c}"), DEC_STEPS, done=1) for c in S8]
        scan = sem("scan")
        SCAN = 4
        bias_split = sem("bias_split")
        SPLIT = 6
        bias_products = sem("bias_products")
        enc_bias = sem("enc_bias")
        enc_prep = sem("enc_prep")
        HALVINGS = 8
        ENC_PREP = HALVINGS + 2
        w_hi, w_lo = sem("w_hi"), sem("w_lo")
        dec_mean = sem("dec_mean")
        dec_prep = sem("dec_prep")
        DEC_PREP = 4
        x_turned = sem("x_turned")
        z_in = sem("z_in")
        z_lo, z_hi = sem("z_lo"), sem("z_hi")
        gates = sem("gates")
        v_cleared = sem("v_cleared")
        c_new, ig_new = sem("c_new"), sem("ig_new")
        c_tanh = sem("c_tanh")
        h_new = sem("h_new")
        h_turned = sem("h_turned")
        h_kept = sem("h_kept")
        h_saved = sem("h_saved")

        def slots(base, start, *tiles):
            return carve(base, start, *(n * CH for n in tiles))[0]

        tok_space = [slots(base, start, 1, 1, 1, 1, 1, 1, 1)
                     for base, start in ((hidden, 0), (hidden, N), (xn, 0), (dec_sb, 0))]
        gru_space = [slots(base, start, 1, 1, 1, 1, 2, 2)
                     for base, start in [(memory, s * N) for s in S4]
                     + [(hidden, 0), (hidden, N), (xn, 0), (dec_sb, 0)]]
        fin_space = [(memory[:, s * CH:(s + 1) * CH], memory[:, N + s * CH:N + (s + 1) * CH]) for s in S8]
        logit, top, total = (v[0:RT, :] for v in carve(hidden, 0, RG * E, RG, RG)[0])
        logit3 = logit.rearrange("p (g e) -> p g e", e=E)
        enc_x = ([(mixed[:, x:x + 2 * CH], mixed[:, r:r + CH]) for x, r in
                  ((0, 2 * CH), (N, 3 * CH), (N + 2 * CH, N + 6 * CH), (N + 4 * CH, N + 7 * CH))]
                 + [slots(memory, s * N + 4 * CH, 2, 1) for s in S4])
        enc_a = [slots(memory, s * N, 2, 2) for s in S4]
        dec_x = [[mem4[:, j, chunk(c)] for j in range(3)] for c in S8]
        dec_space = [slots(base, start, 2, 2, 4) for base, start in
                     ((mixed, 0), (mixed, 8 * CH), (lstm_sb, 0), (lstm_sb, 8 * CH))]
        dec_a = [(a, b[:, 0:2 * CH]) for a, _, b in dec_space]
        dec_hi = [(a, b[:, 2 * CH:]) for _, a, b in dec_space]
        mem_hi = [b for _, _, b in dec_space] + [lstm_sb[:, 16 * CH:20 * CH], hidden[:, 0:4 * CH]] + [
            b for _, _, b in dec_space[2:]]
        w_high = hidden[:, 7 * DF:7 * DF + DEC_W]
        W_HIGH = 7 * DF - SPLIT_FROM * SPLIT_W
        assert SPLIT_FROM + SPLIT_STEPS == T - 1 and SPLIT_W * SPLIT_STEPS == DEC_W
        dec_wh = views(w_high, DEC_COLS[:6])
        (km0, km1, ks0, ks1, prob0, prob1, pt0, pt1, rec0, rec1, vodd, mx0, mx1, ot0, ot1), att_end = carve(
            memory, 0, 4 * 8 * T, 4 * 8 * T, 2 * CH, 2 * CH, NH * TP, NH * TP, NH * T, NH * T, 4 * T, 4 * T,
            BC * 8 * 32, NH, NH, 2 * CH, 2 * CH)
        assert att_end <= 4 * N
        (qs0, qs1, hc0, hc1), _ = carve(dec_sb, 0, 2 * CH + 16, 2 * CH + 16, 2 * CH + 32, 2 * CH + 32)
        masked = [v.rearrange("p (m b h t) -> p m b h t", m=2, b=2, h=8) for v in (km0, km1)]
        prob = [v.rearrange("p (h t) -> p h t", h=NH) for v in (prob0, prob1)]
        probT = [v.rearrange("p (h bt) -> p h bt", h=8) for v in (pt0, pt1)]
        rec = [rec0, rec1]
        mx = [mx0, mx1]
        vb = [v.rearrange("p (b h c) -> p b h c", b=BC, h=8) for v in (vbd[:, :], vodd)]
        hc = [v.rearrange("p (k n) -> p k n", k=2) for v in (hc0, hc1)]
        qs, ks = (qs0, qs1), (ks0, ks1)
        ot = (ot0, ot1)
        (b32, btmp), split_end = carve(mixed, SPLIT_CHUNK * CH, 4 * DF, 2 * DF)
        assert split_end <= N
        btmp = btmp.bitcast(BF16)
        (gate, xs, hT), _ = carve(hidden, 0, 4 * DF, 4 * P, DF)
        xs4 = xs.rearrange("p (r k c) -> p r k c", r=2, k=2)
        hT2 = hT.rearrange("p (k c) -> p k c", k=2)
        wl = lstm_sb[:, :].rearrange("p (w k n) -> p w k n", w=4, k=2)

        def v_places(c, half, copy):
            for h in (0, 1):
                for o in (0, 1):
                    src = ps[64 * h:64 * h + 64, 6 + half, :].rearrange(
                        "p (b g o d) -> p b g o d", b=2, g=8, o=2)[:, :, :, o, :]
                    last = copy(vb[c][64 * o:64 * o + 64, 4 * half + h:4 * half + h + 3:2, :,
                                      DH * o:DH * (o + 1)], src)
            return last

        def rounded(ap):
            return bass.AP(tensor=alias[ap.tensor.name], offset=ap.offset, ap=[list(x) for x in ap.ap])

        block = ctx.enter_context(nc.Block())

        @block.sync
        def _(sp):
            sp.dma_start(const_sb[:, :], consts).then_inc(tokw_in, 16)
            sp.dma_start(lstm_sb[:, 0:tw], tokw).then_inc(tokw_in, 16)
            sp.dma_start(wembed_sb, wembed).then_inc(tokw_in, 16)
            sp.dma_start(bcoord_sb, bcoord).then_inc(tokw_in, 16)
            sp.dma_start(bspin_sb, bspin).then_inc(tokw_in, 16)
            sp.dma_start(rb_sb, rbias.partition_broadcast(P)).then_inc(tokw_in, 16)
            for k in range(NCH // 2):
                pair = slice(2 * k * CH, 2 * (k + 1) * CH)
                sp.dma_start(mem4[:, :, pair], patches[:, 0:4, pair]).then_inc(patches_in[k], 16)
                sp.dma_start(mix2[:, :, pair], patches[:, 4:6, pair]).then_inc(patches_in[k], 16)
            with sp.Fori(0, E) as e:
                for c in (0, 1):
                    sp.wait_ge(ao[c].sem, ao[c].before(e * LOOPS))
                sp.dma_start(enc_sb[:, :], encw[e]).then_inc(enc_in, 16)
                sp.wait_ge(ro.sem, ro.before(1))
                for c in S8:
                    sp.wait_ge(de[c].sem, de[c].before(e))
                sp.dma_start(lstm_sb[:, :], lstmw[e]).then_inc(lstm_in, 16)
                sp.dma_start(b32, lstmb[e]).then_inc(lstmb_in, 16)
                for c in (0, 1):
                    sp.wait_ge(ao[c].sem, ao[c].before((e + 1) * LOOPS))
                sp.dma_start(dec_sb[:, :], decw[e]).then_inc(dec_in, 16)
                sp.dma_start(sel_sb[:, :], selw[e]).then_inc(dec_in, 16)
            for c in S8:
                sp.wait_ge(de[c].sem, de[c].before(E))
            sp.dma_start(out, acc[:, :]).then_inc(saved, 16)
            sp.wait_ge(saved, 16)

        @block.tensor
        def _(pe):
            def mm(o, l, r, start=True, stop=True, **kw):
                return pe.matmul(o, l, r, start=start, stop=stop, **kw)

            def average(st, it, need, s, m, x, k):
                pe.wait_ge(st[s].sem, st[s].after(it, need))
                for j in range(k):
                    last = mm(bank(2 * (s % 4) + m), avg[:, :], tile(x, j), j == 0, j == k - 1)
                last.then_inc(st[s].sem, 1)

            def product(st, s, w, stride, rhs, k, ms=(0, 1)):
                for m in ms:
                    for j in range(k):
                        last = mm(bank(2 * (s % 4) + m), w[:, j * stride + m * P:j * stride + (m + 1) * P], rhs(j),
                                  j == 0, j == k - 1)
                last.then_inc(st[s].sem, 1)

            pe.wait_ge(tokw_in, 96)
            pe.wait_ge(clear, 5)
            def tok_out(c):
                pe.wait_ge(tk[c].sem, tk[c].after(0, "affine"))
                mm(bank(2 * (c % 4) + 1), tok["wo"], tok_space[c % 4][4]).then_inc(tk[c].sem, 1)

            for i in range(ITERS):
                part = [(s, i * STREAMS + s) for s in S4]
                for s, c in part:
                    if c % 2 == 0:
                        pe.wait_ge(patches_in[c // 2], 32)
                    if i:
                        pe.wait_ge(tk[c - STREAMS].sem, tk[c - STREAMS].after(0, "center"))
                    product(tk, c, tok["wp"], P, lambda j: mem4[:, j, chunk(c)] if j < 4 else mix2[:, j - 4, chunk(c)],
                            KP, (0,))
                for s, c in part:
                    if i:
                        tok_out(c - STREAMS)
                for s, c in part:
                    raw = tok_space[s][3]
                    if i:
                        pe.wait_ge(tk[c - STREAMS].sem, tk[c - STREAMS].after(0, "store"))
                    pe.wait_ge(tk[c].sem, tk[c].after(0, "addpos"))
                    mm(bank(2 * s + 1, rows=8), tok["wc"], raw)
                    mm(bank(2 * s, rows=4), tok["ws"], raw).then_inc(tk[c].sem, 1)
                for s, c in part:
                    x, sq, rs, raw, co, sp_, xm = tok_space[s]
                    pe.wait_ge(tk[c].sem, tk[c].after(0, "sq2"))
                    mm(bank(2 * s), ones4, sp_[0:4, :])
                    mm(bank(2 * s + 1), wembed_sb, co[0:8, :]).then_inc(tk[c].sem, 1)
                for s, c in part:
                    average(tk, 0, "add", c, 0, tok_space[s][0], 1)
                for s, c in part:
                    average(tk, 0, "square", c, 1, tok_space[s][1], 1)
            for c in range(STREAMS, NCH):
                tok_out(c)

            for c in S8:
                pe.wait_ge(tk[c].sem, tk[c].before(1))
            for s in S8:
                mm(bank(s), avg[:, :], acc[:, chunk(s)]).then_inc(gr[s].sem, 1)
            for s in S8:
                pe.wait_ge(gr[s].sem, gr[s].after(0, "square"))
                mm(bank(s), avg[:, :], gru_space[s][1]).then_inc(gr[s].sem, 1)
            for part in (S8[:4], S8[4:]):
                for need, k in (("norm", 0), ("fbias", 1), ("ibias", 2)):
                    for s in part:
                        pe.wait_ge(gr[s].sem, gr[s].after(0, need))
                        mm(bank(s), tile(tok["wg"], k, P), gru_space[s][0]).then_inc(gr[s].sem, 1)

            pe.wait_ge(scan, SCAN)
            for s in S8:
                mm(bank(s), avg[:, :], acc[:, chunk(s)]).then_inc(fi[s].sem, 1)
            for s in S8:
                pe.wait_ge(fi[s].sem, fi[s].after(0, "square"))
                mm(bank(s), avg[:, :], fin_space[s][0]).then_inc(fi[s].sem, 1)
            for g in range(RG):
                s = g * RT // CH
                if g * RT % CH == 0:
                    pe.wait_ge(fi[s].sem, fi[s].after(0, "norm"))
                last = mm(ps[0:RT, 0, g * E:(g + 1) * E], xn[:, g * RT:(g + 1) * RT], tok["wr"])
            last.then_inc(ro.sem, 1)
            pe.wait_ge(ro.sem, ro.after(0, "weight"))
            for g in range(RG):
                s, at = g * RT // CH, g * RT % CH
                last = pe.transpose(ps[0:E, s, at:at + RT], logit[:, g * E:(g + 1) * E], ident[0:RT, 0:RT])
            last.then_inc(ro.sem, 1)
            pe.wait_ge(ro.sem, ro.before(1))

            with pe.Fori(0, E) as e:
                def enc_average(c):
                    pe.wait_ge(en[c].sem, en[c].after(e, "square"))
                    for j in (0, 1):
                        last = mm(bank(2 * (c % 4) + 1), avg[:, :], tile(enc_a[c % 4][1], j), j == 0, j == 1)
                    last.then_inc(en[c].sem, 1)

                pe.wait_ge(enc_in, e * 16 + 16)
                pe.wait_ge(de[7].sem, de[7].after(e, "sqrt", -1))
                held(pe)
                for k in (0, 1):
                    mm(ps[:, 7, 0:1], avg[:, :], enc["b2"][:, k:k + 1], k == 0, k == 1)
                for m in (0, 1):
                    for k in (0, 1):
                        last = mm(ps[:, 7, 2 + m:3 + m], enc["aow"][:, k * DF + m * P:k * DF + (m + 1) * P],
                                  enc["bv"][:, k:k + 1], k == 0, k == 1)
                last.then_inc(bias_products, 1)
                for i in range(ITERS):
                    for s in S4:
                        c = i * STREAMS + s
                        if i == 0:
                            pe.wait_ge(de[c + STREAMS].sem, de[c + STREAMS].after(e, "sqrt", -1))
                            if s == 3:
                                pe.wait_ge(enc_bias, e + 1)
                        else:
                            pe.wait_ge(en[c - STREAMS].sem, en[c - STREAMS].after(e, "sqrt"))
                        product(en, c, enc["w1"], 0, lambda j: xn[:, chunk(c)], 1)
                    if i == 0:
                        pe.wait_ge(enc_prep, e * ENC_PREP + ENC_PREP)
                    for s in S4:
                        c = i * STREAMS + s
                        pe.wait_ge(en[c].sem, en[c].after(e, "relu"))
                        product(en, c, enc["w2"], DF, lambda j: tile(enc_a[s][0], j), 2)
                    for s in S4:
                        enc_average(i * STREAMS + s)

                def project(c, w0, st):
                    for m in (0, 1):
                        for k in (0, 1):
                            at = k * 3 * DF + w0 + m * P
                            last = mm(bank(6 + m), enc["aiw"][:, at:at + P], hc[c][:, k, 0:CH], k == 0, k == 1)
                    last.then_inc(st.sem, 1)

                def project_q(c, it, shift):
                    pe.wait_ge(ai[c].sem, ai[c].after(it, "copy", shift))
                    project(c, 0, ai[c])

                def project_k(c, it, shift):
                    pe.wait_ge(ai[c].sem, ai[c].after(it, "qevac", shift))
                    project(c, DF, ai[c])

                def project_v(c, it, shift):
                    pe.wait_ge(ai[c].sem, ai[c].after(it, "kevac", shift))
                    for p in range(4):
                        for k in (0, 1):
                            for h in (0, 1):
                                b0 = (2 * p + h) * T
                                last = mm(ps[64 * h:64 * h + 64, 6 + p // 2, (p % 2) * DF:(p % 2 + 1) * DF],
                                          hc[c][:, k, b0:b0 + TP],
                                          enc["aiw"][:, k * 3 * DF + 2 * DF:(k + 1) * 3 * DF], k == 0, k == 1)
                    last.then_inc(ai[c].sem, 1)

                def project_out(c, pit, pshift):
                    for q in (0, 1):
                        pe.wait_ge(su[q].sem, su[q].after(pit, "norm", pshift))
                    for m in (0, 1):
                        for k in (0, 1):
                            last = mm(bank(6 + m), enc["aow"][:, k * DF + m * P:k * DF + (m + 1) * P],
                                      tile(ot[c], k), k == 0, k == 1)
                    last.then_inc(ao[c].sem, 1)

                def scores(u, pit, shift):
                    c, p, st, b = u // 4 % 2, u % 4, pr[u % 2], 3 * (u % 2)
                    pe.wait_ge(mk[u % 2].sem, mk[u % 2].after(pit, "maskp", shift))
                    pe.wait_ge(st.sem, st.before(pit, shift))
                    for m in (0, 1):
                        for h in (0, 1):
                            b0 = m * CH + (2 * p + h) * T
                            last = mm(ps[64 * h:64 * h + 64, b + m, 0:CH], qs[c][:, b0:b0 + TP],
                                      masked[u % 2][:, m, h, :, :].rearrange("p h t -> p (h t)"))
                    last.then_inc(st.sem, 1)

                def turn_probs(u, pit, shift):
                    st, b = pr[u % 2], 3 * (u % 2)
                    pe.wait_ge(st.sem, st.after(pit, "exp", shift))
                    for hp in range(8):
                        at = (hp % 4) * P
                        last = pe.transpose(ps[:, b + hp // 4, at:at + P],
                                            prob[u % 2][:, 2 * hp:2 * hp + 2, :].rearrange("p h t -> p (h t)"), ident)
                    last.then_inc(st.sem, 1)

                def weigh(u, pit, shift):
                    c, p, st, b = u // 4 % 2, u % 4, su[u % 2], 3 * (u % 2) + 2
                    pe.wait_ge(pr[u % 2].sem, pr[u % 2].after(pit, "turned", shift))
                    pe.wait_ge(st.sem, st.before(pit, shift))
                    for m in (0, 1):
                        for h in (0, 1):
                            for q in range(4):
                                at = m * 2 * T + h * T
                                mm(ps[32 * q:32 * q + 32, b, at:at + T], vb[c][:, 2 * p + h, 4 * m + q, :],
                                   probT[u % 2][:, 4 * m + q, h * T:(h + 1) * T])
                    for q in range(4):
                        last = mm(ps[32 * q:32 * q + 32, b, 4 * T:8 * T], const["onesbd"], probT[u % 2][:, q::4, :])
                    last.then_inc(st.sem, 1)

                def slot(i, u, first, final):
                    c, p = u // 4, u % 4
                    cit, pit = e * LOOPS + i, e * (2 * SLOTS) + i * (SLOTS // 2)
                    scores(u, pit, u // 2)
                    nxt = (1 - c, cit, c)
                    has_next = not (final and c == 1)
                    if p == 0 and not (first and u == 0):
                        weigh((u - 1) % SLOTS, pit, (u - 1) // 2)
                    if p == 0 and has_next:
                        pe.wait_ge(ai[c].sem, ai[c].after(cit, "vlast"))
                        project_q(*nxt)
                    if p == 1 and not (first and c == 0):
                        if has_next:
                            pe.wait_ge(ai[1 - c].sem, ai[1 - c].after(cit, "qevac", c))
                        project_out(1 - c, pit, u // 2 - 1)
                    if p == 2 and has_next:
                        if not (first and c == 0):
                            pe.wait_ge(ao[1 - c].sem, ao[1 - c].after(cit, "store", c - 1))
                        project_k(*nxt)
                    if p == 3 and has_next:
                        project_v(*nxt)
                    if u == 1:
                        pe.wait_ge(ai[0].sem, ai[0].after(cit, "vlast"))
                    if u == 5:
                        pe.wait_ge(ai[1].sem, ai[1].after(cit, "vlast"))
                    if p != 0:
                        weigh(u - 1, pit, (u - 1) // 2)
                    turn_probs(u, pit, u // 2)

                pe.wait_ge(en[7].sem, en[7].after(e, "sqrt"))
                project_q(0, e * LOOPS, 0)
                project_k(0, e * LOOPS, 0)
                project_v(0, e * LOOPS, 0)
                for c in range(STREAMS, NCH - 1):
                    pe.wait_ge(en[c].sem, en[c].after(e, "sqrt"))
                for u in range(SLOTS):
                    slot(0, u, True, False)
                with pe.Fori(1, LOOPS - 1) as i:
                    for u in range(SLOTS):
                        slot(i, u, False, False)
                for u in range(SLOTS):
                    slot(LOOPS - 1, u, False, True)
                weigh(SLOTS - 1, e * (2 * SLOTS), 2 * SLOTS - 1)
                pe.wait_ge(ao[0].sem, ao[0].after(e * LOOPS, "store", LOOPS - 1))
                project_out(1, e * (2 * SLOTS), 2 * SLOTS - 1)

                pe.wait_ge(lstm_in, e * 16 + 16)
                pe.wait_ge(bias_split, e * SPLIT + SPLIT)

                def input_part(t, par, between=None):
                    pe.wait_ge(x_turned, e * T + t + 1)
                    for half in (0, 1):
                        mm(ps[:, 2 * par + half, :], ones_fb[:, :, :].rearrange("p d b -> p (d b)"),
                           bias3[:, half * 512:half * 512 + 512], True, False, skip_group_check=True)
                        for k in (0, 1):
                            for d in (0, 1):
                                last = mm(ps[64 * d:64 * d + 64, 2 * par + half, :], xs4[:, par, k, 64 * d:64 * d + 64],
                                          wl[:, 2 * d, k, half * 512:half * 512 + 512], False, False,
                                          skip_group_check=True)
                            if half == 1 and k == 0 and between:
                                between()
                    last.then_inc(z_in, 1)

                def step(t, par, last_step=False):
                    pe.wait_ge(h_kept, e * (T + 1) + t + 1)
                    for half in (0, 1):
                        for k in (0, 1):
                            for d in (0, 1):
                                last = mm(ps[64 * d:64 * d + 64, 2 * par + half, :], hT2[:, k, 64 * d:64 * d + 64],
                                          wl[:, 2 * d + 1, k, half * 512:half * 512 + 512], False, k == 1,
                                          skip_group_check=True)
                        last.then_inc(z_lo if half == 0 else z_hi, 1)

                    def turn_h():
                        pe.wait_ge(h_new, e * T + t + 1)
                        for k in (0, 1):
                            turned = pe.transpose(ps[:, 4, k * P:(k + 1) * P], hstep[:, k * P:(k + 1) * P], ident)
                        turned.then_inc(h_turned, 1)

                    if last_step:
                        turn_h()
                    else:
                        input_part(t + 1, 1 - par, turn_h)

                input_part(0, 0)
                with pe.Fori(0, T // 2) as i:
                    step(i * 2, 0)
                    step(i * 2 + 1, 1)
                step(T - 1, 0, last_step=True)

                def split_product(c, w, stride, hi, lo, k, ms=(0, 1)):
                    for m in ms:
                        for j in range(k):
                            at = slice(j * stride + m * P, j * stride + (m + 1) * P)
                            o = bank(2 * (c % 4) + m)
                            mm(o, rounded(dec_wh[w][:, at]), rounded(hi(j)), j == 0, False)
                            mm(o, rounded(dec_wh[w][:, at]), rounded(lo(j)), False, False)
                            last = mm(o, rounded(dec[w][:, at]), rounded(hi(j)), False, j == k - 1)
                    last.then_inc(de[c].sem, 1)

                pe.wait_ge(dec_in, e * 32 + 32)
                pe.wait_ge(w_lo, e * SPLIT_STEPS + SPLIT_STEPS)
                held(pe)
                mm(ps[:, 7, 0:1], avg[:, :], dec["db2"]).then_inc(dec_mean, 1)
                for i in range(ITERS):
                    part = [(s, i * STREAMS + s) for s in S4]
                    for name, need, w in (("s1", "mlo", "sw1"), ("t1", "slo", "tw1")):
                        for s, c in part:
                            if name == "s1" and i:
                                pe.wait_ge(de[c - STREAMS].sem, de[c - STREAMS].after(e, "sqrt"))
                            elif name == "s1" and s == 3:
                                pe.wait_ge(dec_prep, e * DEC_PREP + DEC_PREP)
                            pe.wait_ge(de[c].sem, de[c].after(e, need))
                            split_product(c, w, DF, lambda j: tile(mem_hi[c], j), lambda j: mem4[:, j, chunk(c)], 4)
                    for need, w, src in (("tlo", "sw2", 0), ("sig", "tw2", 1), ("glo", "dw1", 0)):
                        for s, c in part:
                            pe.wait_ge(de[c].sem, de[c].after(e, need))
                            split_product(c, w, DF, lambda j: tile(dec_hi[s][src], j),
                                          lambda j: tile(dec_a[s][src], j), 2)
                    for s, c in part:
                        pe.wait_ge(de[c].sem, de[c].after(e, "dlo"))
                        mm(bank(2 * s + 1), sel_sb[:, :], routed[:, chunk(c)]).then_inc(de[c].sem, 1)
                    for s, c in part:
                        pe.wait_ge(de[c].sem, de[c].after(e, "kept"))
                        split_product(c, "dw2", P, lambda j: tile(dec_hi[s][1], j),
                                      lambda j: tile(dec_a[s][1], j), 2, (0,))
                    for s, c in part:
                        pe.wait_ge(de[c].sem, de[c].after(e, "square"))
                        mm(bank(2 * s + 1), avg[:, :], tile(dec_a[s][1], 0)).then_inc(de[c].sem, 1)

        @block.vector
        def _(dve):
            V = nc.vector

            def ts(o, i, a, b, op0, op1=None):
                return V.tensor_scalar(o, i, a, b, op0, op1) if op1 else V.tensor_scalar(o, i, a, None, op0)

            def recip(st, it, s, rs):
                dve.wait_ge(st[s].sem, st[s].after(it, "sqrt"))
                V.reciprocal(rs, rs).then_inc(st[s].sem, 1)

            def norm(st, it, s, x, rs, k, o=None):
                dve.wait_ge(st[s].sem, st[s].after(it, "recip"))
                x3 = x.rearrange("p (k n) -> p k n", k=k)
                V.tensor_tensor(x3 if o is None else o, x3, rs.unsqueeze(1).broadcast_to([P, k, CH]),
                                ALU.mult).then_inc(st[s].sem, 1)

            def centre(prep, n, w, wide):
                w3 = w.rearrange("p (k n) -> p k n", k=2)
                V.tensor_reduce(rowsum[:, 0:2], w3, AX.X, ALU.add).then_inc(prep, 1)
                dve.wait_ge(prep, n + 1)
                ts(rowsum[:, 2:4], rowsum[:, 0:2], 1.0 / wide, None, ALU.mult).then_inc(prep, 1)
                dve.wait_ge(prep, n + 2)
                V.tensor_tensor(w3, w3, rowsum[:, 2:4].unsqueeze(2).broadcast_to([P, 2, wide]),
                                ALU.subtract).then_inc(prep, 1)

            V.memset(avg[:, :], 1.0 / P)
            V.memset(hidden[:, 2 * N:2 * N + 16], 0.0)
            V.memset(vbd[:, :], 0.0)
            V.memset(routed[:, :], 0.0)
            V.memset(ones_fb[:, :, :], 0.0).then_inc(clear, 1)
            dve.wait_ge(clear, 1)
            for r in (0, 32, 64):
                V.memset(ones_fb[r:r + 2, 1, :], 1.0)
                V.memset(ones_fb[r:r + 1, 0, :], 1.0).then_inc(clear, 1)
            dve.wait_ge(clear, 4)
            for r in (0, 32, 64):
                V.memset(ones_fb[r:r + 1, 1, :], 0.0)
            started = [(st.sem, st.start) for st in tk + gr + fi + [ro] + en + ai + ao + pr + mk + su + de]
            for c, (first, value) in enumerate(started + [(h_saved, 1)]):
                V.memset(cell[:, c:c + 1], 0.0).then_inc(first, value)
            dve.wait_ge(tokw_in, 96)
            V.memset(ones4, 1.0)
            ts(tok["pos"], tok["pos"], tok["bp"], None, ALU.add).then_inc(clear, 1)

            dve.wait_ge(clear, 5)
            for i in range(ITERS):
                part = [(s, i * STREAMS + s) for s in S4]
                for s, c in part:
                    raw = tok_space[s][3]
                    dve.wait_ge(tk[c].sem, tk[c].after(0, "embed"))
                    V.tensor_tensor(raw.rearrange("p (b t) -> p b t", t=T),
                                    bank(2 * s).rearrange("p (b t) -> p b t", t=T),
                                    tok["pos"].unsqueeze(1).broadcast_to([P, BC, T]), ALU.add).then_inc(tk[c].sem, 1)
                for s, c in part:
                    x, sq, rs, raw, co, sp_, xm = tok_space[s]
                    dve.wait_ge(tk[c].sem, tk[c].after(0, "man"))
                    V.tensor_tensor(xm, xm, bank(2 * s), ALU.mult).then_inc(tk[c].sem, 1)
                for s, c in part:
                    x, sq, rs, raw, co, sp_, xm = tok_space[s]
                    dve.wait_ge(tk[c].sem, tk[c].after(0, "mul"))
                    V.tensor_tensor(x, xm, raw, ALU.add).then_inc(tk[c].sem, 1)
                for s, c in part:
                    x = tok_space[s][0]
                    dve.wait_ge(tk[c].sem, tk[c].after(0, "mean"))
                    V.tensor_tensor(x, x, bank(2 * s), ALU.subtract).then_inc(tk[c].sem, 1)
                for s, c in part:
                    recip(tk, 0, c, tok_space[s][2])
                    norm(tk, 0, c, tok_space[s][0], tok_space[s][2], 1)

            for s in S8:
                dve.wait_ge(gr[s].sem, gr[s].after(0, "mean"))
                V.tensor_tensor(gru_space[s][0], acc[:, chunk(s)], bank(s), ALU.subtract).then_inc(gr[s].sem, 1)
            def gru_norm(s):
                recip(gr, 0, s, gru_space[s][2])
                norm(gr, 0, s, gru_space[s][0], gru_space[s][2], 1)

            def gru_relu(s):
                x, sq, rs, ph, pf, re = gru_space[s]
                dve.wait_ge(gr[s].sem, gr[s].after(0, "hbias"))
                ts(re, pf, -1.0, 0.0, ALU.mult, ALU.max).then_inc(gr[s].sem, 1)

            for s in range(6):
                gru_norm(s)
            for s in S4:
                gru_relu(s)
            for s in (6, 7):
                gru_norm(s)
            for s in range(4, 8):
                gru_relu(s)
            for s in S8:
                x, sq, rs, ph, pf, re = gru_space[s]
                dve.wait_ge(gr[s].sem, gr[s].after(0, "soft"))
                V.tensor_tensor(rs, tile(re, 0), tile(re, 1), ALU.subtract)
                ts(tile(pf, 0), ph, 0.0, None, ALU.min).then_inc(gr[s].sem, 1)
            for s in S8:
                x, sq, rs, ph, pf, re = gru_space[s]
                dve.wait_ge(gr[s].sem, gr[s].after(0, "gates"))
                V.scalar_tensor_tensor(out=x, in0=ph, scalar=0.0, in1=x, op0=ALU.max,
                                       op1=ALU.add).then_inc(gr[s].sem, 1)
                dve.wait_ge(gr[s].sem, gr[s].after(0, "gh"))
                V.tensor_tensor(mixed[:, N + s * CH:N + (s + 1) * CH], x, sq, ALU.mult).then_inc(gr[s].sem, 1)
            for s in S8:
                dve.wait_ge(gr[s].sem, gr[s].before(1))
            f0 = mixed[:, 0:N].rearrange("p (b t) -> p b t", t=T)[:, :, 0]
            g0 = mixed[:, N:2 * N].rearrange("p (b t) -> p b t", t=T)[:, :, 0]
            V.scalar_tensor_tensor(out=g0, in0=f0, scalar=H_INIT, in1=g0, op0=ALU.mult, op1=ALU.add).then_inc(scan, 1)
            dve.wait_ge(scan, 1)
            V.memset(f0, 0.0).then_inc(scan, 1)
            dve.wait_ge(scan, 2)
            V.tensor_tensor_scan(memory[:, 0:N], mixed[:, 0:N], mixed[:, N:2 * N], 0.0, ALU.mult,
                                 ALU.add).then_inc(scan, 1)
            dve.wait_ge(scan, 3)
            V.tensor_tensor(acc[:, :], acc[:, :], memory[:, 0:N], ALU.add).then_inc(scan, 1)

            for s in S8:
                dve.wait_ge(fi[s].sem, fi[s].after(0, "mean"))
                V.tensor_tensor(xn[:, chunk(s)], acc[:, chunk(s)], bank(s), ALU.subtract).then_inc(fi[s].sem, 1)
            for s in S8:
                recip(fi, 0, s, fin_space[s][1])
                norm(fi, 0, s, xn[:, chunk(s)], fin_space[s][1], 1)
            every = [RT, RG, E]
            dve.wait_ge(ro.sem, ro.after(0, "logits"))
            V.tensor_tensor(logit3, ps[0:RT, 0, 0:RG * E].rearrange("p (g e) -> p g e", e=E),
                            rb_sb[0:RT, :].unsqueeze(1).broadcast_to(every), ALU.add).then_inc(ro.sem, 1)
            dve.wait_ge(ro.sem, ro.after(0, "bias"))
            V.tensor_reduce(top, logit3, AX.X, ALU.max).then_inc(ro.sem, 1)
            dve.wait_ge(ro.sem, ro.after(0, "max"))
            V.tensor_tensor(logit3, logit3, top.unsqueeze(2).broadcast_to(every), ALU.subtract).then_inc(ro.sem, 1)
            dve.wait_ge(ro.sem, ro.after(0, "exp"))
            V.tensor_reduce(total, logit3, AX.X, ALU.add).then_inc(ro.sem, 1)
            dve.wait_ge(ro.sem, ro.after(0, "sum"))
            V.reciprocal(total, total).then_inc(ro.sem, 1)
            dve.wait_ge(ro.sem, ro.after(0, "recip"))
            V.tensor_tensor(logit3, logit3, total.unsqueeze(2).broadcast_to(every), ALU.mult).then_inc(ro.sem, 1)
            dve.wait_ge(ro.sem, ro.after(0, "turned"))
            V.tensor_copy(routed[0:E, 0:4 * CH].rearrange("p (s n) -> p s n", s=4),
                          ps[0:E, 0:4, 0:CH]).then_inc(ro.sem, 1)

            with dve.Fori(0, E) as e:
                def normalise(c):
                    recip(en, e, c, enc_x[c][1])
                    norm(en, e, c, enc_x[c][0], enc_x[c][1], 2)

                for c in range(STREAMS + 1):
                    normalise(c)

                def q_evac(c, it, shift):
                    dve.wait_ge(ai[c].sem, ai[c].after(it, "q", shift))
                    for m in (0, 1):
                        last = ts(tile(qs[c], m), bank(6 + m), enc["bq"][:, m:m + 1], DH ** -0.5, ALU.add, ALU.mult)
                    last.then_inc(ai[c].sem, 1)

                def v_evac(c, it, shift):
                    dve.wait_ge(ai[c].sem, ai[c].after(it, "v", shift))
                    v_places(c, 0, V.tensor_copy).then_inc(ai[c].sem, 1)

                def mask(u, cit, cshift, pit, shift):
                    c, p = u // 4 % 2, u % 4
                    if shift is not None:
                        dve.wait_ge(pr[u % 2].sem, pr[u % 2].after(pit, "scores", shift - 1))
                    if p == 0:
                        dve.wait_ge(ai[c].sem, ai[c].after(cit, "kevac", cshift))
                    kk = ks[c][:, 2 * p * T:2 * (p + 1) * T].rearrange("p (b t) -> p b t", b=2)
                    V.tensor_tensor(masked[u % 2][:, 0, :, :, :], kk.unsqueeze(2).broadcast_to([P, 2, 8, T]),
                                    const["mask"].unsqueeze(1).unsqueeze(3).broadcast_to([P, 2, 8, T]),
                                    ALU.mult).then_inc(mk[u % 2].sem, 1)

                def finish_pair(u, pit, shift):
                    c, p, st, b = u // 4 % 2, u % 4, su[u % 2], 3 * (u % 2) + 2
                    dve.wait_ge(st.sem, st.after(pit, "pv", shift))
                    V.reciprocal(rec[u % 2], ps[:, b, 4 * T:8 * T]).then_inc(st.sem, 1)
                    dve.wait_ge(st.sem, st.after(pit, "recip", shift))
                    o = ot[c].rearrange("p (m n) -> p m n", m=2)[:, :, 2 * p * T:2 * (p + 1) * T]
                    V.tensor_tensor(o, ps[:, b, 0:4 * T].rearrange("p (m n) -> p m n", m=2),
                                    rec[u % 2].rearrange("p (m n) -> p m n", m=2), ALU.mult).then_inc(st.sem, 1)

                def split_bias(step):
                    if step == 0:
                        dve.wait_ge(lstmb_in, e * 16 + 16)
                    else:
                        dve.wait_ge(bias_split, e * SPLIT + step)
                    if step % 2 == 0:
                        V.tensor_copy(btmp, b32).then_inc(bias_split, 1)
                    else:
                        r = 16 * (step - 1)
                        V.tensor_copy(bias3[r:r + 32, :], btmp[r:r + 32, :])
                        if step == 1:
                            V.tensor_copy(bias3[96:128, :], btmp[96:128, :])
                        if step < SPLIT - 1:
                            V.tensor_tensor(b32, b32, btmp, ALU.subtract).then_inc(bias_split, 1)
                        else:
                            V.memset(cell[:, :], 0.0).then_inc(bias_split, 1)

                def slot(i, u, first, final):
                    c, p, st, b = u // 4, u % 4, pr[u % 2], 3 * (u % 2)
                    cit, pit = e * LOOPS + i, e * (2 * SLOTS) + i * (SLOTS // 2)
                    has_next = not (final and c == 1)
                    sc = two(b).rearrange("p m (h t) -> p m h t", t=T)
                    mx3 = mx[u % 2].rearrange("p (m h) -> p m h", m=2)
                    if not (final and u == SLOTS - 1):
                        mask((u + 1) % SLOTS, cit, (u + 1) // SLOTS, pit, None if first and u == 0 else (u + 1) // 2)
                    dve.wait_ge(st.sem, st.after(pit, "scores", u // 2))
                    V.tensor_reduce(mx3, sc, AX.X, ALU.max).then_inc(st.sem, 1)
                    dve.wait_ge(st.sem, st.after(pit, "max", u // 2))
                    V.tensor_tensor(prob[u % 2][:, :, 0:T].rearrange("p (m h) t -> p m h t", m=2), sc,
                                    mx3.unsqueeze(3).broadcast_to([P, 2, 8, T]), ALU.subtract).then_inc(st.sem, 1)
                    if p == 3 and has_next:
                        v_evac(1 - c, cit, c)
                    if not (first and u == 0):
                        finish_pair((u - 1) % SLOTS, pit, (u - 1) // 2)
                    if p == 0 and has_next:
                        q_evac(1 - c, cit, c)
                    if first and 1 <= u <= SPLIT:
                        split_bias(u - 1)

                for c in (0, 1):
                    V.memset(qs[c][:, 2 * CH:2 * CH + 16], 0.0)
                q_evac(0, e * LOOPS, 0)
                for c in range(STREAMS + 1, NCH - 1):
                    normalise(c)
                mask(0, e * LOOPS, 0, None, None)
                normalise(NCH - 1)
                v_evac(0, e * LOOPS, 0)
                for c in S8:
                    dve.wait_ge(en[c].sem, en[c].before(e, 1))
                dve.wait_ge(v_cleared, e + 1)
                for c in (0, 1):
                    V.memset(prob[c][:, :, T:TP], 0.0)
                for u in range(SLOTS):
                    slot(0, u, True, False)
                with dve.Fori(1, LOOPS - 1) as i:
                    for u in range(SLOTS):
                        slot(i, u, False, False)
                for u in range(SLOTS):
                    slot(LOOPS - 1, u, False, True)
                finish_pair(SLOTS - 1, e * (2 * SLOTS), 2 * SLOTS - 1)

                for c in (0, 1):
                    dve.wait_ge(ai[c].sem, ai[c].before((e + 1) * LOOPS))
                V.memset(hT, 0.0).then_inc(h_kept, 1)
                def lstm_step(t, split):
                    k = e * T + t
                    dve.wait_ge(gates, k * 3 + 1)
                    V.tensor_tensor(cell[:, :], cell[:, :], gate[:, DF:2 * DF], ALU.mult).then_inc(c_new, 1)
                    dve.wait_ge(gates, k * 3 + 2)
                    V.tensor_tensor(gate[:, 0:DF], gate[:, 0:DF], gate[:, 2 * DF:3 * DF], ALU.mult).then_inc(ig_new, 1)
                    dve.wait_ge(c_new, k * 2 + 1)
                    dve.wait_ge(ig_new, k + 1)
                    V.tensor_tensor(cell[:, :], cell[:, :], gate[:, 0:DF], ALU.add).then_inc(c_new, 1)
                    dve.wait_ge(c_tanh, k + 1)
                    dve.wait_ge(gates, k * 3 + 3)
                    V.tensor_tensor(hstep[:, :], gate[:, 3 * DF:], hstep[:, :], ALU.mult).then_inc(h_new, 1)
                    dve.wait_ge(h_turned, k + 1)
                    dve.wait_ge(h_saved, k * 2 + 1)
                    V.tensor_copy(hT, ps[:, 4, 0:DF]).then_inc(h_kept, 1)
                    if split:
                        at = bass.ds(t * SPLIT_W - SPLIT_FROM * SPLIT_W, SPLIT_W)
                        dve.wait_ge(w_hi, e * SPLIT_STEPS + t + (1 - SPLIT_FROM))
                        V.tensor_tensor(alias["dec_sb"][:, at], dec_sb[:, at],
                                        alias["hidden"][:, bass.ds(t * SPLIT_W + W_HIGH, SPLIT_W)],
                                        ALU.subtract).then_inc(w_lo, 1)

                with dve.Fori(0, SPLIT_FROM) as t:
                    lstm_step(t, False)
                dve.wait_ge(dec_in, e * 32 + 32)
                centre(dec_prep, e * DEC_PREP, dec["dw2"], P)
                with dve.Fori(SPLIT_FROM, SPLIT_FROM + SPLIT_STEPS) as t:
                    lstm_step(t, True)
                lstm_step(T - 1, False)

                def rest(c, need, x, hi):
                    dve.wait_ge(de[c].sem, de[c].after(e, need))
                    V.tensor_tensor(rounded(x), x, rounded(hi), ALU.subtract).then_inc(de[c].sem, 1)

                def tail(c):
                    x, rs, w = dec_x[c]
                    recip(de, e, c, rs)
                    dve.wait_ge(de[c].sem, de[c].after(e, "recip"))
                    V.scalar_tensor_tensor(out=x, in0=x, scalar=dec["g"], in1=rs, op0=ALU.mult,
                                           op1=ALU.mult).then_inc(de[c].sem, 1)
                    dve.wait_ge(de[c].sem, de[c].after(e, "norm"))
                    V.scalar_tensor_tensor(out=x, in0=x, scalar=dec["beta"], in1=w, op0=ALU.add,
                                           op1=ALU.mult).then_inc(de[c].sem, 1)
                    dve.wait_ge(de[c].sem, de[c].after(e, "weigh"))
                    V.tensor_tensor(acc[:, chunk(c)], acc[:, chunk(c)], x, ALU.add).then_inc(de[c].sem, 1)

                def rest_mem(c):
                    rest(c, "mhi", mem4[:, :, chunk(c)], mem_hi[c].rearrange("p (k n) -> p k n", k=4))

                rest_mem(0)
                dve.wait_ge(dec_mean, e + 1)
                V.tensor_tensor(dec["db2"], dec["db2"], ps[:, 7, 0:1], ALU.subtract).then_inc(dec_prep, 1)
                for c in (1, 2, 3):
                    rest_mem(c)
                for i in range(ITERS):
                    part = [(s, i * STREAMS + s) for s in S4]
                    for need, o in (("shi", 0), ("thi", 1)):
                        for s, c in part:
                            rest(c, need, dec_a[s][o], dec_hi[s][o])
                            if need == "shi" and c in (4, 5):
                                tail(c - 2)
                    for s, c in part:
                        a, b = dec_a[s]
                        dve.wait_ge(de[c].sem, de[c].after(e, "tanh"))
                        V.tensor_tensor(a, a, b, ALU.mult).then_inc(de[c].sem, 1)
                        dve.wait_ge(de[c].sem, de[c].after(e, "gate"))
                        V.tensor_copy(rounded(dec_hi[s][0]), a).then_inc(de[c].sem, 1)
                        rest(c, "ghi", a, dec_hi[s][0])
                    for s, c in part:
                        rest(c, "dhi", dec_a[s][1], dec_hi[s][1])
                    if i == 0:
                        rest_mem(4)
                        rest_mem(5)
                    for s, c in part:
                        dve.wait_ge(de[c].sem, de[c].after(e, "d2"))
                        ts(dec_x[c][0], bank(2 * s), dec["db2"], None, ALU.add).then_inc(de[c].sem, 1)
                    if i == 0:
                        tail(0)
                        rest_mem(6)
                        tail(1)
                        rest_mem(7)
                    else:
                        for c in range(STREAMS, NCH):
                            tail(c)

        @block.scalar
        def _(act):
            A = nc.scalar.activation
            ID = ACT.Identity

            def square(st, it, s, sq, x):
                act.wait_ge(st[s].sem, st[s].after(it, "center"))
                A(sq, x, ACT.Square).then_inc(st[s].sem, 1)

            def deviation(st, it, s, rs, b, scale=1.0):
                act.wait_ge(st[s].sem, st[s].after(it, "var"))
                A(rs, bank(b), ACT.Sqrt, bias=eps[:, 0:1], scale=scale).then_inc(st[s].sem, 1)

            def evac(st, it, s, need, o, bias, func=ID):
                act.wait_ge(st[s].sem, st[s].after(it, need))
                for m in (0, 1):
                    last = A(tile(o, m), bank(2 * (s % 4) + m), func, bias=bias[:, m:m + 1])
                last.then_inc(st[s].sem, 1)

            act.wait_ge(eps_set, 1)
            def tok_store(c):
                act.wait_ge(tk[c].sem, tk[c].after(0, "out"))
                A(acc[:, chunk(c)], bank(2 * (c % 4) + 1), ID, bias=tok["bo"]).then_inc(tk[c].sem, 1)

            for i in range(ITERS):
                part = [(s, i * STREAMS + s) for s in S4]
                for s, c in part:
                    co, sp_ = tok_space[s][4:6]
                    act.wait_ge(tk[c].sem, tk[c].after(0, "coord"))
                    A(co[0:8, :], bank(2 * s + 1, rows=8), ID, bias=bcoord_sb).then_inc(tk[c].sem, 1)
                    A(sp_[0:4, :], bank(2 * s, rows=4), ACT.Square, bias=bspin_sb).then_inc(tk[c].sem, 1)
                for s, c in part:
                    act.wait_ge(tk[c].sem, tk[c].after(0, "proj"))
                    A(tok_space[s][6], bank(2 * s + 1), ID, bias=tok["be"]).then_inc(tk[c].sem, 1)
                for s, c in part:
                    square(tk, 0, c, tok_space[s][1], tok_space[s][0])
                for s, c in part:
                    deviation(tk, 0, c, tok_space[s][2], 2 * s + 1)
                for s, c in part:
                    act.wait_ge(tk[c].sem, tk[c].after(0, "norm"))
                    A(tok_space[s][4], tok_space[s][0], ID, bias=tok["beta"], scale=tok["g"]).then_inc(tk[c].sem, 1)
                for s, c in part:
                    tok_store(c)

            for s in S8:
                square(gr, 0, s, gru_space[s][1], gru_space[s][0])
            for s in S8:
                deviation(gr, 0, s, gru_space[s][2], s)
            for part in (S8[:4], S8[4:]):
                for k, need in enumerate(("pref", "prei", "preh")):
                    for s in part:
                        x, sq, rs, ph, pf, re = gru_space[s]
                        act.wait_ge(gr[s].sem, gr[s].after(0, need))
                        A(ph if k == 2 else tile(pf, k), bank(s), ID, bias=tok["bg"][:, k:k + 1]).then_inc(gr[s].sem, 1)
                for need, func, how in (("relu", ACT.Abs, {}), ("abs", ACT.Exp, {"scale": -1.0}),
                                        ("exp", ACT.Ln, {"bias": 1.0})):
                    for s in part:
                        pf = gru_space[s][4]
                        act.wait_ge(gr[s].sem, gr[s].after(0, need))
                        A(pf, pf, func, **how).then_inc(gr[s].sem, 1)
            for s in S8:
                x, sq, rs, ph, pf, re = gru_space[s]
                act.wait_ge(gr[s].sem, gr[s].after(0, "diff"))
                A(mixed[:, chunk(s)], rs, ACT.Sigmoid, scale=-1.0)
                A(sq, rs, ACT.Sigmoid)
                A(x, tile(pf, 0), ACT.Sigmoid).then_inc(gr[s].sem, 1)

            for s in S8:
                square(fi, 0, s, fin_space[s][0], xn[:, chunk(s)])
            for s in S8:
                deviation(fi, 0, s, fin_space[s][1], s)
            act.wait_ge(ro.sem, ro.after(0, "shift"))
            A(logit, logit, ACT.Exp).then_inc(ro.sem, 1)
            act.wait_ge(ro.sem, ro.after(0, "kept0"))
            A(routed[0:E, 4 * CH:].rearrange("p (s n) -> p s n", s=4), ps[0:E, 4:8, 0:CH],
              ACT.Copy).then_inc(ro.sem, 1)

            with act.Fori(0, E) as e:
                def affine(c):
                    act.wait_ge(en[c].sem, en[c].after(e, "norm"))
                    for m in (0, 1):
                        last = A(hid2[:, m, chunk(c)], tile(enc_x[c][0], m), ID,
                                 bias=enc["beta"][:, m:m + 1], scale=enc["g"][:, m:m + 1])
                    last.then_inc(en[c].sem, 1)

                act.wait_ge(bias_products, e + 1)
                for m in (0, 1):
                    A(enc_fixed[:, m:m + 1], ps[:, 7, 0:1], ID, bias=enc["b2"][:, m:m + 1], scale=-0.5)
                    last = A(enc_fixed[:, 2 + m:3 + m], ps[:, 7, 2 + m:3 + m], ID, bias=enc["bo"][:, m:m + 1])
                last.then_inc(enc_bias, 1)
                act.wait_ge(enc_bias, e + 1)
                for i in range(ITERS):
                    for c in range(i * STREAMS, (i + 1) * STREAMS):
                        act.wait_ge(de[c].sem, de[c].before(e))
                    for s in S4:
                        evac(en, e, i * STREAMS + s, "w1", enc_a[s][0], enc["b1"], ACT.Relu)
                    for s in S4:
                        c = i * STREAMS + s
                        evac(en, e, c, "w2", enc_x[c][0], enc_fixed[:, 0:2])
                        act.wait_ge(en[c].sem, en[c].after(e, "bias"))
                        A(enc_a[s][1], enc_x[c][0], ACT.Square).then_inc(en[c].sem, 1)
                        if i and s < 2:
                            affine(s)
                    for s in S4:
                        c = i * STREAMS + s
                        deviation(en, e, c, enc_x[c][1], 2 * s + 1, scale=0.5)
                    if i:
                        affine(2)
                        affine(3)

                def k_evac(c, it, shift):
                    act.wait_ge(ai[c].sem, ai[c].after(it, "k", shift))
                    for m in (0, 1):
                        last = A(tile(ks[c], m), bank(6 + m), ID, bias=enc["bk"][:, m:m + 1])
                    last.then_inc(ai[c].sem, 1)

                def v_evac(c, it, shift):
                    act.wait_ge(ai[c].sem, ai[c].after(it, "v", shift))
                    v_places(c, 1, lambda o, i: A(o, i, ACT.Copy)).then_inc(ai[c].sem, 1)

                def store_out(c, it, shift, at):
                    act.wait_ge(ao[c].sem, ao[c].after(it, "out", shift))
                    for m in (0, 1):
                        last = A(mix2[:, m, bass.ds(at, CH)], bank(6 + m), ID,
                                 bias=enc_fixed[:, 2 + m:3 + m])
                    last.then_inc(ao[c].sem, 1)

                def slot(i, u, first, final):
                    c, p, st, b = u // 4, u % 4, pr[u % 2], 3 * (u % 2)
                    cit, pit = e * LOOPS + i, e * (2 * SLOTS) + i * (SLOTS // 2)
                    act.wait_ge(st.sem, st.after(pit, "shift", u // 2))
                    A(prob[u % 2][:, :, 0:T], prob[u % 2][:, :, 0:T], ACT.Exp).then_inc(st.sem, 1)
                    if p == 1 and not (first and c == 0):
                        store_out(1 - c, cit, c - 1, i * (2 * CH) + (c - 1) * CH)
                    if p == 2 and not (final and c == 1):
                        k_evac(1 - c, cit, c)
                    if p == 3 and not (final and c == 1):
                        v_evac(1 - c, cit, c)
                    act.wait_ge(st.sem, st.after(pit, "turn", u // 2))
                    src = ps[:, b:b + 2, :].rearrange("p m (hb t) -> p m hb t", t=TP)[:, :, :, 0:T]
                    A(probT[u % 2].rearrange("p (m h) (b t) -> p m (h b) t", m=2, b=2), src,
                      ACT.Copy).then_inc(st.sem, 1)

                k_evac(0, e * LOOPS, 0)
                for c in range(STREAMS, NCH):
                    affine(c)
                v_evac(0, e * LOOPS, 0)
                act.wait_ge(v_cleared, e + 1)
                for u in range(SLOTS):
                    slot(0, u, True, False)
                with act.Fori(1, LOOPS - 1) as i:
                    for u in range(SLOTS):
                        slot(i, u, False, False)
                for u in range(SLOTS):
                    slot(LOOPS - 1, u, False, True)
                store_out(1, e * LOOPS, LOOPS - 1, (NCH - 1) * CH)
                def lstm_step(t, par, split=False):
                    k = e * T + t
                    act.wait_ge(z_lo, k + 1)
                    A(gate[:, 0:2 * DF], ps[:, 2 * par, :], ACT.Sigmoid).then_inc(gates, 1)
                    act.wait_ge(z_hi, k + 1)
                    A(gate[:, 2 * DF:3 * DF], ps[:, 2 * par + 1, 0:DF], ACT.Tanh).then_inc(gates, 1)
                    A(gate[:, 3 * DF:], ps[:, 2 * par + 1, DF:], ACT.Sigmoid).then_inc(gates, 1)
                    act.wait_ge(c_new, k * 2 + 2)
                    A(hstep[:, :], cell[:, :], ACT.Tanh).then_inc(c_tanh, 1)
                    if split:
                        A(alias["hidden"][:, bass.ds(t * SPLIT_W + W_HIGH, SPLIT_W)],
                          dec_sb[:, bass.ds(t * SPLIT_W - SPLIT_FROM * SPLIT_W, SPLIT_W)], ACT.Copy).then_inc(w_hi, 1)

                with act.Fori(0, SPLIT_FROM // 2) as i:
                    lstm_step(i * 2, 0)
                    lstm_step(i * 2 + 1, 1)
                act.wait_ge(dec_prep, e * DEC_PREP + (DEC_PREP - 1))
                with act.Fori(SPLIT_FROM // 2, T // 2) as i:
                    lstm_step(i * 2, 0, True)
                    lstm_step(i * 2 + 1, 1, True)
                lstm_step(T - 1, 0)

                def keep_rounded(c, need, hi, x):
                    act.wait_ge(de[c].sem, de[c].after(e, need))
                    A(rounded(hi), x, ACT.Copy).then_inc(de[c].sem, 1)

                def round_mem(c):
                    A(rounded(mem_hi[c]).rearrange("p (k n) -> p k n", k=4), mem4[:, :, chunk(c)],
                      ACT.Copy).then_inc(de[c].sem, 1)

                act.wait_ge(h_saved, e * (2 * T) + 2 * T + 1)
                for c in S4:
                    round_mem(c)
                for i in range(ITERS):
                    part = [(s, i * STREAMS + s) for s in S4]
                    for need, o, w, func, hi in (("s1", 0, "sb1", ACT.Relu, "srelu"), ("t1", 1, "tb1", ACT.Relu, "trelu"),
                                                 ("s2", 0, "sb2", ACT.Sigmoid, None), ("t2", 1, "tb2", ACT.Tanh, None),
                                                 ("d1", 1, "db1", ACT.Relu, "drelu")):
                        for s, c in part:
                            evac(de, e, c, need, dec_a[s][o], dec[w], func)
                            if hi:
                                keep_rounded(c, hi, dec_hi[s][o], dec_a[s][o])
                    if i == 0:
                        round_mem(4)
                        round_mem(5)
                    for s, c in part:
                        act.wait_ge(de[c].sem, de[c].after(e, "route"))
                        A(dec_x[c][2], bank(2 * s + 1), ACT.Copy).then_inc(de[c].sem, 1)
                    for s, c in part:
                        act.wait_ge(de[c].sem, de[c].after(e, "bias"))
                        A(tile(dec_a[s][1], 0), dec_x[c][0], ACT.Square).then_inc(de[c].sem, 1)
                    for s, c in part:
                        deviation(de, e, c, dec_x[c][1], 2 * s + 1)
                    if i == 0:
                        round_mem(6)
                        round_mem(7)

        @block.gpsimd
        def _(pool):
            G.memset(eps[:, :], EPS).then_inc(eps_set, 1)
            for s in S8:
                x, sq, rs, ph, pf, re = gru_space[s]
                pool.wait_ge(gr[s].sem, gr[s].after(0, "ln"))
                G.tensor_tensor(re, re, pf, ALU.add).then_inc(gr[s].sem, 1)
            with pool.Fori(0, E) as e:
                w3 = enc["w2"].rearrange("p (k n) -> p k n", k=2)
                half3 = cell[:, :].rearrange("p (k n) -> p k n", k=2)
                pool.wait_ge(enc_in, e * 16 + 16)
                pool.wait_ge(clear, 5)
                held(pool)
                G.tensor_tensor(half3, w3[:, :, 0:P], w3[:, :, P:DF], ALU.add).then_inc(enc_prep, 1)
                for level in range(1, HALVINGS):
                    w = P >> level
                    pool.wait_ge(enc_prep, e * ENC_PREP + level)
                    held(pool)
                    G.tensor_tensor(half3[:, :, 0:w], half3[:, :, 0:w], half3[:, :, w:2 * w],
                                    ALU.add).then_inc(enc_prep, 1)
                pool.wait_ge(enc_prep, e * ENC_PREP + HALVINGS)
                held(pool)
                G.tensor_scalar(rowsum[:, 4:6], half3[:, :, 0], 1.0 / DF, None, ALU.mult).then_inc(enc_prep, 1)
                pool.wait_ge(enc_prep, e * ENC_PREP + HALVINGS + 1)
                held(pool)
                G.tensor_tensor(w3, w3, rowsum[:, 4:6].unsqueeze(2).broadcast_to([P, 2, DF]),
                                ALU.subtract).then_inc(enc_prep, 1)

                def copy_chunk(c, it, shift, at):
                    pool.wait_ge(ai[c].sem, ai[c].before(it, shift))
                    held(pool)
                    for k in (0, 1):
                        last = G.tensor_copy(hc[c][:, k, :], hidden[:, bass.ds(at + k * N, CH + 16)])
                    last.then_inc(ai[c].sem, 1)

                def mask(u, pit, shift):
                    c, p, st = u // 4 % 2, u % 4, mk[u % 2]
                    pool.wait_ge(st.sem, st.after(pit, "maskv", shift))
                    kk = ks[c][:, CH + 2 * p * T:CH + 2 * (p + 1) * T].rearrange("p (b t) -> p b t", b=2)
                    G.tensor_tensor(masked[u % 2][:, 1, :, :, :], kk.unsqueeze(2).broadcast_to([P, 2, 8, T]),
                                    const["mask"].unsqueeze(1).unsqueeze(3).broadcast_to([P, 2, 8, T]),
                                    ALU.mult).then_inc(st.sem, 1)

                def slot(i, u, final):
                    c, p = u // 4, u % 4
                    cit, pit = e * LOOPS + i, e * (2 * SLOTS) + i * (SLOTS // 2)
                    if p == 2 and not final:
                        copy_chunk(c, cit, 1, i * (2 * CH) + (c + 2) * CH)
                    if not (final and u == SLOTS - 1):
                        mask((u + 1) % SLOTS, pit, (u + 1) // 2)

                for first in (0, 1):
                    for c in (first, first + 1):
                        pool.wait_ge(en[c].sem, en[c].before(e, 1))
                    held(pool)
                    copy_chunk(first, e * LOOPS, 0, first * CH)
                mask(0, e * (2 * SLOTS), 0)
                for c in S8:
                    pool.wait_ge(en[c].sem, en[c].before(e, 1))
                held(pool)
                G.memset(vodd, 0.0).then_inc(v_cleared, 1)
                with pool.Fori(0, LOOPS - 1) as i:
                    for u in range(SLOTS):
                        slot(i, u, False)
                for u in range(SLOTS):
                    slot(LOOPS - 1, u, True)
                for c in (0, 1):
                    pool.wait_ge(ao[c].sem, ao[c].before(e * LOOPS, LOOPS))
                held(pool)

                def save(t):
                    k = e * T + t
                    pool.wait_ge(h_kept, e * (T + 1) + t + 2)
                    held(pool)
                    G.tensor_copy(mem4[:, 0:2, bass.ds(t, NB, step=T)], hT2[:, :, 0:64]).then_inc(h_saved, 1)
                    G.tensor_copy(mem4[:, 2:4, bass.ds(t * -1 + (T - 1), NB, step=T)], hT2[:, :, 64:128]).then_inc(h_saved, 1)

                def turn(t, par):
                    G.tensor_copy(xs4[:, par, :, 0:64], mix2[:, :, bass.ds(t, NB, step=T)])
                    G.tensor_copy(xs4[:, par, :, 64:128],
                                  mix2[:, :, bass.ds(t * -1 + (T - 1), NB, step=T)]).then_inc(x_turned, 1)

                turn(0, 0)
                turn(1, 1)
                with pool.Fori(0, T // 2 - 1) as i:
                    for par in (0, 1):
                        save(i * 2 + par)
                        pool.wait_ge(z_in, e * T + i * 2 + (par + 1))
                        held(pool)
                        turn(i * 2 + (par + 2), par)
                save(T - 3)
                pool.wait_ge(z_in, e * T + T - 2)
                held(pool)
                turn(T - 1, 0)
                save(T - 2)
                save(T - 1)


def pack(inputs, names):
    parts = []
    for name in names:
        a = np.asarray(inputs["L0_ffn_" + name])
        if a.ndim == 2:
            a = a[:, :, None]
        e, r, w = a.shape
        parts.append(a.reshape(e, r // P, P, w).transpose(0, 2, 1, 3).reshape(e, P, -1))
    return np.ascontiguousarray(np.concatenate(parts, axis=2))


def kernel(**inputs):
    import concourse.bacc as bacc
    from concourse.bass_utils import run_bass_kernel_spmd

    t = {k[7:]: np.asarray(v) for k, v in inputs.items() if k.startswith("L0_tok_")}
    x = np.asarray(inputs["x"])
    patches = x.reshape(NB, 3, GRID, PATCH, GRID, PATCH).transpose(1, 3, 5, 0, 2, 4).reshape(KP, P, N)
    patches = patches.transpose(1, 0, 2)
    wp = t["W_patch"].reshape(KP, P, P).transpose(1, 0, 2).reshape(P, KP * P)
    wg = np.asarray(inputs["L0_attn_W"]).T
    bg = np.asarray(inputs["L0_attn_b"]).reshape(3, P).T
    tokw = np.concatenate(
        [wp, t["W_out"], wg, np.asarray(inputs["L0_ffn_router_w"]), t["W_coord"], t["W_spinor"]]
        + [t[k][:, None] for k in ("b_patch", "b_embed", "ln_gamma", "ln_beta", "b_out")]
        + [bg, t["pos_embed"][0].T], axis=1)
    f = np.float32
    consts = np.concatenate(
        [np.eye(P, dtype=f), np.kron(np.eye(8, dtype=f), np.ones((DH, 1), f)),
         np.kron(np.eye(2, dtype=f), np.ones((TP, DH), f))], axis=1)
    selw = np.zeros((E, P, P), f)
    for k in range(E):
        selw[k, k] = 1.0
    encw = pack(inputs, ["enc_w1", "enc_w2", "attn_in_w", "attn_out_w", "enc_b1", "enc_b2", "enc_g", "enc_beta",
                         "attn_in_b", "attn_out_b"])
    decw = pack(inputs, ["sig_w1", "tan_w1", "sig_w2", "tan_w2", "dec_w1", "dec_w2", "sig_b1", "sig_b2", "tan_b1",
                         "tan_b2", "dec_b1", "dec_b2", "dec_g", "dec_beta"])
    lstmw = pack(inputs, ["lstm_wi_f", "lstm_wh_f", "lstm_wi_b", "lstm_wh_b"])
    lstmb = np.stack([np.asarray(inputs["L0_ffn_lstm_b_f"]), np.asarray(inputs["L0_ffn_lstm_b_b"])], axis=1)
    lstmb = np.tile(lstmb, (1, P // 2, 1))
    arrays = {
        "patches": patches, "tokw": tokw, "wembed": t["W_embed"], "bcoord": t["b_coord"][:, None],
        "bspin": t["b_spinor"][:, None], "rbias": np.asarray(inputs["L0_ffn_router_b"]), "consts": consts,
        "selw": selw, "encw": encw, "lstmw": lstmw, "lstmb": lstmb, "decw": decw,
    }
    arrays = {k: np.ascontiguousarray(v) for k, v in arrays.items()}
    nc = bacc.Bacc("TRN2", target_bir_lowering=False, num_devices=1)
    aps = {k: nc.dram_tensor("in_" + k, v.shape, mybir.dt.from_np(v.dtype), kind="ExternalInput").ap()
           for k, v in arrays.items()}
    out = nc.dram_tensor("out", (P, N), F32, kind="ExternalOutput").ap()
    build(nc, out=out, **aps)
    r = run_bass_kernel_spmd(nc, [{"in_" + k: v for k, v in arrays.items()}], core_ids=[0])
    return np.ascontiguousarray(r.results[0]["out"].reshape(P, NB, T).transpose(1, 2, 0))
```
